# Optimizing a Trainium2 kernel written in Bass

```python
import numpy as np
import jax
import jax.numpy as jnp

def _softmax(x, axis=-1):
    return jax.nn.softmax(x, axis=axis)

def _gelu(x):
    return jax.nn.gelu(x, approximate=True)

def _silu(x):
    return jax.nn.silu(x)

def _sigmoid(x):
    return jax.nn.sigmoid(x)

def _layernorm(x, axis=-1, eps=1e-05):
    m = jnp.mean(x, axis=axis, keepdims=True)
    v = jnp.var(x, axis=axis, keepdims=True)
    return (x - m) / jnp.sqrt(v + eps)

def _scatter_add(tgt, idx, src, axis=0):
    return tgt.at[idx].add(src)

def _segment_sum(src, seg, n):
    return jax.ops.segment_sum(src, seg, n)
kernel_name = 'mk_xattn_ffn_d2_seqx_r4_727f46'

def setup_inputs(seed: int=0):
    np.random.seed(seed)
    _w = jnp.asarray

    def _rec_inputs():
        import jax
        import jax.numpy as jnp
        _rk = jax.random.key(seed)
        x = -0.0002928 + 1 * jax.random.normal(jax.random.fold_in(_rk, 1), (16, 256, 256), jnp.float32)
        _lenS = 256 - jax.random.randint(jax.random.fold_in(_rk, 7), (16,), 0, max(1, 256 // 4) + 1, jnp.int32)
        _lenS2 = 77 - jax.random.randint(jax.random.fold_in(_rk, 8), (16,), 0, max(1, 77 // 4) + 1, jnp.int32)
        _ctx_1024P = jax.random.normal(jax.random.fold_in(_rk, 11), (16, 16, 256), jnp.float32)
        _ctx_1024c = jax.random.dirichlet(jax.random.fold_in(_rk, 511), 0.3 * jnp.ones((16,), jnp.float32), (16, 77))
        _ctx_1024t = jnp.einsum('bsk,bkd->bsd', _ctx_1024c, _ctx_1024P)
        _ctx_1024t = _ctx_1024t * jax.lax.rsqrt(jnp.mean(jnp.square(_ctx_1024t)) + 1e-12) * 0.953939
        ctx_1024 = 4.13588e-05 + 0.999923 * (_ctx_1024t + 0.3 * jax.random.normal(jax.random.fold_in(_rk, 611), (16, 77, 256), jnp.float32))
        return (x, ctx_1024)
    x, ctx_1024 = _rec_inputs()

    def _L0_xattn_setup():
        import jax, jax.numpy as jnp
        import numpy as np
        E = 256
        KD = 256
        H = 16
        DH = E // H
        EPS = 1e-05

        def layernorm(x, gamma, beta):
            mu = jnp.mean(x, axis=-1, keepdims=True)
            var = jnp.mean(jnp.square(x - mu), axis=-1, keepdims=True)
            return (x - mu) * jax.lax.rsqrt(var + EPS) * gamma + beta
        key = jax.random.key(seed)
        ks = jax.random.split(key, 16)
        B, QN, KN = (4, 256, 512)
        s_q = 1.0 / np.sqrt(E)
        s_k = 1.0 / np.sqrt(KD)
        return {'q': jax.random.normal(ks[0], (B, QN, E), jnp.float32), 'k': jax.random.normal(ks[1], (B, KN, KD), jnp.float32), 'v': jax.random.normal(ks[2], (B, KN, KD), jnp.float32), 'Wq': jax.random.uniform(ks[3], (E, E), jnp.float32, -s_q, s_q), 'bq': jax.random.uniform(ks[4], (E,), jnp.float32, -s_q, s_q), 'Wk': jax.random.uniform(ks[5], (E, KD), jnp.float32, -s_k, s_k), 'bk': jax.random.uniform(ks[6], (E,), jnp.float32, -s_k, s_k), 'Wv': jax.random.uniform(ks[7], (E, KD), jnp.float32, -s_k, s_k), 'bv': jax.random.uniform(ks[8], (E,), jnp.float32, -s_k, s_k), 'Wp': jax.random.uniform(ks[9], (E, E), jnp.float32, -s_q, s_q), 'bp': jax.random.uniform(ks[10], (E,), jnp.float32, -s_q, s_q), 'q_gamma': jnp.ones((DH,), jnp.float32), 'q_beta': jnp.zeros((DH,), jnp.float32), 'k_gamma': jnp.ones((DH,), jnp.float32), 'k_beta': jnp.zeros((DH,), jnp.float32)}
    _L0_xattn_all = _L0_xattn_setup()
    _L0_xattn_in = {k: v for k, v in _L0_xattn_all.items() if k in ('Wq', 'bq', 'Wk', 'bk', 'Wv', 'bv', 'Wp', 'bp', 'q_gamma', 'q_beta', 'k_gamma', 'k_beta')}
    del _L0_xattn_all

    def _L0_ffn_setup():
        import jax, jax.numpy as jnp
        import numpy as np
        NUM_EXPERTS = 8
        TOP_K = 2
        MOE_DIM = 512

        def _moe_forward(x, moe_router, moe_w13, moe_w2):
            b, s, d = x.shape
            x_flat = x.reshape(b * s, d)
            router_logits = jnp.einsum('td,de->te', x_flat, moe_router)
            topk_logits, topk_idx = jax.lax.top_k(router_logits, TOP_K)
            topk_weights = jax.nn.softmax(topk_logits, axis=-1).astype(x.dtype)
            tokens = x_flat.shape[0]
            expert_ids = topk_idx.reshape(tokens * TOP_K)
            dispatch_weights = topk_weights.reshape(tokens * TOP_K)
            sort_idx = jnp.argsort(expert_ids, axis=0)
            token_ids = jnp.arange(tokens * TOP_K, dtype=jnp.int32) // TOP_K
            token_ids_sort = token_ids[sort_idx]
            x_sort = x_flat[token_ids_sort]
            w_sort = dispatch_weights[sort_idx].astype(x_flat.dtype)
            group_sizes = jnp.bincount(expert_ids, length=NUM_EXPERTS).astype(jnp.int32)
            w13_out = jax.lax.ragged_dot(x_sort, moe_w13, group_sizes)
            gate, up = jnp.split(w13_out, [MOE_DIM], axis=-1)
            hidden = jax.nn.silu(gate) * up
            out_dispatch = jax.lax.ragged_dot(hidden, moe_w2, group_sizes)
            out_flat = jnp.zeros_like(x_flat).at[token_ids_sort].add(out_dispatch * w_sort[:, None], mode='drop')
            return out_flat.reshape(b, s, d)
        key = jax.random.key(seed)
        k1, k2, k3, k4 = jax.random.split(key, 4)
        B, S, D = (4, 512, 256)
        x = jax.random.normal(k1, (B, S, D), dtype=jnp.float32)
        moe_router = jax.random.normal(k2, (D, NUM_EXPERTS), dtype=jnp.float32) * 0.02
        moe_w13 = jax.random.normal(k3, (NUM_EXPERTS, D, 2 * MOE_DIM), dtype=jnp.float32) * 0.02
        moe_w2 = jax.random.normal(k4, (NUM_EXPERTS, MOE_DIM, D), dtype=jnp.float32) * 0.02
        return {'x': x, 'moe_router': moe_router, 'moe_w13': moe_w13, 'moe_w2': moe_w2}
    _L0_ffn_all = _L0_ffn_setup()
    _L0_ffn_in = {k: v for k, v in _L0_ffn_all.items() if k in ('moe_router', 'moe_w13', 'moe_w2')}
    del _L0_ffn_all

    def _L1_xattn_setup():
        import jax, jax.numpy as jnp
        import numpy as np
        C = 256
        B, SQ, SKV = (4, 512, 512)
        key = jax.random.key(seed)
        ks = jax.random.split(key, 10)
        s = 1.0 / np.sqrt(C)
        return {'x': jax.random.normal(ks[0], (B, SQ, C), jnp.float32), 'content_embeddings': jax.random.normal(ks[1], (B, SKV, C), jnp.float32), 'Wq': jax.random.normal(ks[2], (C, C), jnp.float32) * s, 'bq': jnp.zeros((C,), jnp.float32), 'Wk': jax.random.normal(ks[3], (C, C), jnp.float32) * s, 'bk': jnp.zeros((C,), jnp.float32), 'Wv': jax.random.normal(ks[4], (C, C), jnp.float32) * s, 'bv': jnp.zeros((C,), jnp.float32), 'Wo': jax.random.normal(ks[5], (C, C), jnp.float32) * s, 'bo': jnp.zeros((C,), jnp.float32)}
    _L1_xattn_all = _L1_xattn_setup()
    _L1_xattn_in = {k: v for k, v in _L1_xattn_all.items() if k in ('Wq', 'bq', 'Wk', 'bk', 'Wv', 'bv', 'Wo', 'bo')}
    del _L1_xattn_all

    def _L1_ffn_setup():
        import jax, jax.numpy as jnp
        import numpy as np
        TOPK = 4
        key = jax.random.key(seed)
        ks = jax.random.split(key, 9)
        B, T, D = (4, 512, 256)
        E, H = (32, 128)
        HS = H * TOPK
        s = lambda k, shape, fan: jax.random.normal(k, shape, dtype=jnp.float32) / np.sqrt(fan)
        return {'x': jax.random.normal(ks[0], (B, T, D), dtype=jnp.float32), 'router_w': s(ks[1], (E, D), D), 'router_bias': jnp.zeros((E,), dtype=jnp.float32), 'gate_w': s(ks[2], (E, H, D), D), 'up_w': s(ks[3], (E, H, D), D), 'down_w': s(ks[4], (E, D, H), H), 'sgate_w': s(ks[5], (HS, D), D), 'sup_w': s(ks[6], (HS, D), D), 'sdown_w': s(ks[7], (D, HS), HS)}
    _L1_ffn_all = _L1_ffn_setup()
    _L1_ffn_in = {k: v for k, v in _L1_ffn_all.items() if k in ('router_w', 'router_bias', 'gate_w', 'up_w', 'down_w', 'sgate_w', 'sup_w', 'sdown_w')}
    del _L1_ffn_all
    return {'x': x, 'ctx_1024': ctx_1024, 'L0_xattn_Wq': _L0_xattn_in['Wq'], 'L0_xattn_bq': _L0_xattn_in['bq'], 'L0_xattn_Wk': _L0_xattn_in['Wk'], 'L0_xattn_bk': _L0_xattn_in['bk'], 'L0_xattn_Wv': _L0_xattn_in['Wv'], 'L0_xattn_bv': _L0_xattn_in['bv'], 'L0_xattn_Wp': _L0_xattn_in['Wp'], 'L0_xattn_bp': _L0_xattn_in['bp'], 'L0_xattn_q_gamma': _L0_xattn_in['q_gamma'], 'L0_xattn_q_beta': _L0_xattn_in['q_beta'], 'L0_xattn_k_gamma': _L0_xattn_in['k_gamma'], 'L0_xattn_k_beta': _L0_xattn_in['k_beta'], 'L0_ffn_moe_router': _L0_ffn_in['moe_router'], 'L0_ffn_moe_w13': _L0_ffn_in['moe_w13'], 'L0_ffn_moe_w2': _L0_ffn_in['moe_w2'], 'L1_xattn_Wq': _L1_xattn_in['Wq'], 'L1_xattn_bq': _L1_xattn_in['bq'], 'L1_xattn_Wk': _L1_xattn_in['Wk'], 'L1_xattn_bk': _L1_xattn_in['bk'], 'L1_xattn_Wv': _L1_xattn_in['Wv'], 'L1_xattn_bv': _L1_xattn_in['bv'], 'L1_xattn_Wo': _L1_xattn_in['Wo'], 'L1_xattn_bo': _L1_xattn_in['bo'], 'L1_ffn_router_w': _L1_ffn_in['router_w'], 'L1_ffn_router_bias': _L1_ffn_in['router_bias'], 'L1_ffn_gate_w': _L1_ffn_in['gate_w'], 'L1_ffn_up_w': _L1_ffn_in['up_w'], 'L1_ffn_down_w': _L1_ffn_in['down_w'], 'L1_ffn_sgate_w': _L1_ffn_in['sgate_w'], 'L1_ffn_sup_w': _L1_ffn_in['sup_w'], 'L1_ffn_sdown_w': _L1_ffn_in['sdown_w']}

def reference(x, ctx_1024, L0_xattn_Wq, L0_xattn_bq, L0_xattn_Wk, L0_xattn_bk, L0_xattn_Wv, L0_xattn_bv, L0_xattn_Wp, L0_xattn_bp, L0_xattn_q_gamma, L0_xattn_q_beta, L0_xattn_k_gamma, L0_xattn_k_beta, L0_ffn_moe_router, L0_ffn_moe_w13, L0_ffn_moe_w2, L1_xattn_Wq, L1_xattn_bq, L1_xattn_Wk, L1_xattn_bk, L1_xattn_Wv, L1_xattn_bv, L1_xattn_Wo, L1_xattn_bo, L1_ffn_router_w, L1_ffn_router_bias, L1_ffn_gate_w, L1_ffn_up_w, L1_ffn_down_w, L1_ffn_sgate_w, L1_ffn_sup_w, L1_ffn_sdown_w):
    import jax
    import jax.numpy as jnp

    def _L0_xattn_ref(q, k, v, Wq, bq, Wk, bk, Wv, bv, Wp, bp, q_gamma, q_beta, k_gamma, k_beta):
        import jax, jax.numpy as jnp
        import numpy as np
        E = 256
        KD = 256
        H = 16
        DH = E // H
        EPS = 1e-05

        def layernorm(x, gamma, beta):
            mu = jnp.mean(x, axis=-1, keepdims=True)
            var = jnp.mean(jnp.square(x - mu), axis=-1, keepdims=True)
            return (x - mu) * jax.lax.rsqrt(var + EPS) * gamma + beta
        B, QN, _ = q.shape
        KN = k.shape[1]
        scale = DH ** (-0.5)
        qh = (q @ Wq.T + bq).reshape(B, QN, H, DH).transpose(0, 2, 1, 3)
        kh = (k @ Wk.T + bk).reshape(B, KN, H, DH).transpose(0, 2, 1, 3)
        vh = (v @ Wv.T + bv).reshape(B, KN, H, DH).transpose(0, 2, 1, 3)
        qh = layernorm(qh, q_gamma, q_beta) * scale
        kh = layernorm(kh, k_gamma, k_beta)
        attn = jax.nn.softmax(jnp.einsum('bhqd,bhkd->bhqk', qh, kh), axis=-1)
        x = jnp.einsum('bhqk,bhkd->bhqd', attn, vh)
        x = x.transpose(0, 2, 1, 3).reshape(B, QN, E)
        return x @ Wp.T + bp

    def _L0_ffn_ref(x, moe_router, moe_w13, moe_w2):
        import jax, jax.numpy as jnp
        import numpy as np
        NUM_EXPERTS = 8
        TOP_K = 2
        MOE_DIM = 512

        def _moe_forward(x, moe_router, moe_w13, moe_w2):
            b, s, d = x.shape
            x_flat = x.reshape(b * s, d)
            router_logits = jnp.einsum('td,de->te', x_flat, moe_router)
            topk_logits, topk_idx = jax.lax.top_k(router_logits, TOP_K)
            topk_weights = jax.nn.softmax(topk_logits, axis=-1).astype(x.dtype)
            tokens = x_flat.shape[0]
            expert_ids = topk_idx.reshape(tokens * TOP_K)
            dispatch_weights = topk_weights.reshape(tokens * TOP_K)
            sort_idx = jnp.argsort(expert_ids, axis=0)
            token_ids = jnp.arange(tokens * TOP_K, dtype=jnp.int32) // TOP_K
            token_ids_sort = token_ids[sort_idx]
            x_sort = x_flat[token_ids_sort]
            w_sort = dispatch_weights[sort_idx].astype(x_flat.dtype)
            group_sizes = jnp.bincount(expert_ids, length=NUM_EXPERTS).astype(jnp.int32)
            w13_out = jax.lax.ragged_dot(x_sort, moe_w13, group_sizes)
            gate, up = jnp.split(w13_out, [MOE_DIM], axis=-1)
            hidden = jax.nn.silu(gate) * up
            out_dispatch = jax.lax.ragged_dot(hidden, moe_w2, group_sizes)
            out_flat = jnp.zeros_like(x_flat).at[token_ids_sort].add(out_dispatch * w_sort[:, None], mode='drop')
            return out_flat.reshape(b, s, d)
        return _moe_forward(x, moe_router, moe_w13, moe_w2)

    def _L1_xattn_ref(x, content_embeddings, Wq, bq, Wk, bk, Wv, bv, Wo, bo):
        import jax, jax.numpy as jnp
        import numpy as np
        C = 256
        B, SQ, SKV = (4, 512, 512)
        queries = x @ Wq.T + bq
        keys = content_embeddings @ Wk.T + bk
        values = content_embeddings @ Wv.T + bv
        scale = 1.0 / jnp.sqrt(jnp.asarray(C, x.dtype))
        scores = jnp.einsum('bqc,bkc->bqk', queries, keys) * scale
        attn = jax.nn.softmax(scores, axis=-1)
        attended = jnp.einsum('bqk,bkc->bqc', attn, values)
        out = x + attended
        return out @ Wo.T + bo

    def _L1_ffn_ref(x, router_w, router_bias, gate_w, up_w, down_w, sgate_w, sup_w, sdown_w):
        import jax, jax.numpy as jnp
        import numpy as np
        TOPK = 4
        B, T, D = x.shape
        flat = x.reshape(B * T, D)
        logits = flat.astype(jnp.float32) @ router_w.T + router_bias
        scores = jax.nn.softmax(logits, axis=-1)
        topk_scores, topk_idx = jax.lax.top_k(scores, TOPK)
        topk_scores = topk_scores / jnp.clip(topk_scores.sum(axis=-1, keepdims=True), 1e-12, None)
        h = jax.nn.silu(jnp.einsum('nd,ehd->neh', flat, gate_w)) * jnp.einsum('nd,ehd->neh', flat, up_w)
        expert_out = jnp.einsum('neh,edh->ned', h, down_w)
        sel = jnp.take_along_axis(expert_out, topk_idx[:, :, None], axis=1)
        out = (sel * topk_scores.astype(flat.dtype)[:, :, None]).sum(axis=1)
        out = out + jax.nn.silu(flat @ sgate_w.T) * (flat @ sup_w.T) @ sdown_w.T
        return out.reshape(B, T, D)
    x = x + _L0_xattn_ref(_layernorm(x, axis=-1), ctx_1024, ctx_1024, L0_xattn_Wq, L0_xattn_bq, L0_xattn_Wk, L0_xattn_bk, L0_xattn_Wv, L0_xattn_bv, L0_xattn_Wp, L0_xattn_bp, L0_xattn_q_gamma, L0_xattn_q_beta, L0_xattn_k_gamma, L0_xattn_k_beta)
    x = x + _L0_ffn_ref(_layernorm(x, axis=-1), L0_ffn_moe_router, L0_ffn_moe_w13, L0_ffn_moe_w2)
    x = x + _L1_xattn_ref(_layernorm(x, axis=-1), ctx_1024, L1_xattn_Wq, L1_xattn_bq, L1_xattn_Wk, L1_xattn_bk, L1_xattn_Wv, L1_xattn_bv, L1_xattn_Wo, L1_xattn_bo)
    x = x + _L1_ffn_ref(_layernorm(x, axis=-1), L1_ffn_router_w, L1_ffn_router_bias, L1_ffn_gate_w, L1_ffn_up_w, L1_ffn_down_w, L1_ffn_sgate_w, L1_ffn_sup_w, L1_ffn_sdown_w)
    return x

_drawn_inputs = setup_inputs


def setup_inputs(seed=0):
    import zlib

    import numpy as np

    out = dict(_drawn_inputs(seed))
    spreads = {'L0_xattn_q_gamma': (1.0, 0.6),
     'L0_xattn_q_beta': (0.0, 0.573),
     'L0_xattn_k_gamma': (1.0, 0.6),
     'L0_xattn_k_beta': (0.0, 0.8),
     'L1_xattn_bq': (0.0, 0.317),
     'L1_xattn_bk': (0.0, 0.8),
     'L1_xattn_bv': (0.0, 0.1),
     'L1_xattn_bo': (0.0, 0.1),
     'L1_ffn_router_bias': (0.0, 0.1)}
    factors = {'L0_xattn_bq': 5.961, 'L0_xattn_bk': 8.0, 'L0_ffn_moe_router': 2.725}
    for name, (base, spread) in spreads.items():
        noise = np.random.default_rng([zlib.crc32(name.encode()), seed]).standard_normal(out[name].shape)
        drawn = base * np.exp(spread * noise) if base else spread * noise
        out[name] = jnp.asarray(drawn.astype(out[name].dtype))
    for name, factor in factors.items():
        out[name] = (out[name] * factor).astype(out[name].dtype)
    return out
```

```python
import numpy as np
from contextlib import ExitStack

import concourse.bass as bass
from concourse import mybir

F32 = mybir.dt.float32
F16 = mybir.dt.float16
BF16 = mybir.dt.bfloat16
I32 = mybir.dt.int32
U32 = mybir.dt.uint32
ALU = mybir.AluOpType
ACT = mybir.ActivationFunctionType
AX = mybir.AxisListType

P = 128
D = 256
DC = D // P
NB, SQ, LK = 16, 256, 77
NTOK = NB * SQ
NT = NTOK // P
H, DH = 16, 16
HG = 8
NG = H // HG
EPS = 1e-5
E0, K0, M0 = 8, 2, 512
E1, K1, M1 = 32, 4, 128
MS = 512
NS0 = NTOK * K0 // P + E0
NS1 = NTOK * K1 // P + E1
MID = NTOK // 2


class At:

    def __init__(self, loop, mul, off):
        self.loop, self.mul, self.off = loop, mul, off

    @property
    def n(self):
        return self.off if self.loop is None else self.loop * self.mul + self.off

    def shift(self, d):
        return At(self.loop, self.mul, self.off + d)

    def div(self, k):
        return At(self.loop, self.mul // k, self.off // k)

    def mod(self, k):
        return self.off % k

    def within(self, count):
        return self.loop is not None or 0 <= self.off < count


def steps(eng, first, last, total, body, step):
    for s in range(first):
        step(At(None, 0, s))
    with eng.Fori(0, (last - first) // body) as i:
        for u in range(body):
            step(At(i, body, first + u))
    for s in range(last, total):
        step(At(None, 0, s))


def wait(eng, sem, count):
    if isinstance(count, int) and count <= 0:
        return
    eng.wait_ge(sem, count)


def semaphores(nc, ctx, prefix):
    taken = []

    def clear():
        nc.clear_and_free_semaphores(taken)
        nc.all_engine_barrier()

    def sem(name):
        taken.append(nc.alloc_semaphore(prefix + name))
        return taken[-1]

    ctx.callback(clear)
    return sem


def wait_alone(eng, sem, count, s_passed):
    if isinstance(count, int) and count <= 0:
        return
    eng.wait_ge(sem, count)
    eng.sem_inc(s_passed, 1)


def inverse_root(pool, out, var, minus_half, s_eps, s_rstd, t):
    pool.tensor_scalar(out, var, EPS, None, ALU.add).then_inc(s_eps, 1)
    pool.wait_ge(s_eps, t.n + 1)
    pool.tensor_tensor(out, out, minus_half, ALU.pow).then_inc(s_rstd, 1)


class LayerNorm:

    def __init__(self, sb, sem, name, s_passed, minus_half):
        self.minus_half, self.s_eps = minus_half, sem(f"{name}_eps")
        self.stats = [sb(f"{name}_stats{i}", [P, 6]) for i in range(2)]
        self.mv = [sb(f"{name}_mv{i}", [P, 2]) for i in range(2)]
        self.rstd = [sb(f"{name}_rstd{i}", [P, 1]) for i in range(2)]
        self.s_stats, self.s_mv, self.s_rstd = (sem(f"{name}_{n}") for n in ("stats", "mv", "rstd"))
        self.s_passed = s_passed

    def moments(self, dve, x, t):
        p = t.mod(2)
        dve.bn_stats(self.stats[p][:, :], x).then_inc(self.s_stats, 1)
        wait_alone(dve, self.s_stats, t.n + 1, self.s_passed[0])
        dve.bn_aggr(self.mv[p][:, :], self.stats[p][:, :]).then_inc(self.s_mv, 1)

    def invert(self, pool, t):
        p = t.mod(2)
        wait_alone(pool, self.s_mv, t.n + 1, self.s_passed[1])
        inverse_root(pool, self.rstd[p][:, :], self.mv[p][:, 1:2], self.minus_half[:, 0:1], self.s_eps, self.s_rstd, t)

    def apply(self, dve, x, out, t):
        p = t.mod(2)
        dve.wait_ge(self.s_rstd, t.n + 1)
        return dve.tensor_scalar(out, x, self.mv[p][:, 0:1], self.rstd[p][:, :], ALU.subtract, ALU.mult)


def heads_of(ap):
    return ap.rearrange("p (h d) -> p h d", d=DH)


def qkv_phase(nc, g):
    ctx = ExitStack()
    with ctx:
        def sb(name, shape, dt=F32):
            return ctx.enter_context(nc.sbuf_tensor("qkv_" + name, shape, dt))

        sem = semaphores(nc, ctx, "qkv_")

        wq, wk, wv = (sb(n, [P, 3 * D]) for n in ("wq", "wk", "wv"))
        wmean = sb("wmean", [P, 2, 3 * H])
        gb = sb("gb", [P, 6])
        ctx_b = [sb(f"ctx_b{i}", [P, DC * LK]) for i in range(2)]
        ksq = [sb(f"ksq{i}", [P, D]) for i in range(2)]
        kn = [sb(f"kn{i}", [P, D]) for i in range(2)]
        kvar = [sb(f"kvar{i}", [P, H]) for i in range(2)]
        krstd = [sb(f"krstd{i}", [P, H]) for i in range(2)]
        x_in = [sb(f"x_in{i}", [P, D]) for i in range(2)]
        xn = [sb(f"xn{i}", [P, D]) for i in range(2)]
        xnT = [sb(f"xnT{i}", [P, D]) for i in range(2)]
        qsq = [sb(f"qsq{i}", [P, D]) for i in range(2)]
        qn = [sb(f"qn{i}", [P, D]) for i in range(2)]
        qvar = [sb(f"qvar{i}", [P, H]) for i in range(2)]
        qrstd = [sb(f"qrstd{i}", [P, H]) for i in range(2)]
        s_w, s_gb, s_wm, s_wc, s_gs, s_ones, s_v1, s_half = (sem(n) for n in (
            "s_w", "s_gb", "s_wm", "s_wc", "s_gs", "s_ones", "s_v1", "s_half"))
        s_ctx = [sem(f"s_ctx{i}") for i in range(2)]
        s_x = [sem(f"s_x{i}") for i in range(2)]
        k_mm, v_mm, k_sq, k_var, k_rstd, k_norm, k_t, k_out, v_out = (sem(n) for n in (
            "k_mm", "v_mm", "k_sq", "k_var", "k_rstd", "k_norm", "k_t", "k_out", "v_out"))
        passed = [sem(f"passed_{n}") for n in ("dve", "pool", "act")]
        ln = LayerNorm(sb, sem, "ln", passed, g.minus_half)
        x_norm, x_t, x_out, q_mm, q_sq, q_var, q_rstd, q_norm, q_t, q_out = (sem(n) for n in (
            "x_norm", "x_t", "x_out", "q_mm", "q_sq", "q_var", "q_rstd", "q_norm", "q_t", "q_out"))
        k_eps, q_eps = sem("k_eps"), sem("q_eps")
        ps_k, ps_v, ps_kt = g.bank[0], g.bank[1], g.bank[2]
        ps_xt, ps_q, ps_qt = g.bank[3:5], g.bank[5:7], g.bank[7]
        block = ctx.enter_context(nc.Block())

        @block.sync
        def _(sp):
            for dst, src in ((wq, g.ins["wq"]), (wk, g.ins["wk"]), (wv, g.ins["wv"]), (g.ident, g.ins["ident"])):
                sp.dma_start(dst[:, :], src).then_inc(s_w, 16)
            sp.dma_start(gb[:, 0:4], g.ins["gb"]).then_inc(s_gb, 16)

            def load_ctx(b):
                wait(sp, v_mm, b.shift(-1).n)
                sp.dma_start(ctx_b[b.mod(2)][:, :], g.ins["ctx"][bass.ds(b.n * P, P), :]).then_inc(s_ctx[b.mod(2)], 16)

            def load_x(t):
                wait(sp, x_norm, t.shift(-1).n)
                sp.dma_start(x_in[t.mod(2)][:, :], g.ins["x"][bass.ds(t.n * P, P), :]).then_inc(s_x[t.mod(2)], 16)

            steps(sp, 2, NB, NB, 2, load_ctx)
            steps(sp, 2, NT, NT, 2, load_x)

        @block.gpsimd
        def _(pool):
            pool.memset(g.ones[:, :], 1.0).then_inc(s_ones, 1)
            pool.memset(g.minus_half[:, :], -0.5).then_inc(s_half, 1)
            pool.wait_ge(s_half, 1)
            pool.memset(g.v_all[:, :], 1.0).then_inc(s_v1, 1)

            def invert(b, s_var, s_rstd, var, rstd, s_eps, rows):
                p = b.mod(2)
                wait_alone(pool, s_var, b.n + 1, passed[1])
                inverse_root(pool, rstd[p][0:rows, :], var[p][0:rows, :], g.minus_half[0:rows, :], s_eps, s_rstd, b)

            steps(pool, 2, NB, NB, 2, lambda b: invert(b, k_var, k_rstd, kvar, krstd, k_eps, LK))

            def tile(s):
                if s.within(NT):
                    ln.invert(pool, s)
                t = s.shift(-2)
                if t.within(NT):
                    invert(t, q_var, q_rstd, qvar, qrstd, q_eps, P)

            steps(pool, 6, NT, NT + 2, 2, tile)

        @block.vector
        def _(dve):
            dve.wait_ge(s_w, 64)
            for j, w in enumerate((wq, wk)):
                dve.tensor_reduce(wmean[:, j, :], heads_of(w[:, :]), AX.X, ALU.add).then_inc(s_wm, 1)
                dve.wait_ge(s_wm, 2 * j + 1)
                dve.tensor_scalar(wmean[:, j, :], wmean[:, j, :], 1.0 / DH, None, ALU.mult).then_inc(s_wm, 1)
                dve.wait_ge(s_wm, 2 * j + 2)
                dve.tensor_tensor(heads_of(w[:, :]), heads_of(w[:, :]),
                                  wmean[:, j, :].unsqueeze(2).broadcast_to([P, 3 * H, DH]),
                                  ALU.subtract).then_inc(s_wc, 1)
            dve.wait_ge(s_gb, 16)
            dve.tensor_scalar(gb[:, 4:6], gb[:, 0:2], float(DH) ** -0.5, None, ALU.mult).then_inc(s_gs, 1)

            def sum_k(b):
                p = b.mod(2)
                dve.wait_ge(k_sq, b.n + 1)
                dve.tensor_reduce(kvar[p][0:LK, :], heads_of(ksq[p][0:LK, :]), AX.X, ALU.add).then_inc(k_var, 1)
            def norm_k(s):
                b = s.shift(-1)
                if b.within(NB):
                    apply_k(b)
                if s.within(NB):
                    sum_k(s)

            def apply_k(b):
                p = b.mod(2)
                dve.wait_ge(k_rstd, b.n + 1)
                wait(dve, k_t, b.shift(-1).n)
                dve.tensor_tensor(heads_of(kn[p][0:LK, :]), heads_of(ps_k[0:LK, 0:D]),
                                  krstd[p][0:LK, :].unsqueeze(2).broadcast_to([LK, H, DH]),
                                  ALU.mult).then_inc(k_norm, 1)

            steps(dve, 2, NB, NB + 1, 2, norm_k)

            def tile(s):
                t = s.shift(-3)
                if t.within(NT):
                    p = t.mod(2)
                    dve.wait_ge(q_rstd, t.n + 1)
                    wait(dve, q_t, t.shift(-1).n)
                    dve.tensor_tensor(heads_of(qn[p][:, :]), heads_of(ps_q[p][:, 0:D]),
                                      qrstd[p][:, :].unsqueeze(2).broadcast_to([P, H, DH]),
                                      ALU.mult).then_inc(q_norm, 1)
                t = s.shift(-1)
                if t.within(NT):
                    p = t.mod(2)
                    wait(dve, x_t, t.shift(-1).n)
                    ln.apply(dve, x_in[p][:, :], xn[p][:, :], t).then_inc(x_norm, 1)
                t = s
                if t.within(NT):
                    dve.wait_ge(s_x[t.mod(2)], (t.div(2).n + 1) * 16)
                    ln.moments(dve, x_in[t.mod(2)][:, :], t)
                t = s.shift(-2)
                if t.within(NT):
                    p = t.mod(2)
                    dve.wait_ge(q_sq, t.n + 1)
                    dve.tensor_reduce(qvar[p][:, :], heads_of(qsq[p][:, :]), AX.X, ALU.add).then_inc(q_var, 1)

            steps(dve, 6, NT, NT + 3, 2, tile)

        @block.scalar
        def _(act):
            act.wait_ge(s_v1, 1)
            act.wait_ge(s_gs, 1)

            def batch(s):
                b = s
                if b.within(NB):
                    p = b.mod(2)
                    act.wait_ge(k_mm, b.n + 1)
                    wait(act, k_var, b.shift(-1).n)
                    act.activation(ksq[p][0:LK, :], ps_k[0:LK, 0:D], ACT.Square, scale=DH ** -0.5).then_inc(k_sq, 1)
                    wait_alone(act, v_mm, b.n + 1, passed[2])
                    act.activation(
                        g.v_all[0:LK, bass.ds(b.n * (H * (DH + 1)), H * (DH + 1))]
                        .rearrange("p (h d) -> p h d", h=H)[:, :, 0:DH],
                        heads_of(ps_v[0:LK, 0:D]), ACT.Copy).then_inc(v_out, 1)
                b = s.shift(-1)
                if b.within(NB):
                    wait_alone(act, k_t, b.n + 1, passed[2])
                    for gr in range(NG):
                        last = act.activation(g.kT_all[:, bass.ds(b.n * (NG * LK) + gr * LK, LK)],
                                              ps_kt[:, gr * LK:(gr + 1) * LK], ACT.Identity,
                                              bias=gb[:, 3:4], scale=gb[:, 2:3])
                    last.then_inc(k_out, 1)

            steps(act, 2, NB, NB + 1, 2, batch)

            def tile(s):
                t = s.shift(-1)
                if t.within(NT):
                    p = t.mod(2)
                    act.wait_ge(x_t, t.n + 1)
                    wait(act, q_mm, t.shift(-1).n)
                    act.activation(xnT[p][:, :], ps_xt[p][:, 0:D], ACT.Copy).then_inc(x_out, 1)
                t = s.shift(-2)
                if t.within(NT):
                    p = t.mod(2)
                    act.wait_ge(q_mm, t.n + 1)
                    wait(act, q_var, t.shift(-1).n)
                    act.activation(qsq[p][:, :], ps_q[p][:, 0:D], ACT.Square, scale=DH ** -0.5).then_inc(q_sq, 1)
                t = s.shift(-4)
                if t.within(NT):
                    wait_alone(act, q_t, t.n + 1, passed[2])
                    act.activation(g.qT_all[:, bass.ds(t.n * D, D)], ps_qt[:, 0:D], ACT.Identity,
                                   bias=gb[:, 5:6], scale=gb[:, 4:5]).then_inc(q_out, 1)

            steps(act, 6, NT, NT + 4, 2, tile)

        @block.tensor
        def _(pe):
            pe.wait_ge(s_w, 64)
            pe.wait_ge(s_ones, 1)
            pe.wait_ge(s_wc, 2)

            def batch(s):
                b = s
                if b.within(NB):
                    p = b.mod(2)
                    pe.wait_ge(s_ctx[p], (b.div(2).n + 1) * 16)
                    wait(pe, k_norm, b.n)
                    for c in range(DC):
                        pe.matmul(ps_k[0:LK, 0:D], ctx_b[p][:, c * LK:(c + 1) * LK], wk[:, c * D:(c + 1) * D],
                                  start=(c == 0), stop=False)
                    pe.matmul(ps_k[0:LK, 0:D], g.ones[:, 0:LK], wk[:, 2 * D:3 * D], start=False, stop=True)\
                        .then_inc(k_mm, 1)
                    wait(pe, v_out, b.n)
                    for c in range(DC):
                        pe.matmul(ps_v[0:LK, 0:D], ctx_b[p][:, c * LK:(c + 1) * LK], wv[:, c * D:(c + 1) * D],
                                  start=(c == 0), stop=False)
                    pe.matmul(ps_v[0:LK, 0:D], g.ones[:, 0:LK], wv[:, 2 * D:3 * D], start=False, stop=True)\
                        .then_inc(v_mm, 1)
                b = s.shift(-1)
                if b.within(NB):
                    p = b.mod(2)
                    pe.wait_ge(k_norm, b.n + 1)
                    wait(pe, k_out, b.n)
                    for gr in range(NG):
                        last = pe.transpose(ps_kt[:, gr * LK:(gr + 1) * LK], kn[p][0:LK, gr * P:(gr + 1) * P],
                                            g.ident[0:LK, 0:LK])
                    last.then_inc(k_t, 1)

            steps(pe, 2, NB, NB + 1, 2, batch)

            def tile(s):
                t = s.shift(-1)
                if t.within(NT):
                    p = t.mod(2)
                    pe.wait_ge(x_norm, t.n + 1)
                    wait(pe, x_out, t.shift(-1).n)
                    for c in range(DC):
                        last = pe.transpose(ps_xt[p][:, c * P:(c + 1) * P], xn[p][:, c * P:(c + 1) * P], g.ident[:, :])
                    last.then_inc(x_t, 1)
                t = s.shift(-2)
                if t.within(NT):
                    p = t.mod(2)
                    pe.wait_ge(x_out, t.n + 1)
                    wait(pe, q_norm, t.shift(-1).n)
                    for c in range(DC):
                        pe.matmul(ps_q[p][:, 0:D], xnT[p][:, c * P:(c + 1) * P], wq[:, c * D:(c + 1) * D],
                                  start=(c == 0), stop=False)
                    pe.matmul(ps_q[p][:, 0:D], g.ones[:, :], wq[:, 2 * D:3 * D], start=False, stop=True)\
                        .then_inc(q_mm, 1)
                t = s.shift(-4)
                if t.within(NT):
                    p = t.mod(2)
                    pe.wait_ge(q_norm, t.n + 1)
                    wait(pe, q_out, t.n)
                    for c in range(DC):
                        last = pe.transpose(ps_qt[:, c * P:(c + 1) * P], qn[p][:, c * P:(c + 1) * P], g.ident[:, :])
                    last.then_inc(q_t, 1)

            steps(pe, 6, NT, NT + 4, 2, tile)


def top_of(dve, g, scores, top, ix, t, s_scores, s_top, s_ix, passed):
    wait_alone(dve, s_scores, t.n + 1, passed[0])
    dve.max(top[:, :], scores[:, :]).then_inc(s_top, 1)
    wait_alone(dve, s_top, t.n + 1, passed[0])
    dve.max_index(ix[:, :], top[:, :], scores[:, :]).then_inc(s_ix, 1)
    dve.tensor_copy(g.top_v[:, bass.ds(t.n * 8, 8)], top[:, :])
    wait_alone(dve, s_ix, t.n + 1, passed[0])
    dve.tensor_copy(g.top_i[:, bass.ds(t.n * 8, 8)], ix[:, :])


def attention0_phase(nc, g):
    ctx = ExitStack()
    with ctx:
        def sb(name, shape, dt=F32):
            return ctx.enter_context(nc.sbuf_tensor("at0_" + name, shape, dt))

        sem = semaphores(nc, ctx, "at0_")

        NU = NT * NG
        VW = H * (DH + 1)
        HW = HG * LK // 2
        wp = sb("wp", [P, DC * D])
        wr = sb("wr", [P, DC * E0])
        bp = sb("bp", [P, D])
        hmask = sb("hmask", [P, HG])
        q_s = [sb(f"q_s{i}", [P, D]) for i in range(2)]
        kblk = [sb(f"kblk{i}", [P, NG * HG * LK]) for i in range(2)]
        v_s = [sb(f"v_s{i}", [P, VW]) for i in range(2)]
        x_in = [sb(f"x_in{i}", [P, D]) for i in range(2)]
        xb = [sb(f"xb{i}", [P, D]) for i in range(2)]
        mx = [sb(f"mx{i}", [P, HG]) for i in range(2)]
        pr = [sb(f"pr{i}", [P, HG * LK]) for i in range(2)]
        prT = [sb(f"prT{i}", [P, HG * P]) for i in range(2)]
        rec = [sb(f"rec{i}", [P, H]) for i in range(2)]
        o = [sb(f"o{i}", [P, D]) for i in range(2)]
        oT = [sb(f"oT{i}", [P, D]) for i in range(2)]
        x1 = [sb(f"x1{i}", [P, D]) for i in range(2)]
        xn = [sb(f"xn{i}", [P, D]) for i in range(2)]
        xnT = [sb(f"xnT{i}", [P, D]) for i in range(2)]
        lg = [sb(f"lg{i}", [P, E0]) for i in range(2)]
        top = [sb(f"top{i}", [P, 8]) for i in range(2)]
        ix = [sb(f"ix{i}", [P, 8], U32) for i in range(2)]
        s_w, s_next = sem("s_w"), sem("s_next")
        s_x, x1_st, xn_st = ([sem(f"{n}{i}") for i in range(2)] for n in ("s_x", "x1_st", "xn_st"))
        kv_ready, q_ready, xb_ready, s_mm, mx_ready, sub_done, exp_done, tp_mm, tp_out, pv_mm, rec_ready, o_norm = (
            sem(n) for n in ("kv_ready", "q_ready", "xb_ready", "s_mm", "mx_ready", "sub_done", "exp_done", "tp_mm",
                             "tp_out", "pv_mm", "rec_ready", "o_norm"))
        o_t, o_out, wp_mm, x1_done, x_norm, x_t, x_out, r_mm, lg_done, m8_done, ix_done = (
            sem(n) for n in ("o_t", "o_out", "wp_mm", "x1_done", "x_norm", "x_t", "x_out", "r_mm", "lg_done",
                             "m8_done", "ix_done"))
        passed = [sem(f"passed_{n}") for n in ("dve", "pool", "act")]
        ln = LayerNorm(sb, sem, "ln", passed, g.minus_half)
        ps_s, ps_tp = g.pair[0], g.pair[1]
        ps_o, ps_ot, ps_wp, ps_x = g.bank[4:8]
        block = ctx.enter_context(nc.Block())
        T_O, T_WP, T_X, T_R = 5, 6, 8, 9
        FIRST, BODY, TOTAL = 16, 8, NU + T_R + 1

        def tile_at(u, skew):
            s = u.shift(-skew)
            return s.div(2) if s.mod(2) == 0 and s.within(NU) else None

        @block.sync
        def _(sp):
            for dst, src in ((wp, g.ins["wp"]), (wr, g.ins["wr0"]), (bp, g.ins["bp"]), (hmask, g.ins["hmask"])):
                sp.dma_start(dst[:, :], src).then_inc(s_w, 16)
            for dst, src in ((g.tri, g.ins["tri"]), (g.iota, g.ins["iota"]), (g.iota16, g.ins["iota16"]),
                             (g.not_first, g.ins["not_first"]), (g.tokval, g.ins["tokval"])):
                sp.dma_start(dst[:, :], src).then_inc(s_next, 16)
            n = DC * 2 * M0
            for e in range(E0):
                sp.dma_start(g.w13[:, e * n:(e + 1) * n], g.ins["w13"][:, e * n:(e + 1) * n]).then_inc(s_next, 16)

            def tile(s):
                t = s
                if t.within(NT):
                    wait(sp, xb_ready, t.shift(-1).n)
                    sp.dma_start(x_in[t.mod(2)][:, :], g.ins["x"][bass.ds(t.n * P, P), :]).then_inc(s_x[t.mod(2)], 16)
                t = s.shift(-4)
                if t.within(NT):
                    p = t.mod(2)
                    sp.wait_ge(x1_done, t.n + 1)
                    sp.dma_start(g.x1[bass.ds(t.n * P, P), :], x1[p][:, :]).then_inc(x1_st[p], 16)
                    sp.wait_ge(x_norm, t.n + 1)
                    sp.dma_start(g.xn[bass.ds(t.n * P, P), :], xn[p][:, :]).then_inc(xn_st[p], 16)

            steps(sp, 6, NT, NT + 4, 2, tile)
            for p in range(2):
                sp.wait_ge(x1_st[p], NT // 2 * 16)
                sp.wait_ge(xn_st[p], NT // 2 * 16)
            sp.wait_ge(s_next, (5 + E0) * 16)

        @block.gpsimd
        def _(pool):
            pool.wait_ge(s_w, 64)

            def half(u):
                t = tile_at(u, 0)
                if t is not None:
                    p, b = t.mod(2), t.div(2)
                    if t.mod(2) == 0:
                        bp_ = b.mod(2)
                        wait_alone(pool, s_mm, b.shift(-1).n * 4, passed[1])
                        for gr in range(NG):
                            kT = g.kT_all[:, bass.ds(b.n * (NG * LK) + gr * LK, LK)]
                            pool.tensor_tensor(
                                kblk[bp_][:, gr * HG * LK:(gr + 1) * HG * LK].rearrange("p (h k) -> p h k", h=HG),
                                kT.unsqueeze(1).broadcast_to([P, HG, LK]),
                                hmask[:, :].unsqueeze(2).broadcast_to([P, HG, LK]), ALU.mult).then_inc(kv_ready, 1)
                        wait_alone(pool, pv_mm, b.shift(-1).n * 4, passed[1])
                        pool.tensor_copy(v_s[bp_][0:LK, :], g.v_all[0:LK, bass.ds(b.n * VW, VW)]).then_inc(kv_ready, 1)
                    wait_alone(pool, s_mm, t.shift(-1).n * 2, passed[1])
                    pool.tensor_copy(q_s[p][:, :], g.qT_all[:, bass.ds(t.n * D, D)]).then_inc(q_ready, 1)
                t = tile_at(u, 4)
                if t is not None:
                    p = t.mod(2)
                    pool.wait_ge(s_x[p], (t.div(2).n + 1) * 16)
                    wait(pool, x1_done, t.shift(-1).n)
                    pool.tensor_tensor(xb[p][:, :], x_in[p][:, :], bp[:, :], ALU.add).then_inc(xb_ready, 1)
                t = tile_at(u, T_WP)
                if t is not None:
                    ln.invert(pool, t)

            steps(pool, FIRST, NU, TOTAL, BODY, half)

        @block.vector
        def _(dve):
            def half(u):
                if u.within(NU):
                    p = u.mod(2)
                    s3 = ps_s[:, :, 0:HW].rearrange("p a (h k) -> p a h k", k=LK)
                    dve.wait_ge(s_mm, u.n + 1)
                    dve.tensor_reduce(mx[p][:, :].rearrange("p (a h) -> p a h", a=2), s3, AX.X, ALU.max)\
                        .then_inc(mx_ready, 1)
                    dve.wait_ge(mx_ready, u.n + 1)
                    wait(dve, tp_mm, u.shift(-1).n)
                    dve.tensor_tensor(
                        pr[p][:, :].rearrange("p (a h k) -> p a h k", a=2, k=LK), s3,
                        mx[p][:, :].rearrange("p (a h) -> p a h", a=2).unsqueeze(3).broadcast_to([P, 2, HG // 2, LK]),
                        ALU.subtract).then_inc(sub_done, 1)
                t = tile_at(u, 3)
                if t is not None:
                    p = t.mod(2)
                    ov = ps_o[:, 0:VW].rearrange("p (h d) -> p h d", h=H)
                    dve.wait_ge(pv_mm, t.n * 2 + 2)
                    dve.reciprocal(rec[p][:, :].unsqueeze(2), ov[:, :, DH:DH + 1]).then_inc(rec_ready, 1)
                    dve.wait_ge(rec_ready, t.n + 1)
                    wait(dve, o_t, t.shift(-1).n)
                    dve.tensor_tensor(heads_of(o[p][:, :]), ov[:, :, 0:DH],
                                      rec[p][:, :].unsqueeze(2).broadcast_to([P, H, DH]), ALU.mult).then_inc(o_norm, 1)
                t = tile_at(u, T_WP + 1)
                if t is not None:
                    p = t.mod(2)
                    wait(dve, xn_st[p], t.div(2).n * 16)
                    wait(dve, x_t, t.shift(-1).n)
                    ln.apply(dve, x1[p][:, :], xn[p][:, :], t).then_inc(x_norm, 1)
                t = tile_at(u, T_WP)
                if t is not None:
                    p = t.mod(2)
                    dve.wait_ge(wp_mm, t.n + 1)
                    dve.wait_ge(xb_ready, t.n + 1)
                    wait(dve, x1_st[p], t.div(2).n * 16)
                    dve.tensor_tensor(x1[p][:, :], ps_wp[:, 0:D], xb[p][:, :], ALU.add).then_inc(x1_done, 1)
                    dve.wait_ge(x1_done, t.n + 1)
                    ln.moments(dve, x1[p][:, :], t)
                t = tile_at(u, T_R)
                if t is not None:
                    p = t.mod(2)
                    dve.wait_ge(r_mm, t.n + 1)
                    dve.tensor_copy(lg[p][:, :], ps_x[:, D:D + E0]).then_inc(lg_done, 1)
                    top_of(dve, g, lg[p], top[p], ix[p], t, lg_done, m8_done, ix_done, passed)

            steps(dve, FIRST, NU, TOTAL, BODY, half)

        @block.scalar
        def _(act):
            def half(u):
                v = u.shift(-1)
                if v.within(NU):
                    p = v.mod(2)
                    act.wait_ge(tp_mm, v.n + 1)
                    wait(act, pv_mm, v.shift(-1).n)
                    act.activation(prT[p][0:LK, :].rearrange("p (a k) -> p a k", a=2), ps_tp[0:LK, :, :], ACT.Copy)\
                        .then_inc(tp_out, 1)
                if u.within(NU):
                    p = u.mod(2)
                    act.wait_ge(sub_done, u.n + 1)
                    act.activation(pr[p][:, :], pr[p][:, :], ACT.Exp).then_inc(exp_done, 1)
                t = tile_at(u, T_O)
                if t is not None:
                    p = t.mod(2)
                    act.wait_ge(o_t, t.n + 1)
                    wait(act, wp_mm, t.shift(-1).n)
                    act.activation(oT[p][:, :], ps_ot[:, 0:D], ACT.Copy).then_inc(o_out, 1)
                t = tile_at(u, T_X)
                if t is not None:
                    p = t.mod(2)
                    act.wait_ge(x_t, t.n + 1)
                    wait(act, r_mm, t.shift(-1).n)
                    act.activation(xnT[p][:, :], ps_x[:, 0:D], ACT.Copy).then_inc(x_out, 1)

            steps(act, FIRST, NU, TOTAL, BODY, half)

        @block.tensor
        def _(pe):
            pe.wait_ge(s_w, 64)

            def half(u):
                if u.within(NU):
                    gr, t = u.mod(2), u.div(2)
                    p, b = t.mod(2), t.div(2)
                    pe.wait_ge(kv_ready, b.n * 3 + 3)
                    pe.wait_ge(q_ready, t.n + 1)
                    wait(pe, sub_done, u.n)
                    for a in range(2):
                        last = pe.matmul(ps_s[:, a, 0:HW], q_s[p][:, gr * P:(gr + 1) * P],
                                         kblk[b.mod(2)][:, (2 * gr + a) * HW:(2 * gr + a + 1) * HW],
                                         start=True, stop=True)
                    last.then_inc(s_mm, 1)
                v = u.shift(-1)
                if v.within(NU):
                    p = v.mod(2)
                    pe.wait_ge(exp_done, v.n + 1)
                    wait(pe, tp_out, v.n)
                    for h in range(HG):
                        last = pe.transpose(ps_tp[0:LK, h // 4, (h % 4) * P:(h % 4 + 1) * P],
                                            pr[p][:, h * LK:(h + 1) * LK], g.ident[:, :])
                    last.then_inc(tp_mm, 1)
                v = u.shift(-2)
                if v.within(NU):
                    p, gr, t = v.mod(2), v.mod(2), v.div(2)
                    b = t.div(2)
                    pe.wait_ge(tp_out, v.n + 1)
                    if gr == 0:
                        wait(pe, o_norm, t.n)
                    for h in range(HG):
                        c = (gr * HG + h) * (DH + 1)
                        last = pe.matmul(ps_o[:, c:c + DH + 1], prT[p][0:LK, h * P:(h + 1) * P],
                                         v_s[b.mod(2)][0:LK, c:c + DH + 1], start=True, stop=True)
                    last.then_inc(pv_mm, 1)
                t = tile_at(u, T_O)
                if t is not None:
                    p = t.mod(2)
                    pe.wait_ge(o_norm, t.n + 1)
                    wait(pe, o_out, t.n)
                    for c in range(DC):
                        last = pe.transpose(ps_ot[:, c * P:(c + 1) * P], o[p][:, c * P:(c + 1) * P], g.ident[:, :])
                    last.then_inc(o_t, 1)
                t = tile_at(u, T_WP)
                if t is not None:
                    p = t.mod(2)
                    pe.wait_ge(o_out, t.n + 1)
                    wait(pe, x1_done, t.n)
                    for c in range(DC):
                        last = pe.matmul(ps_wp[:, 0:D], oT[p][:, c * P:(c + 1) * P], wp[:, c * D:(c + 1) * D],
                                         start=(c == 0), stop=(c == DC - 1))
                    last.then_inc(wp_mm, 1)
                t = tile_at(u, T_R)
                if t is not None:
                    p = t.mod(2)
                    pe.wait_ge(x_out, t.n + 1)
                    for c in range(DC):
                        last = pe.matmul(ps_x[:, D:D + E0], xnT[p][:, c * P:(c + 1) * P], wr[:, c * E0:(c + 1) * E0],
                                         start=(c == 0), stop=(c == DC - 1))
                    last.then_inc(r_mm, 1)
                t = tile_at(u, T_X)
                if t is not None:
                    p = t.mod(2)
                    pe.wait_ge(x_norm, t.n + 1)
                    wait(pe, x_out, t.n)
                    wait(pe, lg_done, t.n)
                    for c in range(DC):
                        last = pe.transpose(ps_x[:, c * P:(c + 1) * P], xn[p][:, c * P:(c + 1) * P], g.ident[:, :])
                    last.then_inc(x_t, 1)

            steps(pe, FIRST, NU, TOTAL, BODY, half)


class Router:

    def __init__(self, nc, ctx, sem, g, name, n_exp, k, n_slot_tiles, banks):
        self.g, self.E, self.K, self.NS = g, n_exp, k, n_slot_tiles

        def sb(n, shape, dt=F32):
            return ctx.enter_context(nc.sbuf_tensor(f"{name}_{n}", shape, dt))

        E, K, NS = n_exp, k, n_slot_tiles
        self.chosen = sb("chosen", [P, NT * K])
        self.onehot = sb("onehot", [P, NT * K * E], BF16)
        self.prod = sb("prod", [P, NT * K * E])
        self.pair = [sb(f"pair{i}", [P, NT * E], BF16) for i in range(2)]
        self.mask = sb("mask", [P, NT * E], BF16)
        self.tri16 = sb("tri16", [P, P], BF16)
        self.ones16 = sb("ones16", [P, P], BF16)
        self.zero16 = sb("zero16", [P, P], F16)
        self.tot = sb("tot", [P, E * NT])
        self.incl = sb("incl", [P, E * NT])
        self.first = sb("first", [P, NT * E])
        self.count_i = sb("count_i", [P, E], I32)
        self.tiles_i = sb("tiles_i", [P, E], I32)
        self.tiles = sb("tiles", [P, E])
        self.base = sb("base", [P, E])
        self.base_slot = sb("base_slot", [P, E])
        self.e_cmp = self.prod[0:1, :].bitcast(BF16)[:, 0:NS * E]
        self.e_sum = sb("e_sum", [1, NS])
        self.slot_f = sb("slot_f", [P, NT * K])
        self.lo_i = sb("lo_i", [P, NT * K], I32)
        self.hi_i = sb("hi_i", [P, NT * K], I32)
        self.lo = sb("lo", [P, NT * K])
        self.hi = sb("hi", [P, NT * K])
        self.at_lo = [sb(f"at_lo{i}", [P, P], F16) for i in range(4)]
        self.at_hi = [sb(f"at_hi{i}", [P, NS], F16) for i in range(4)]
        self.wsum = sb("wsum", [P, NT])
        self.wrec = sb("wrec", [P, NT])
        self.wexp = sb("wexp", [P, NT])
        self.done, self.s_mask, self.s_count, self.s_one, self.s_pair, self.s_table, self.s_wdiff, self.s_wexp = (
            sem(n) for n in ("done", "mask", "count", "one", "onehots", "table", "wdiff", "wexp"))
        self.ps_pos, self.ps_tot, self.ps_tab = banks

    def chunks(self):
        n = NT * self.E
        return [(i, min(n, i + 512)) for i in range(0, n, 512)]

    def tensor_counts(self, pe):
        pe.wait_ge(self.s_mask, 1)
        for j, (a, b) in enumerate(self.chunks()):
            pe.matmul(self.ps_pos[:, j, 0:b - a], self.tri16[:, :], self.mask[:, a:b], start=True, stop=True)
            last = pe.matmul(self.ps_tot[:, j, 0:b - a], self.ones16[:, :], self.mask[:, a:b], start=True, stop=True)
        last.then_inc(self.s_count, 1)

    def tensor_table(self, pe, c):
        pe.wait_ge(self.s_one, c.n + 1)
        pe.matmul(self.ps_tab[:, 0:self.NS], self.at_lo[c.mod(4)][:, :], self.at_hi[c.mod(4)][:, :],
                  start=False, stop=False).then_inc(self.s_pair, 1)

    def tensor_table_open(self, pe):
        pe.matmul(self.ps_tab[:, 0:self.NS], self.zero16[:, :], self.g.iota16[:, 0:self.NS], start=True, stop=False)

    def tensor_table_close(self, pe):
        pe.matmul(self.ps_tab[:, 0:self.NS], self.zero16[:, :], self.g.iota16[:, 0:self.NS], start=False, stop=True)\
            .then_inc(self.s_pair, 1)

    def vector(self, dve, weights):
        g, E, K, NS = self.g, self.E, self.K, self.NS
        links = [0]

        def link(ins):
            links[0] += 1
            ins.then_inc(self.done, 1)
            dve.wait_ge(self.done, links[0])

        top_i = g.top_i[:, :].rearrange("p (t k) -> p t k", k=8)[:, :, 0:K]
        tk = self.chosen[:, :].rearrange("p (t k) -> p t k", k=K)
        iota_e = g.iota[:, 0:E]
        onehot = self.onehot[:, :].rearrange("p (t k e) -> p t k e", k=K, e=E)
        dve.tensor_copy(self.tri16[:, :], g.tri[:, :])
        dve.tensor_copy(self.ones16[:, :], g.ones[:, :])
        dve.memset(self.zero16[:, :], 0.0)
        link(dve.tensor_copy(tk, top_i))
        link(dve.tensor_tensor(self.onehot[:, :].rearrange("p (c e) -> p c e", e=E),
                               iota_e.unsqueeze(1).broadcast_to([P, NT * K, E]),
                               self.chosen[:, :].unsqueeze(2).broadcast_to([P, NT * K, E]), ALU.is_equal))
        mask = self.mask[:, :].rearrange("p (t e) -> p t e", e=E)
        if K == 2:
            dve.tensor_tensor(mask, onehot[:, :, 0, :], onehot[:, :, 1, :], ALU.add).then_inc(self.s_mask, 1)
        else:
            halves = [x[:, :].rearrange("p (t e) -> p t e", e=E) for x in self.pair]
            dve.tensor_tensor(halves[0], onehot[:, :, 0, :], onehot[:, :, 1, :], ALU.add)
            link(dve.tensor_tensor(halves[1], onehot[:, :, 2, :], onehot[:, :, 3, :], ALU.add))
            dve.tensor_tensor(mask, halves[0], halves[1], ALU.add).then_inc(self.s_mask, 1)
        dve.wait_ge(self.s_count, 1)
        tot_et = self.tot[:, :].rearrange("p (e t) -> p t e", e=E)
        for j, (a, b) in enumerate(self.chunks()):
            last = dve.tensor_copy(tot_et[:, a // E:b // E, :],
                                   self.ps_tot[:, j, 0:b - a].rearrange("p (t e) -> p t e", e=E))
        link(last)
        link(dve.tensor_tensor_scan(self.incl[:, :], g.not_first[:, 0:E * NT], self.tot[:, :], 0.0, ALU.mult, ALU.add))
        incl3 = self.incl[:, :].rearrange("p (e t) -> p e t", t=NT)
        tot3 = self.tot[:, :].rearrange("p (e t) -> p e t", t=NT)
        link(dve.tensor_scalar(self.count_i[:, :].unsqueeze(2), incl3[:, :, NT - 1:NT], float(P - 1), None, ALU.add))
        link(dve.tensor_scalar(self.tiles_i[:, :], self.count_i[:, :], 7, None, ALU.arith_shift_right))
        link(dve.tensor_copy(self.tiles[:, :], self.tiles_i[:, :]))
        link(dve.tensor_tensor_scan(self.base[:, :], g.ones[:, 0:E], self.tiles[:, :], 0.0, ALU.mult, ALU.add))
        link(dve.tensor_tensor(self.base[:, :], self.base[:, :], self.tiles[:, :], ALU.subtract))
        link(dve.tensor_scalar(self.base_slot[:, :], self.base[:, :], float(P), None, ALU.mult))
        link(dve.tensor_tensor(incl3, incl3, tot3, ALU.subtract))
        link(dve.tensor_tensor(incl3, incl3, self.base_slot[:, :].unsqueeze(2).broadcast_to([P, E, NT]), ALU.add))
        first = self.first[:, :].rearrange("p (t e) -> p t e", e=E)
        incl_te = self.incl[:, :].rearrange("p (e t) -> p t e", t=NT)
        for j, (a, b) in enumerate(self.chunks()):
            last = dve.tensor_tensor(first[:, a // E:b // E, :],
                                     self.ps_pos[:, j, 0:b - a].rearrange("p (t e) -> p t e", e=E),
                                     incl_te[:, a // E:b // E, :], ALU.add)
        link(last)
        link(dve.tensor_tensor(self.prod[:, :].rearrange("p (t k e) -> p t k e", k=K, e=E), onehot,
                               first.unsqueeze(2).broadcast_to([P, NT, K, E]), ALU.mult))
        link(dve.tensor_reduce(self.slot_f[:, :], self.prod[:, :].rearrange("p (c e) -> p c e", e=E), AX.X, ALU.add))
        link(dve.tensor_copy(g.slot[:, 0:NT * K], self.slot_f[:, :]))
        dve.tensor_scalar(self.lo_i[:, :], g.slot[:, 0:NT * K], P - 1, None, ALU.bitwise_and)
        link(dve.tensor_scalar(self.hi_i[:, :], g.slot[:, 0:NT * K], 7, None, ALU.arith_shift_right))
        dve.tensor_copy(self.lo[:, :], self.lo_i[:, :])
        link(dve.tensor_copy(self.hi[:, :], self.hi_i[:, :]))

        def onehots(c):
            wait(dve, self.s_pair, c.shift(-3).n)
            dve.tensor_scalar(self.at_lo[c.mod(4)][:, :], g.iota16[:, 0:P], self.lo[:, bass.ds(c.n, 1)], None,
                              ALU.is_equal)
            dve.tensor_scalar(self.at_hi[c.mod(4)][:, :], g.iota16[:, 0:NS], self.hi[:, bass.ds(c.n, 1)],
                              g.tokval[:, bass.ds(c.div(K).n, 1)], ALU.is_equal, ALU.mult).then_inc(self.s_one, 1)

        steps(dve, 4, NT * K, NT * K, 4, onehots)
        dve.wait_ge(self.s_pair, NT * K + 1)
        dve.tensor_scalar(g.token[:, 0:NS], self.ps_tab[:, 0:NS], float(MID), None, ALU.add).then_inc(self.s_table, 1)
        link(dve.tensor_tensor(self.e_cmp.rearrange("p (j e) -> p j e", e=E),
                               self.base[0:1, :].unsqueeze(1).broadcast_to([1, NS, E]),
                               g.iota[0:1, 0:NS].unsqueeze(2).broadcast_to([1, NS, E]), ALU.is_le))
        link(dve.tensor_reduce(self.e_sum[0:1, :], self.e_cmp.rearrange("p (j e) -> p j e", e=E), AX.X, ALU.add))
        link(dve.tensor_scalar(g.expert[0:1, 0:NS], self.e_sum[0:1, :], -1.0, None, ALU.add))
        weights(dve, link)


def route0_phase(nc, g):
    ctx = ExitStack()
    with ctx:
        sem = semaphores(nc, ctx, "r0_")
        r = Router(nc, ctx, sem, g, "r0", E0, K0, NS0, (g.pair[0], g.pair[1], g.bank[4]))
        s_w2 = sem("w2")
        block = ctx.enter_context(nc.Block())
        top = g.top_v[:, :].rearrange("p (t k) -> p t k", k=8)
        w = g.weight[:, 0:NT * K0].rearrange("p (t k) -> p t k", k=K0)

        @block.sync
        def _(sp):
            for e in range(E0):
                n = M0 // P * D
                sp.dma_start(g.w2[:, e * n:(e + 1) * n], g.ins["w2"][:, e * n:(e + 1) * n]).then_inc(s_w2, 16)
            sp.wait_ge(s_w2, 16 * E0)

        @block.vector
        def _(dve):
            def weights(dve, link):
                dve.tensor_tensor(r.wsum[:, :].unsqueeze(2), top[:, :, 1:2], top[:, :, 0:1], ALU.subtract)\
                    .then_inc(r.s_wdiff, 1)
                dve.wait_ge(r.s_wexp, 1)
                link(dve.tensor_scalar(r.wsum[:, :], r.wexp[:, :], 1.0, None, ALU.add))
                link(dve.reciprocal(w[:, :, 0:1], r.wsum[:, :].unsqueeze(2)))
                link(dve.tensor_tensor(w[:, :, 1:2], w[:, :, 0:1], r.wexp[:, :].unsqueeze(2), ALU.mult))

            r.vector(dve, weights)

        @block.scalar
        def _(act):
            act.wait_ge(r.s_wdiff, 1)
            act.activation(r.wexp[:, :], r.wsum[:, :], ACT.Exp).then_inc(r.s_wexp, 1)

        @block.tensor
        def _(pe):
            r.tensor_counts(pe)
            r.tensor_table_open(pe)
            steps(pe, 4, NT * K0, NT * K0, 4, lambda c: r.tensor_table(pe, c))
            r.tensor_table_close(pe)


def moe0_phase(nc, g):
    ctx = ExitStack()
    with ctx:
        def sb(name, shape, dt=F32):
            return ctx.enter_context(nc.sbuf_tensor("m0_" + name, shape, dt))

        sem = semaphores(nc, ctx, "m0_")

        MC = M0 // P
        idx = [sb(f"idx{i}", [P, 1], I32) for i in range(2)]
        xg = [sb(f"xg{i}", [P, D]) for i in range(2)]
        xT = [sb(f"xT{i}", [P, D]) for i in range(2)]
        sg = [sb(f"sg{i}", [P, M0]) for i in range(2)]
        h = [sb(f"h{i}", [P, M0]) for i in range(2)]
        hT = [sb(f"hT{i}", [P, M0]) for i in range(2)]
        y = [sb(f"y{i}", [P, D]) for i in range(2)]
        passed = sem("passed_pool")
        s_g, y_st = ([sem(f"{n}{i}") for i in range(2)] for n in ("s_g", "y_st"))
        idx_ready, x_t, x_out, gu_mm, silu_done, h_done, h_t, h_out, y_mm, y_out = (
            sem(n) for n in ("idx_ready", "x_t", "x_out", "gu_mm", "silu_done", "h_done", "h_t", "h_out", "y_mm",
                             "y_out"))
        ps_gu, ps_x, ps_ht, ps_y = g.pair[0:2], g.bank[4], g.bank[5], g.bank[6]
        block = ctx.enter_context(nc.Block())

        @block.gpsimd
        def _(pool):
            def gather(j):
                p = j.mod(2)
                wait_alone(pool, x_t, j.shift(-1).n, passed)
                pool.tensor_copy(idx[p][:, :], g.token[:, bass.ds(j.n, 1)]).then_inc(idx_ready, 1)
                wait_alone(pool, idx_ready, j.n + 1, passed)
                pool.indirect_dma_start(out=xg[p][:, :], out_offset=None, in_=g.xn,
                                        in_offset=bass.IndirectOffsetOnAxis(ap=idx[p][:, :], axis=0))\
                    .then_inc(s_g[p], 16)

            steps(pool, 2, NS0, NS0, 2, gather)

        @block.sync
        def _(sp):
            def store(j):
                p = j.mod(2)
                sp.wait_ge(y_out, j.n + 1)
                sp.dma_start(g.y0[bass.ds(j.n * P, P), :], y[p][:, :]).then_inc(y_st[p], 16)

            steps(sp, 2, NS0, NS0, 2, store)
            for p in range(2):
                sp.wait_ge(y_st[p], NS0 // 2 * 16)

        @block.scalar
        def _(act):
            def step(s):
                j = s.shift(-2)
                if j.within(NS0):
                    p = j.mod(2)
                    act.wait_ge(h_t, j.n + 1)
                    wait(act, y_mm, j.shift(-1).n)
                    act.activation(hT[p][:, :], ps_ht[:, 0:M0], ACT.Copy).then_inc(h_out, 1)
                j = s
                if j.within(NS0):
                    p = j.mod(2)
                    act.wait_ge(x_t, j.n + 1)
                    wait(act, gu_mm, j.shift(-1).n)
                    act.activation(xT[p][:, :], ps_x[:, 0:D], ACT.Copy).then_inc(x_out, 1)
                j = s.shift(-1)
                if j.within(NS0):
                    p = j.mod(2)
                    act.wait_ge(gu_mm, j.n + 1)
                    wait(act, h_done, j.shift(-1).n)
                    act.activation(sg[p][:, :], ps_gu[p][:, 0, :], ACT.Silu).then_inc(silu_done, 1)

            steps(act, 4, NS0, NS0 + 2, 2, step)

        @block.vector
        def _(dve):
            def step(s):
                j = s.shift(-3)
                if j.within(NS0):
                    p = j.mod(2)
                    dve.wait_ge(y_mm, j.n + 1)
                    wait(dve, y_st[p], j.div(2).n * 16)
                    dve.tensor_copy(y[p][:, :], ps_y[:, 0:D]).then_inc(y_out, 1)
                j = s.shift(-1)
                if j.within(NS0):
                    p = j.mod(2)
                    dve.wait_ge(silu_done, j.n + 1)
                    wait(dve, h_t, j.shift(-1).n)
                    dve.tensor_tensor(h[p][:, :], ps_gu[p][:, 1, :], sg[p][:, :], ALU.mult).then_inc(h_done, 1)

            steps(dve, 6, NS0, NS0 + 3, 2, step)

        @block.tensor
        def _(pe):
            def step(s):
                j = s
                if j.within(NS0):
                    p = j.mod(2)
                    pe.wait_ge(s_g[p], (j.div(2).n + 1) * 16)
                    wait(pe, x_out, j.n)
                    for c in range(DC):
                        last = pe.transpose(ps_x[:, c * P:(c + 1) * P], xg[p][:, c * P:(c + 1) * P], g.ident[:, :])
                    last.then_inc(x_t, 1)
                j = s.shift(-1)
                if j.within(NS0):
                    p = j.mod(2)
                    e = pe.value_load(g.expert[0:1, bass.ds(j.n, 1)], min_val=0, max_val=E0 - 1)
                    pe.wait_ge(x_out, j.n + 1)
                    wait(pe, h_done, j.shift(-1).n)
                    for half in range(2):
                        for c in range(DC):
                            at = (c * 2 + half) * M0
                            last = pe.matmul(ps_gu[p][:, half, :], xT[p][:, c * P:(c + 1) * P],
                                             g.w13[:, bass.ds(e * (DC * 2 * M0) + at, M0)],
                                             start=(c == 0), stop=(c == DC - 1))
                    last.then_inc(gu_mm, 1)
                j = s.shift(-2)
                if j.within(NS0):
                    p = j.mod(2)
                    pe.wait_ge(h_done, j.n + 1)
                    wait(pe, h_out, j.n)
                    for c in range(MC):
                        last = pe.transpose(ps_ht[:, c * P:(c + 1) * P], h[p][:, c * P:(c + 1) * P], g.ident[:, :])
                    last.then_inc(h_t, 1)
                j = s.shift(-3)
                if j.within(NS0):
                    p = j.mod(2)
                    e = pe.value_load(g.expert[0:1, bass.ds(j.n, 1)], min_val=0, max_val=E0 - 1)
                    pe.wait_ge(h_out, j.n + 1)
                    wait(pe, y_out, j.n)
                    for c in range(MC):
                        last = pe.matmul(ps_y[:, 0:D], hT[p][:, c * P:(c + 1) * P],
                                         g.w2[:, bass.ds(e * (MC * D) + c * D, D)],
                                         start=(c == 0), stop=(c == MC - 1))
                    last.then_inc(y_mm, 1)

            steps(pe, 6, NS0, NS0 + 3, 2, step)


def attention1_phase(nc, g):
    ctx = ExitStack()
    with ctx:
        def sb(name, shape, dt=F32):
            return ctx.enter_context(nc.sbuf_tensor("at1_" + name, shape, dt))

        sem = semaphores(nc, ctx, "at1_")

        SCALE = float(D) ** -0.5
        wq, wk, wv, wo = (sb(n, [P, DC * D]) for n in ("wq", "wk", "wv", "wo"))
        wr = sb("wr", [P, DC * E1])
        qb, kb, qbs = (sb(n, [P, DC]) for n in ("qb", "kb", "qbs"))
        bv, bo, rb = sb("bv", [P, D]), sb("bo", [P, D]), sb("rb", [P, E1])
        ring = lambda name, shape, dt=F32, n=2: [sb(f"{name}{i}", shape, dt) for i in range(n)]
        idx = [ring(f"idx{k}_", [P, 1], I32) for k in range(K0)]
        yg = [ring(f"yg{k}_", [P, D]) for k in range(K0)]
        x1, x2, x2r, xb = (ring(n, [P, D]) for n in ("x1_", "x2_", "x2r", "xb"))
        xn, xnb = ring("xn", [P, D]), ring("xnb", [P, D], n=4)
        ctx_s = ring("ctx", [P, DC * LK])
        kT = ring("kT", [P, DC * LK])
        v = ring("v", [P, D])
        xnT, qT = ring("xnT", [P, D]), ring("qT", [P, D])
        nmx, den, rec = ring("nmx", [P, 1]), ring("den", [P, 1]), ring("rec", [P, 1])
        pr, prT = ring("pr", [P, LK]), ring("prT", [P, P])
        o, oT = ring("o", [P, D]), ring("oT", [P, D])
        x3, xm, xmT = ring("x3_", [P, D]), ring("xm", [P, D]), ring("xmT", [P, D])
        lg, lmx, ez, sume, rsum, sc = (ring(n, [P, w]) for n, w in (
            ("lg", E1), ("lmx", 1), ("ez", E1), ("sume", 1), ("rsum", 1), ("sc", E1)))
        top, ix = ring("top", [P, 8]), ring("ix", [P, 8], U32)
        s_w, s_next, s_qbs = sem("s_w"), sem("s_next"), sem("s_qbs")
        passed = [sem(f"passed_{n}") for n in ("dve", "pool", "act")]
        s_passed_sp = sem("passed_sp")
        lna = LayerNorm(sb, sem, "lna", passed, g.minus_half)
        lnm = LayerNorm(sb, sem, "lnm", passed, g.minus_half)
        s_x1, s_x2r, s_ctx, x2_st, x3_st, xm_st = ([sem(f"{n}{i}") for i in range(2)] for n in (
            "s_x1", "s_x2r", "s_ctx", "x2_st", "x3_st", "xm_st"))
        s_y = [[sem(f"s_y{k}_{i}") for i in range(2)] for k in range(K0)]
        (idx_ready, half_sum, x2_done, xn_done, xnb_ready, xb_ready, x_t, x_out, q_mm, q_out, kv_mm, kv_out, s_mm,
         max_done, exp_done, rec_done, p_t, p_out, pv_mm, o_done, o_t, o_out, wo_mm, x3_done, xm_done, xm_t, xm_out,
         r_mm, lg_done, lmx_done, ez_done, rsum_done, sc_done, top_done, ix_done) = (sem(n) for n in (
             "idx_ready", "half_sum", "x2_done", "xn_done", "xnb_ready", "xb_ready", "x_t", "x_out", "q_mm", "q_out",
             "kv_mm", "kv_out", "s_mm", "max_done", "exp_done", "rec_done", "p_t", "p_out", "pv_mm", "o_done", "o_t",
             "o_out", "wo_mm", "x3_done", "xm_done", "xm_t", "xm_out", "r_mm", "lg_done", "lmx_done", "ez_done",
             "rsum_done", "sc_done", "top_done", "ix_done"))
        ps_x, ps_q, ps_s, ps_t, ps_o, ps_wo, ps_m, ps_kv = g.bank
        block = ctx.enter_context(nc.Block())
        SUM, XN, Q, S, PT, PV, OT, WO, XM, XMT, R, SC = 1, 2, 3, 4, 5, 6, 7, 8, 9, 10, 11, 12
        FIRST, BODY = 12, 4

        def stage(s, skew):
            t = s.shift(-skew)
            return t if t.within(NT) else None

        def rows(t):
            return bass.ds(t.n * P, P)

        @block.sync
        def _(sp):
            for dst, src in ((wq, g.ins["wq1"]), (wk, g.ins["wk1"]), (wv, g.ins["wv1"]), (wo, g.ins["wo1"]), (wr, g.ins["wr1"]),
                             (qb, g.ins["bq1"]), (kb, g.ins["bk1"]), (bv, g.ins["bv1"]), (bo, g.ins["bo1"]), (rb, g.ins["rb1"])):
                sp.dma_start(dst[:, :], src).then_inc(s_w, 16)

            def step(s):
                if (t := stage(s, 0)) is not None:
                    p, b = t.mod(2), t.div(2)
                    wait(sp, x2_done, t.shift(-1).n)
                    sp.dma_start(x1[p][:, :], g.x1[rows(t), :]).then_inc(s_x1[p], 16)
                    if t.mod(2) == 0:
                        wait(sp, kv_mm, b.shift(-1).n)
                        sp.dma_start(ctx_s[b.mod(2)][:, :], g.ins["ctx"][rows(b), :]).then_inc(s_ctx[b.mod(2)], 16)
                if (t := stage(s, SUM + 1)) is not None:
                    p = t.mod(2)
                    sp.wait_ge(x2_done, t.n + 1)
                    sp.dma_start(g.x2[rows(t), :], x2[p][:, :]).then_inc(x2_st[p], 16)
                if (t := stage(s, PV)) is not None:
                    p = t.mod(2)
                    wait_alone(sp, x2_st[p], (t.div(2).n + 1) * 16, s_passed_sp)
                    wait(sp, xb_ready, t.shift(-1).n)
                    sp.dma_start(x2r[p][:, :], g.x2[rows(t), :]).then_inc(s_x2r[p], 16)
                if (t := stage(s, XM + 1)) is not None:
                    p = t.mod(2)
                    sp.wait_ge(x3_done, t.n + 1)
                    sp.dma_start(g.x3[rows(t), :], x3[p][:, :]).then_inc(x3_st[p], 16)
                    sp.wait_ge(xm_done, t.n + 1)
                    sp.dma_start(g.xn4[rows(t), :], xm[p][:, :]).then_inc(xm_st[p], 16)

            steps(sp, FIRST, NT, NT + XM + 2, BODY, step)
            for p in range(2):
                for st in (x2_st, x3_st, xm_st):
                    sp.wait_ge(st[p], NT // 2 * 16)
            sp.wait_ge(s_next, 4 * 16)

        @block.gpsimd
        def _(pool):
            pool.wait_ge(s_w, 160)

            def step(s):
                if (t := stage(s, 0)) is not None:
                    p = t.mod(2)
                    wait_alone(pool, x2_done, t.shift(-1).n, passed[1])
                    for k in range(K0):
                        pool.tensor_copy(idx[k][p][:, :], g.slot[:, bass.ds(t.n * K0 + k, 1)]).then_inc(idx_ready, 1)
                    wait_alone(pool, idx_ready, t.n * K0 + K0, passed[1])
                    for k in range(K0):
                        pool.indirect_dma_start(out=yg[k][p][:, :], out_offset=None, in_=g.y0,
                                                in_offset=bass.IndirectOffsetOnAxis(ap=idx[k][p][:, :], axis=0))\
                            .then_inc(s_y[k][p], 16)
                if (t := stage(s, SUM)) is not None:
                    lna.invert(pool, t)
                if (t := stage(s, XN)) is not None:
                    wait(pool, o_done, t.shift(-3).n)
                    pool.wait_ge(xn_done, t.n + 1)
                    pool.tensor_tensor(xnb[t.mod(4)][:, :], xn[t.mod(2)][:, :], bv[:, :], ALU.add).then_inc(xnb_ready, 1)
                if (t := stage(s, OT)) is not None:
                    p = t.mod(2)
                    wait(pool, x3_done, t.shift(-1).n)
                    pool.wait_ge(s_x2r[p], (t.div(2).n + 1) * 16)
                    pool.tensor_tensor(xb[p][:, :], x2r[p][:, :], bo[:, :], ALU.add).then_inc(xb_ready, 1)
                if (t := stage(s, WO)) is not None:
                    lnm.invert(pool, t)

            steps(pool, FIRST, NT, NT + WO, BODY, step)

        @block.vector
        def _(dve):
            dve.wait_ge(s_w, 160)
            dve.tensor_scalar(qbs[:, :], qb[:, :], SCALE, None, ALU.mult).then_inc(s_qbs, 1)

            def step(s):
                if (t := stage(s, S)) is not None:
                    p = t.mod(2)
                    dve.wait_ge(s_mm, t.n + 1)
                    dve.tensor_reduce(nmx[p][:, :], ps_s[:, 0:LK], AX.X, ALU.max, negate=True).then_inc(max_done, 1)
                if (t := stage(s, SC)) is not None:
                    p = t.mod(2)
                    dve.wait_ge(ez_done, t.n + 1)
                    dve.reciprocal(rsum[p][:, :], sume[p][:, :]).then_inc(rsum_done, 1)
                    dve.wait_ge(rsum_done, t.n + 1)
                    dve.tensor_scalar(sc[p][:, :], ez[p][:, :], rsum[p][:, :], None, ALU.mult).then_inc(sc_done, 1)
                    top_of(dve, g, sc[p], top[p], ix[p], t, sc_done, top_done, ix_done, passed)
                if (t := stage(s, PV)) is not None:
                    p = t.mod(2)
                    dve.wait_ge(pv_mm, t.n + 1)
                    dve.wait_ge(xnb_ready, t.n + 1)
                    dve.wait_ge(rec_done, t.n + 1)
                    wait(dve, o_t, t.shift(-1).n)
                    dve.scalar_tensor_tensor(o[p][:, :], ps_o[:, 0:D], rec[p][:, :], xnb[t.mod(4)][:, :],
                                             ALU.mult, ALU.add).then_inc(o_done, 1)
                if (t := stage(s, XN)) is not None:
                    p = t.mod(2)
                    wait(dve, x_t, t.shift(-1).n)
                    wait(dve, xnb_ready, t.shift(-1).n)
                    lna.apply(dve, x2[p][:, :], xn[p][:, :], t).then_inc(xn_done, 1)
                if (t := stage(s, XM)) is not None:
                    p = t.mod(2)
                    wait(dve, xm_st[p], t.div(2).n * 16)
                    wait(dve, xm_t, t.shift(-1).n)
                    lnm.apply(dve, x3[p][:, :], xm[p][:, :], t).then_inc(xm_done, 1)
                if (t := stage(s, WO)) is not None:
                    p = t.mod(2)
                    dve.wait_ge(wo_mm, t.n + 1)
                    dve.wait_ge(xb_ready, t.n + 1)
                    wait(dve, x3_st[p], t.div(2).n * 16)
                    dve.tensor_tensor(x3[p][:, :], ps_wo[:, 0:D], xb[p][:, :], ALU.add).then_inc(x3_done, 1)
                    dve.wait_ge(x3_done, t.n + 1)
                    lnm.moments(dve, x3[p][:, :], t)
                if (t := stage(s, R)) is not None:
                    p = t.mod(2)
                    dve.wait_ge(r_mm, t.n + 1)
                    wait(dve, ez_done, t.shift(-1).n)
                    dve.tensor_tensor(lg[p][:, :], ps_m[:, D:D + E1], rb[:, :], ALU.add).then_inc(lg_done, 1)
                    dve.wait_ge(lg_done, t.n + 1)
                    dve.tensor_reduce(lmx[p][:, :], lg[p][:, :], AX.X, ALU.max, negate=True).then_inc(lmx_done, 1)
                if (t := stage(s, SUM)) is not None:
                    p = t.mod(2)
                    dve.wait_ge(s_x1[p], (t.div(2).n + 1) * 16)
                    dve.wait_ge(s_y[0][p], (t.div(2).n + 1) * 16)
                    wait(dve, x2_st[p], t.div(2).n * 16)
                    dve.scalar_tensor_tensor(x2[p][:, :], yg[0][p][:, :], g.weight[:, bass.ds(t.n * K0, 1)],
                                             x1[p][:, :], ALU.mult, ALU.add).then_inc(half_sum, 1)
                    dve.wait_ge(s_y[1][p], (t.div(2).n + 1) * 16)
                    dve.wait_ge(half_sum, t.n + 1)
                    dve.scalar_tensor_tensor(x2[p][:, :], yg[1][p][:, :], g.weight[:, bass.ds(t.n * K0 + 1, 1)],
                                             x2[p][:, :], ALU.mult, ALU.add).then_inc(x2_done, 1)
                    dve.wait_ge(x2_done, t.n + 1)
                    lna.moments(dve, x2[p][:, :], t)
                if (t := stage(s, PT)) is not None:
                    p = t.mod(2)
                    dve.wait_ge(exp_done, t.n + 1)
                    dve.reciprocal(rec[p][:, :], den[p][:, :]).then_inc(rec_done, 1)

            steps(dve, FIRST, NT, NT + SC, BODY, step)

        @block.scalar
        def _(act):
            n = DC * 2 * M1
            for e in range(0, E1, 8):
                act.dma_start(g.gu[:, e * n:(e + 8) * n], g.ins["gu"][:, e * n:(e + 8) * n]).then_inc(s_next, 16)
            act.wait_ge(s_w, 160)
            act.wait_ge(s_qbs, 1)

            def step(s):
                if (t := stage(s, Q)) is not None:
                    p, b = t.mod(2), t.div(2)
                    if t.mod(2) == 0:
                        act.wait_ge(kv_mm, b.n + 1)
                        wait(act, s_mm, b.shift(-1).n * 2)
                        for c in range(DC):
                            act.activation(kT[b.mod(2)][:, c * LK:(c + 1) * LK], ps_kv[:, c * LK:(c + 1) * LK],
                                           ACT.Identity, bias=kb[:, c:c + 1]).then_inc(kv_out, 1)
                        wait(act, pv_mm, b.shift(-1).n * 2)
                        act.activation(v[b.mod(2)][0:LK, :], ps_kv[0:LK, D:2 * D], ACT.Copy).then_inc(kv_out, 1)
                    act.wait_ge(q_mm, t.n + 1)
                    wait(act, s_mm, t.shift(-1).n)
                    for c in range(DC):
                        act.activation(qT[p][:, c * P:(c + 1) * P], ps_q[:, c * P:(c + 1) * P], ACT.Identity,
                                       bias=qbs[:, c:c + 1], scale=SCALE).then_inc(q_out, 1)
                if (t := stage(s, S)) is not None:
                    p = t.mod(2)
                    act.wait_ge(max_done, t.n + 1)
                    wait(act, p_t, t.shift(-1).n)
                    wait(act, rec_done, t.shift(-1).n)
                    act.activation(pr[p][:, :], ps_s[:, 0:LK], ACT.Exp, bias=nmx[p][:, :],
                                   accum_out=den[p][:, :]).then_inc(exp_done, 1)
                if (t := stage(s, PT)) is not None:
                    p = t.mod(2)
                    act.wait_ge(p_t, t.n + 1)
                    wait(act, pv_mm, t.shift(-1).n)
                    act.activation(prT[p][0:LK, :], ps_t[0:LK, 0:P], ACT.Copy).then_inc(p_out, 1)
                if (t := stage(s, XN)) is not None:
                    p = t.mod(2)
                    act.wait_ge(x_t, t.n + 1)
                    wait(act, q_mm, t.shift(-1).n)
                    act.activation(xnT[p][:, :], ps_x[:, 0:D], ACT.Copy).then_inc(x_out, 1)
                if (t := stage(s, OT)) is not None:
                    p = t.mod(2)
                    act.wait_ge(o_t, t.n + 1)
                    wait(act, wo_mm, t.shift(-1).n)
                    act.activation(oT[p][:, :], ps_t[:, P:P + D], ACT.Copy).then_inc(o_out, 1)
                if (t := stage(s, XMT)) is not None:
                    p = t.mod(2)
                    wait_alone(act, xm_t, t.n + 1, passed[2])
                    act.activation(g.xn4T[:, :].rearrange("p (c n) -> p c n", c=DC)[:, :, rows(t)],
                                   ps_m[:, 0:D].rearrange("p (c n) -> p c n", c=DC), ACT.Copy)
                    wait(act, r_mm, t.shift(-1).n)
                    act.activation(xmT[p][:, :], ps_m[:, 0:D], ACT.Copy).then_inc(xm_out, 1)
                if (t := stage(s, R)) is not None:
                    p = t.mod(2)
                    act.wait_ge(lmx_done, t.n + 1)
                    wait(act, sc_done, t.shift(-1).n)
                    act.activation(ez[p][:, :], lg[p][:, :], ACT.Exp, bias=lmx[p][:, :],
                                   accum_out=sume[p][:, :]).then_inc(ez_done, 1)

            steps(act, FIRST, NT, NT + R + 1, BODY, step)

        @block.tensor
        def _(pe):
            pe.wait_ge(s_w, 160)

            def step(s):
                if (t := stage(s, Q)) is not None:
                    p, b = t.mod(2), t.div(2)
                    if t.mod(2) == 0:
                        cs = ctx_s[b.mod(2)]
                        pe.wait_ge(s_ctx[b.mod(2)], (b.div(2).n + 1) * 16)
                        wait(pe, kv_out, b.n * 3)
                        for m in range(DC):
                            for c in range(DC):
                                pe.matmul(ps_kv[:, m * LK:(m + 1) * LK], wk[:, c * D + m * P:c * D + (m + 1) * P],
                                          cs[:, c * LK:(c + 1) * LK], start=(c == 0), stop=(c == DC - 1))
                        for c in range(DC):
                            last = pe.matmul(ps_kv[0:LK, D:2 * D], cs[:, c * LK:(c + 1) * LK],
                                             wv[:, c * D:(c + 1) * D], start=(c == 0), stop=(c == DC - 1))
                        last.then_inc(kv_mm, 1)
                    pe.wait_ge(x_out, t.n + 1)
                    wait(pe, q_out, t.n * 2)
                    for m in range(DC):
                        for c in range(DC):
                            last = pe.matmul(ps_q[:, m * P:(m + 1) * P], wq[:, c * D + m * P:c * D + (m + 1) * P],
                                             xnT[p][:, c * P:(c + 1) * P], start=(c == 0), stop=(c == DC - 1))
                    last.then_inc(q_mm, 1)
                if (t := stage(s, S)) is not None:
                    p, b = t.mod(2), t.div(2)
                    pe.wait_ge(q_out, t.n * 2 + 2)
                    pe.wait_ge(kv_out, b.n * 3 + 3)
                    wait(pe, exp_done, t.n)
                    for c in range(DC):
                        last = pe.matmul(ps_s[:, 0:LK], qT[p][:, c * P:(c + 1) * P],
                                         kT[b.mod(2)][:, c * LK:(c + 1) * LK], start=(c == 0), stop=(c == DC - 1))
                    last.then_inc(s_mm, 1)
                if (t := stage(s, PT)) is not None:
                    p = t.mod(2)
                    pe.wait_ge(exp_done, t.n + 1)
                    wait(pe, p_out, t.n)
                    wait(pe, o_out, t.shift(-2).n)
                    pe.transpose(ps_t[0:LK, 0:P], pr[p][:, :], g.ident[:, :]).then_inc(p_t, 1)
                if (t := stage(s, PV)) is not None:
                    p, b = t.mod(2), t.div(2)
                    pe.wait_ge(p_out, t.n + 1)
                    wait(pe, o_done, t.n)
                    pe.matmul(ps_o[:, 0:D], prT[p][0:LK, :], v[b.mod(2)][0:LK, :], start=True, stop=True)\
                        .then_inc(pv_mm, 1)
                if (t := stage(s, WO)) is not None:
                    p = t.mod(2)
                    pe.wait_ge(o_out, t.n + 1)
                    wait(pe, x3_done, t.n)
                    for c in range(DC):
                        last = pe.matmul(ps_wo[:, 0:D], oT[p][:, c * P:(c + 1) * P], wo[:, c * D:(c + 1) * D],
                                         start=(c == 0), stop=(c == DC - 1))
                    last.then_inc(wo_mm, 1)
                if (t := stage(s, OT)) is not None:
                    p = t.mod(2)
                    pe.wait_ge(o_done, t.n + 1)
                    wait(pe, o_out, t.n)
                    if (q := stage(s, PT)) is not None:
                        pe.wait_ge(p_out, q.n + 1)
                    for c in range(DC):
                        last = pe.transpose(ps_t[:, (c + 1) * P:(c + 2) * P], o[p][:, c * P:(c + 1) * P], g.ident[:, :])
                    last.then_inc(o_t, 1)
                if (t := stage(s, R)) is not None:
                    p = t.mod(2)
                    pe.wait_ge(xm_out, t.n + 1)
                    for c in range(DC):
                        last = pe.matmul(ps_m[:, D:D + E1], xmT[p][:, c * P:(c + 1) * P], wr[:, c * E1:(c + 1) * E1],
                                         start=(c == 0), stop=(c == DC - 1))
                    last.then_inc(r_mm, 1)
                if (t := stage(s, XN)) is not None:
                    p = t.mod(2)
                    pe.wait_ge(xn_done, t.n + 1)
                    wait(pe, x_out, t.n)
                    for c in range(DC):
                        last = pe.transpose(ps_x[:, c * P:(c + 1) * P], xn[p][:, c * P:(c + 1) * P], g.ident[:, :])
                    last.then_inc(x_t, 1)
                if (t := stage(s, XMT)) is not None:
                    p = t.mod(2)
                    pe.wait_ge(xm_done, t.n + 1)
                    wait(pe, xm_out, t.n)
                    wait(pe, lg_done, t.n)
                    for c in range(DC):
                        last = pe.transpose(ps_m[:, c * P:(c + 1) * P], xm[p][:, c * P:(c + 1) * P], g.ident[:, :])
                    last.then_inc(xm_t, 1)

            steps(pe, FIRST, NT, NT + R + 1, BODY, step)


class SharedExpert:

    LAG = 5

    def __init__(self, nc, ctx, sem, g, name, first_block, blocks, banks):
        def sb(n, shape, dt=F32):
            return ctx.enter_context(nc.sbuf_tensor(f"{name}_{n}", shape, dt))

        self.g, self.units, self.t0 = g, 4 * blocks, 4 * first_block
        self.MC = MS // P
        self.sg, self.up = ([sb(f"{n}{i}", [P, MS]) for i in range(2)] for n in ("sg", "up"))
        self.h = [sb(f"h{i}", [P, 512]) for i in range(8)]
        self.ysb, self.x3, self.xs = ([sb(f"{n}{i}", [P, D]) for i in range(2)] for n in ("y", "x3", "xs"))
        self.g_mm, self.u_mm, self.sg_done, self.up_done, self.h_done, self.y_mm, self.y_out, self.xs_done = (
            sem(n) for n in ("g_mm", "u_mm", "sg_done", "up_done", "h_done", "y_mm", "y_out", "xs_done"))
        self.s_x3, self.xs_st = ([sem(f"{n}{i}") for i in range(2)] for n in ("s_x3", "xs_st"))
        self.ps_g, self.ps_u, self.ps_y = banks

    def behind(self, c):
        t = c.shift(-self.LAG)
        return t if t.within(self.units) else None

    def tensor(self, pe, c):
        g = self.g
        if c.within(self.units):
            block = c.div(4)
            for ps, w, s_mm, s_free in ((self.ps_g, g.sg_w, self.g_mm, self.sg_done),
                                        (self.ps_u, g.su_w, self.u_mm, self.up_done)):
                wait(pe, s_free, c.n)
                for d in range(DC):
                    m = c.mod(4)
                    last = pe.matmul(ps[:, :], w[:, d * MS + m * P:d * MS + (m + 1) * P],
                                     g.xn4T[:, bass.ds(block.n * 512 + (d * NTOK + self.t0 * P), 512)],
                                     start=(d == 0), stop=(d == DC - 1))
                last.then_inc(s_mm, 1)
        if (t := self.behind(c)) is not None:
            pe.wait_ge(self.h_done, t.div(4).n * 4 + 4)
            wait(pe, self.y_out, t.n)
            for m in range(self.MC):
                q = t.mod(4)
                last = pe.matmul(self.ps_y[:, 0:D], self.h[4 * t.div(4).mod(2) + m][:, q * P:(q + 1) * P],
                                 g.sd_w[:, m * D:(m + 1) * D], start=(m == 0), stop=(m == self.MC - 1))
            last.then_inc(self.y_mm, 1)

    def scalar(self, act, c):
        if c.within(self.units):
            p = c.mod(2)
            act.wait_ge(self.g_mm, c.n + 1)
            wait(act, self.h_done, c.shift(-1).n)
            act.activation(self.sg[p][:, :], self.ps_g[:, :], ACT.Silu).then_inc(self.sg_done, 1)
            act.wait_ge(self.u_mm, c.n + 1)
            act.activation(self.up[p][:, :], self.ps_u[:, :], ACT.Copy).then_inc(self.up_done, 1)
        if (t := self.behind(c)) is not None:
            p = t.mod(2)
            act.wait_ge(self.y_mm, t.n + 1)
            wait(act, self.xs_done, t.shift(-1).n)
            act.activation(self.ysb[p][:, :], self.ps_y[:, 0:D], ACT.Copy).then_inc(self.y_out, 1)

    def gpsimd(self, pool, c):
        if c.within(self.units):
            p = c.mod(2)
            wait(pool, self.y_mm, (c.div(4).n - 1) * 4)
            pool.wait_ge(self.sg_done, c.n + 1)
            pool.wait_ge(self.up_done, c.n + 1)
            pool.tensor_tensor(self.h[c.mod(8)][:, :], self.sg[p][:, :], self.up[p][:, :], ALU.mult)\
                .then_inc(self.h_done, 1)
        if (t := self.behind(c)) is not None:
            p = t.mod(2)
            pool.wait_ge(self.y_out, t.n + 1)
            pool.wait_ge(self.s_x3[p], (t.div(2).n + 1) * 16)
            wait(pool, self.xs_st[p], t.div(2).n * 16)
            pool.tensor_tensor(self.xs[p][:, :], self.x3[p][:, :], self.ysb[p][:, :], ALU.add).then_inc(self.xs_done, 1)

    def sync(self, sp, c):
        g = self.g
        if (t := self.behind(c)) is not None:
            p = t.mod(2)
            wait(sp, self.xs_done, t.shift(-1).n)
            sp.dma_start(self.x3[p][:, :], g.x3[bass.ds((t.n + self.t0) * P, P), :]).then_inc(self.s_x3[p], 16)
            sp.wait_ge(self.xs_done, t.n + 1)
            sp.dma_start(g.xs[bass.ds((t.n + self.t0) * P, P), :], self.xs[p][:, :]).then_inc(self.xs_st[p], 16)

    def landed(self, sp):
        for p in range(2):
            sp.wait_ge(self.xs_st[p], self.units // 2 * 16)


def route1_phase(nc, g):
    ctx = ExitStack()
    with ctx:
        sem = semaphores(nc, ctx, "r1_")
        r = Router(nc, ctx, sem, g, "r1", E1, K1, NS1, (g.pair[0], g.pair[1], g.bank[4]))
        s_w = sem("w")
        sh = SharedExpert(nc, ctx, sem, g, "sh", 0, NTOK // 512, g.bank[5:8])
        block = ctx.enter_context(nc.Block())
        top = g.top_v[:, :].rearrange("p (t k) -> p t k", k=8)[:, :, 0:K1]
        w = g.weight[:, 0:NT * K1].rearrange("p (t k) -> p t k", k=K1)
        U, TAB, BODY = sh.units, 16, 8
        PER = NT * K1 // (U - TAB)

        @block.sync
        def _(sp):
            for dst, src in ((g.sg_w, g.ins["sg"]), (g.su_w, g.ins["su"]), (g.sd_w, g.ins["sd"])):
                sp.dma_start(dst[:, :], src).then_inc(s_w, 16)
            steps(sp, TAB, U, U + sh.LAG, BODY, lambda c: sh.sync(sp, c))
            sh.landed(sp)

        @block.gpsimd
        def _(pool):
            steps(pool, TAB, U, U + sh.LAG, BODY, lambda c: sh.gpsimd(pool, c))

        @block.scalar
        def _(act):
            steps(act, TAB, U, U + sh.LAG, BODY, lambda c: sh.scalar(act, c))

        @block.vector
        def _(dve):
            def weights(dve, link):
                link(dve.tensor_reduce(r.wsum[:, :], top, AX.X, ALU.add))
                link(dve.tensor_scalar(r.wsum[:, :], r.wsum[:, :], 1e-12, None, ALU.max))
                link(dve.reciprocal(r.wrec[:, :], r.wsum[:, :]))
                link(dve.tensor_tensor(w, top, r.wrec[:, :].unsqueeze(2).broadcast_to([P, NT, K1]), ALU.mult))

            r.vector(dve, weights)

        @block.tensor
        def _(pe):
            pe.wait_ge(s_w, 48)
            r.tensor_counts(pe)
            r.tensor_table_open(pe)

            def unit(c):
                sh.tensor(pe, c)
                if c.within(U) and (c.loop is not None or c.off >= TAB):
                    for i in range(PER):
                        r.tensor_table(pe, At(c.loop, c.mul * PER, (c.off - TAB) * PER + i))

            steps(pe, TAB, U, U + sh.LAG, BODY, unit)
            r.tensor_table_close(pe)


def moe1_phase(nc, g):
    ctx = ExitStack()
    with ctx:
        def sb(name, shape, dt=F32):
            return ctx.enter_context(nc.sbuf_tensor("m1_" + name, shape, dt))

        sem = semaphores(nc, ctx, "m1_")

        NJ = NS1 // 2
        idx = [[sb(f"idx{i}{k}", [P, 1], I32) for k in range(2)] for i in range(2)]
        xg = [sb(f"xg{i}", [P, 2 * D]) for i in range(2)]
        xT = [sb(f"xT{i}", [P, 2 * D]) for i in range(2)]
        sg = [sb(f"sg{i}", [P, 2 * M1]) for i in range(2)]
        h = [sb(f"h{i}", [P, 2 * M1]) for i in range(2)]
        hT = [sb(f"hT{i}", [P, 2 * P]) for i in range(2)]
        y = [sb(f"y{i}", [P, 2 * D]) for i in range(2)]
        passed, s_dn = sem("passed_pool"), sem("s_dn")
        s_g, y_st = ([sem(f"{n}{i}") for i in range(2)] for n in ("s_g", "y_st"))
        idx_ready, x_t, x_out, gu_mm, silu_done, h_done, h_t, h_out, y_mm, y_out = (
            sem(n) for n in ("idx_ready", "x_t", "x_out", "gu_mm", "silu_done", "h_done", "h_t", "h_out", "y_mm",
                             "y_out"))
        ps_x, ps_gu, ps_ht, ps_y = g.bank[0:2], g.bank[2:4], g.bank[4:6], g.bank[6:8]
        block = ctx.enter_context(nc.Block())

        @block.gpsimd
        def _(pool):
            def gather(j):
                p = j.mod(2)
                wait_alone(pool, x_t, j.shift(-1).n, passed)
                for k in range(2):
                    pool.tensor_copy(idx[p][k][:, :], g.token[:, bass.ds(j.n * 2 + k, 1)]).then_inc(idx_ready, 1)
                wait_alone(pool, idx_ready, j.n * 2 + 2, passed)
                for k in range(2):
                    pool.indirect_dma_start(out=xg[p][:, k * D:(k + 1) * D], out_offset=None, in_=g.xn4,
                                            in_offset=bass.IndirectOffsetOnAxis(ap=idx[p][k][:, :], axis=0))\
                        .then_inc(s_g[p], 16)

            steps(pool, 2, NJ, NJ, 2, gather)

        @block.sync
        def _(sp):
            sp.dma_start(g.dn[:, :], g.ins["dn"]).then_inc(s_dn, 16)

            def store(j):
                p = j.mod(2)
                sp.wait_ge(y_out, j.n + 1)
                sp.dma_start(g.y1[bass.ds(j.n * 2 * P, 2 * P), :].rearrange("(a p) n -> p a n", p=P),
                             y[p][:, :].rearrange("p (a n) -> p a n", a=2)).then_inc(y_st[p], 16)

            steps(sp, 2, NJ, NJ, 2, store)
            for p in range(2):
                sp.wait_ge(y_st[p], NJ // 2 * 16)

        def halves(ap):
            return ap.rearrange("p (a x n) -> p a x n", a=2, x=2)

        @block.scalar
        def _(act):
            def step(s):
                j = s.shift(-2)
                if j.within(NJ):
                    p = j.mod(2)
                    act.wait_ge(h_t, j.n + 1)
                    wait(act, y_mm, j.shift(-1).n)
                    act.activation(hT[p][:, :], ps_ht[p][:, 0:2 * P], ACT.Copy).then_inc(h_out, 1)
                j = s
                if j.within(NJ):
                    p = j.mod(2)
                    act.wait_ge(x_t, j.n + 1)
                    wait(act, gu_mm, j.shift(-1).n)
                    act.activation(xT[p][:, :], ps_x[p][:, :], ACT.Copy).then_inc(x_out, 1)
                j = s.shift(-1)
                if j.within(NJ):
                    p = j.mod(2)
                    act.wait_ge(gu_mm, j.n + 1)
                    wait(act, h_done, j.shift(-1).n)
                    act.activation(sg[p][:, :].rearrange("p (a n) -> p a n", a=2), halves(ps_gu[p])[:, :, 0, :],
                                   ACT.Silu).then_inc(silu_done, 1)

            steps(act, 4, NJ, NJ + 2, 2, step)

        @block.vector
        def _(dve):
            def step(s):
                j = s.shift(-3)
                if j.within(NJ):
                    p = j.mod(2)
                    dve.wait_ge(y_mm, j.n + 1)
                    wait(dve, y_st[p], j.div(2).n * 16)
                    dve.tensor_copy(y[p][:, :], ps_y[p][:, :]).then_inc(y_out, 1)
                j = s.shift(-1)
                if j.within(NJ):
                    p = j.mod(2)
                    dve.wait_ge(silu_done, j.n + 1)
                    wait(dve, h_t, j.shift(-1).n)
                    dve.tensor_tensor(h[p][:, :].rearrange("p (a n) -> p a n", a=2), halves(ps_gu[p])[:, :, 1, :],
                                      sg[p][:, :].rearrange("p (a n) -> p a n", a=2), ALU.mult).then_inc(h_done, 1)

            steps(dve, 6, NJ, NJ + 3, 2, step)

        @block.tensor
        def _(pe):
            def expert(j, k):
                return pe.value_load(g.expert[0:1, bass.ds(j.n * 2 + k, 1)], min_val=0, max_val=E1 - 1)

            def step(s):
                j = s
                if j.within(NJ):
                    p = j.mod(2)
                    pe.wait_ge(s_g[p], (j.div(2).n + 1) * 32)
                    wait(pe, x_out, j.shift(-1).n)
                    for c in range(2 * DC):
                        last = pe.transpose(ps_x[p][:, c * P:(c + 1) * P], xg[p][:, c * P:(c + 1) * P], g.ident[:, :])
                    last.then_inc(x_t, 1)
                j = s.shift(-1)
                if j.within(NJ):
                    p = j.mod(2)
                    e = [expert(j, k) for k in range(2)]
                    pe.wait_ge(x_out, j.n + 1)
                    wait(pe, h_done, j.shift(-1).n)
                    for k in range(2):
                        for c in range(DC):
                            at = (k * DC + c) * P
                            last = pe.matmul(ps_gu[p][:, k * 2 * M1:(k + 1) * 2 * M1], xT[p][:, at:at + P],
                                             g.gu[:, bass.ds(e[k] * (DC * 2 * M1) + c * 2 * M1, 2 * M1)],
                                             start=(c == 0), stop=(c == DC - 1))
                    last.then_inc(gu_mm, 1)
                j = s.shift(-2)
                if j.within(NJ):
                    p = j.mod(2)
                    pe.wait_ge(h_done, j.n + 1)
                    wait(pe, h_out, j.shift(-1).n)
                    for k in range(2):
                        last = pe.transpose(ps_ht[p][:, k * P:(k + 1) * P], h[p][:, k * M1:(k + 1) * M1], g.ident[:, :])
                    last.then_inc(h_t, 1)
                j = s.shift(-3)
                if j.within(NJ):
                    p = j.mod(2)
                    e = [expert(j, k) for k in range(2)]
                    if j.loop is None and j.off == 0:
                        pe.wait_ge(s_dn, 16)
                    pe.wait_ge(h_out, j.n + 1)
                    wait(pe, y_out, j.shift(-1).n)
                    for k in range(2):
                        last = pe.matmul(ps_y[p][:, k * D:(k + 1) * D], hT[p][:, k * P:(k + 1) * P],
                                         g.dn[:, bass.ds(e[k] * D, D)], start=True, stop=True)
                    last.then_inc(y_mm, 1)

            steps(pe, 6, NJ, NJ + 3, 2, step)


def sum_phase(nc, g):
    ctx = ExitStack()
    with ctx:
        def sb(name, shape, dt=F32):
            return ctx.enter_context(nc.sbuf_tensor("su_" + name, shape, dt))

        sem = semaphores(nc, ctx, "su_")

        idx = [[sb(f"idx{i}{k}", [P, 1], I32) for k in range(K1)] for i in range(2)]
        yg = [[sb(f"yg{i}{k}", [P, D]) for k in range(K1)] for i in range(2)]
        xs = [sb(f"xs{i}", [P, D]) for i in range(2)]
        acc = [[sb(f"acc{i}{k}", [P, D]) for k in range(K1)] for i in range(2)]
        passed = sem("passed_pool")
        s_g, s_xs, st = ([sem(f"{n}{i}") for i in range(2)] for n in ("s_g", "s_xs", "st"))
        idx_ready, part, done = sem("idx_ready"), sem("part"), sem("done")
        block = ctx.enter_context(nc.Block())

        @block.gpsimd
        def _(pool):
            def gather(t):
                p = t.mod(2)
                wait_alone(pool, done, t.shift(-1).n, passed)
                for k in range(K1):
                    pool.tensor_copy(idx[p][k][:, :], g.slot[:, bass.ds(t.n * K1 + k, 1)]).then_inc(idx_ready, 1)
                wait_alone(pool, idx_ready, t.n * K1 + K1, passed)
                for k in range(K1):
                    pool.indirect_dma_start(out=yg[p][k][:, :], out_offset=None, in_=g.y1,
                                            in_offset=bass.IndirectOffsetOnAxis(ap=idx[p][k][:, :], axis=0))\
                        .then_inc(s_g[p], 16)

            steps(pool, 2, NT, NT, 2, gather)

        @block.sync
        def _(sp):
            def tile(s):
                t = s
                if t.within(NT):
                    wait(sp, done, t.shift(-1).n)
                    sp.dma_start(xs[t.mod(2)][:, :], g.xs[bass.ds(t.n * P, P), :]).then_inc(s_xs[t.mod(2)], 16)
                t = s.shift(-1)
                if t.within(NT):
                    sp.wait_ge(done, t.n + 1)
                    sp.dma_start(g.out[bass.ds(t.n * P, P), :], acc[t.mod(2)][K1 - 1][:, :]).then_inc(st[t.mod(2)], 16)

            steps(sp, 2, NT, NT + 1, 2, tile)
            for p in range(2):
                sp.wait_ge(st[p], NT // 2 * 16)

        @block.vector
        def _(dve):
            def tile(t):
                p = t.mod(2)
                dve.wait_ge(s_xs[p], (t.div(2).n + 1) * 16)
                dve.wait_ge(s_g[p], (t.div(2).n + 1) * 16 * K1)
                wait(dve, st[p], t.div(2).n * 16)
                for k in range(K1):
                    before = xs[p] if k == 0 else acc[p][k - 1]
                    if k:
                        dve.wait_ge(part, t.n * (K1 - 1) + k)
                    dve.scalar_tensor_tensor(acc[p][k][:, :], yg[p][k][:, :], g.weight[:, bass.ds(t.n * K1 + k, 1)],
                                             before[:, :], ALU.mult, ALU.add).then_inc(part if k < K1 - 1 else done, 1)

            steps(dve, 2, NT, NT, 2, tile)


class Core:

    def __init__(self, ins, scratch, out):
        self.ins, self.out = ins, out
        self.x1, self.x2, self.x3, self.xs = (scratch[n] for n in ("x1", "x2", "x3", "xs"))
        self.xn, self.xn4, self.y0, self.y1 = (scratch[n] for n in ("xn", "xn4", "y0", "y1"))


def program(nc, dram_in, out, scratch):
    g = Core(dram_in, scratch, out)
    ctx = ExitStack()
    with ctx:
        def sb(name, shape, dt=F32):
            return ctx.enter_context(nc.sbuf_tensor(name, shape, dt))

        g.ident = sb("ident", [P, P])
        g.ones = sb("ones", [P, P])
        g.minus_half = sb("minus_half", [P, H])
        g.top_v = sb("top_v", [P, NT * 8])
        g.top_i = sb("top_i", [P, NT * 8], U32)
        g.tri = sb("tri", [P, P])
        g.iota = sb("iota", [P, NS1])
        g.iota16 = sb("iota16", [P, NS1], F16)
        g.not_first = sb("not_first", [P, E1 * NT])
        g.tokval = sb("tokval", [P, NT])
        g.slot = sb("slot", [P, NT * K1], I32)
        g.token = sb("token", [P, NS1], I32)
        g.expert = sb("expert", [1, NS1], I32)
        g.weight = sb("weight", [P, NT * K1])
        g.psum = ctx.enter_context(nc.psum_tensor("psum", [P, 8, 512], F32))
        g.bank = [g.psum[:, i, :] for i in range(8)]
        g.pair = [g.psum[:, 2 * i:2 * i + 2, :] for i in range(4)]
        with ExitStack() as l0:
            g.w13 = l0.enter_context(nc.sbuf_tensor("w13", [P, E0 * DC * 2 * M0], F32))
            with ExitStack() as attn:
                g.kT_all = attn.enter_context(nc.sbuf_tensor("kT_all", [P, NB * NG * LK], F32))
                g.v_all = attn.enter_context(nc.sbuf_tensor("v_all", [P, NB * H * (DH + 1)], F32))
                g.qT_all = attn.enter_context(nc.sbuf_tensor("qT_all", [P, NT * D], F32))
                qkv_phase(nc, g)
                attention0_phase(nc, g)
            g.w2 = l0.enter_context(nc.sbuf_tensor("w2", [P, E0 * M0 // P * D], F32))
            route0_phase(nc, g)
            moe0_phase(nc, g)
        with ExitStack() as l1:
            def sb1(name, n):
                return l1.enter_context(nc.sbuf_tensor(name, [P, n], F32))

            g.gu, g.xn4T = sb1("gu", E1 * DC * 2 * M1), sb1("xn4T", DC * NTOK)
            g.sg_w, g.su_w, g.sd_w = sb1("sg_w", DC * MS), sb1("su_w", DC * MS), sb1("sd_w", MS // P * D)
            attention1_phase(nc, g)
            route1_phase(nc, g)
            g.dn = sb1("dn", E1 * D)
            moe1_phase(nc, g)
            sum_phase(nc, g)


def kernel(**inputs):
    import concourse.bacc as bacc
    from concourse.bass_utils import run_bass_kernel_spmd

    a = {k: np.asarray(v) for k, v in inputs.items()}

    def cols(w):
        return w.T.reshape(-1, P, w.shape[0]).transpose(1, 0, 2).reshape(P, -1)

    def row(b, n=P):
        return np.broadcast_to(b, (n, b.shape[0]))

    def with_row(w, b):
        r = np.zeros((P, b.shape[0]), b.dtype)
        r[0] = b
        return np.concatenate([cols(w), r], axis=1)

    f = np.float32
    eye = np.eye(P, dtype=f)
    arrays = {
        "x": a["x"].reshape(NTOK, D),
        "ctx": a["ctx_1024"].reshape(NB, LK, DC, P).transpose(0, 3, 2, 1).reshape(NB * P, DC * LK),
        "wq": with_row(a["L0_xattn_Wq"], a["L0_xattn_bq"]),
        "wk": with_row(a["L0_xattn_Wk"], a["L0_xattn_bk"]),
        "wv": with_row(a["L0_xattn_Wv"], a["L0_xattn_bv"]),
        "wp": cols(a["L0_xattn_Wp"]),
        "bp": row(a["L0_xattn_bp"]),
        "gb": np.stack([np.tile(a["L0_xattn_" + n], HG) for n in ("q_gamma", "q_beta", "k_gamma", "k_beta")], 1),
        "wr0": cols(a["L0_ffn_moe_router"].T),
        "ident": eye,
        "tri": np.triu(np.ones((P, P), f), 1),
        "iota": np.broadcast_to(np.arange(NS1, dtype=f), (P, NS1)),
        "iota16": np.broadcast_to(np.arange(NS1, dtype=np.float16), (P, NS1)),
        "not_first": np.broadcast_to((np.arange(E1 * NT) % NT > 0).astype(f), (P, E1 * NT)),
        "tokval": np.arange(NT, dtype=f)[None, :] * P + np.arange(P, dtype=f)[:, None] - MID,
        "w13": a["L0_ffn_moe_w13"].reshape(E0, DC, P, 2 * M0).transpose(2, 0, 1, 3).reshape(P, -1),
        "wq1": cols(a["L1_xattn_Wq"]),
        "wk1": cols(a["L1_xattn_Wk"]),
        "wv1": cols(a["L1_xattn_Wv"]),
        "wo1": cols(a["L1_xattn_Wo"]),
        "wr1": cols(a["L1_ffn_router_w"]),
        "bq1": a["L1_xattn_bq"].reshape(DC, P).T,
        "bk1": a["L1_xattn_bk"].reshape(DC, P).T,
        "bv1": row(a["L1_xattn_bv"]),
        "bo1": row(a["L1_xattn_bo"]),
        "rb1": row(a["L1_ffn_router_bias"]),
        "gu": np.stack([a["L1_ffn_gate_w"], a["L1_ffn_up_w"]]).reshape(2, E1, M1, DC, P)
        .transpose(4, 1, 3, 0, 2).reshape(P, -1),
        "dn": a["L1_ffn_down_w"].transpose(2, 0, 1).reshape(P, -1),
        "sg": cols(a["L1_ffn_sgate_w"]),
        "su": cols(a["L1_ffn_sup_w"]),
        "sd": cols(a["L1_ffn_sdown_w"]),
        "w2": a["L0_ffn_moe_w2"].reshape(E0, M0 // P, P, D).transpose(2, 0, 1, 3).reshape(P, -1),
        "hmask": np.repeat(np.eye(HG, dtype=f), DH, axis=0),
    }
    arrays = {k: np.ascontiguousarray(v) for k, v in arrays.items()}
    nc = bacc.Bacc("TRN2", target_bir_lowering=False, num_devices=1)
    dram_in = {n: nc.dram_tensor("in_" + n, v.shape, mybir.dt.from_np(v.dtype), kind="ExternalInput").ap()
               for n, v in arrays.items()}
    out = nc.dram_tensor("out", (NTOK, D), F32, kind="ExternalOutput").ap()
    scratch = {n: nc.dram_tensor("t_" + n, s, F32, kind="Internal").ap() for n, s in (
        ("x1", (NTOK, D)), ("xn", (NTOK, D)), ("y0", (NS0 * P, D)), ("y1", (NS1 * P, D)), ("x2", (NTOK, D)), ("x3", (NTOK, D)), ("xn4", (NTOK, D)), ("xs", (NTOK, D)))}
    program(nc, dram_in, out, scratch)
    res = run_bass_kernel_spmd(nc, [{"in_" + n: v for n, v in arrays.items()}], core_ids=[0])
    return res.results[0]["out"].reshape(NB, SQ, D)
```

```python
import numpy as np
from contextlib import ExitStack

import concourse.bass as bass
from concourse import mybir

F32 = mybir.dt.float32
F16 = mybir.dt.float16
BF16 = mybir.dt.bfloat16
I32 = mybir.dt.int32
U32 = mybir.dt.uint32
ALU = mybir.AluOpType
ACT = mybir.ActivationFunctionType
AX = mybir.AxisListType

P = 128
D = 256
DC = D // P
NB, SQ, LK = 16, 256, 77
NTOK = NB * SQ
NT = NTOK // P
H, DH = 16, 16
HG = 8
NG = H // HG
EPS = 1e-5
E0, K0, M0 = 8, 2, 512
E1, K1, M1 = 32, 4, 128
MS = 512
NS0 = NTOK * K0 // P + E0
NS1 = NTOK * K1 // P + E1
MID = NTOK // 2
SHARED_FIRST = 3
GB = 4


class At:

    def __init__(self, loop, mul, off):
        self.loop, self.mul, self.off = loop, mul, off

    @property
    def n(self):
        return self.off if self.loop is None else self.loop * self.mul + self.off

    def shift(self, d):
        return At(self.loop, self.mul, self.off + d)

    def times(self, k):
        return At(self.loop, self.mul * k, self.off * k)

    def div(self, k):
        return At(self.loop, self.mul // k, self.off // k)

    def mod(self, k):
        return self.off % k

    def within(self, count):
        return self.loop is not None or 0 <= self.off < count


def steps(eng, first, last, total, body, step):
    for s in range(first):
        step(At(None, 0, s))
    with eng.Fori(0, (last - first) // body) as i:
        for u in range(body):
            step(At(i, body, first + u))
    for s in range(last, total):
        step(At(None, 0, s))


def few(total, step):
    for s in range(total):
        step(At(None, 0, s))


def wait(eng, sem, count):
    if isinstance(count, int) and count <= 0:
        return
    eng.wait_ge(sem, count)


def semaphores(nc, ctx, prefix):
    taken = []

    def clear():
        nc.clear_and_free_semaphores(taken)
        nc.all_engine_barrier()

    def sem(name):
        taken.append(nc.alloc_semaphore(prefix + name))
        return taken[-1]

    ctx.callback(clear)
    return sem


def wait_alone(eng, sem, count, s_passed):
    if isinstance(count, int) and count <= 0:
        return
    eng.wait_ge(sem, count)
    eng.sem_inc(s_passed, 1)


def inverse_root(pool, out, var, minus_half, s_eps, s_rstd, t):
    pool.tensor_scalar(out, var, EPS, None, ALU.add).then_inc(s_eps, 1)
    pool.wait_ge(s_eps, t.n + 1)
    pool.tensor_tensor(out, out, minus_half, ALU.pow).then_inc(s_rstd, 1)


class LayerNorm:

    def __init__(self, sb, sem, name, s_passed, minus_half):
        self.minus_half, self.s_eps = minus_half, sem(f"{name}_eps")
        self.stats = [sb(f"{name}_stats{i}", [P, 6]) for i in range(2)]
        self.mv = [sb(f"{name}_mv{i}", [P, 2]) for i in range(2)]
        self.rstd = [sb(f"{name}_rstd{i}", [P, 1]) for i in range(2)]
        self.s_stats, self.s_mv, self.s_rstd = (sem(f"{name}_{n}") for n in ("stats", "mv", "rstd"))
        self.s_passed = s_passed

    def moments(self, dve, x, t):
        p = t.mod(2)
        dve.bn_stats(self.stats[p][:, :], x).then_inc(self.s_stats, 1)
        wait_alone(dve, self.s_stats, t.n + 1, self.s_passed[0])
        dve.bn_aggr(self.mv[p][:, :], self.stats[p][:, :]).then_inc(self.s_mv, 1)

    def invert(self, pool, t):
        p = t.mod(2)
        wait_alone(pool, self.s_mv, t.n + 1, self.s_passed[1])
        inverse_root(pool, self.rstd[p][:, :], self.mv[p][:, 1:2], self.minus_half[:, 0:1], self.s_eps, self.s_rstd, t)

    def apply(self, dve, x, out, t):
        p = t.mod(2)
        dve.wait_ge(self.s_rstd, t.n + 1)
        return dve.tensor_scalar(out, x, self.mv[p][:, 0:1], self.rstd[p][:, :], ALU.subtract, ALU.mult)


def heads_of(ap):
    return ap.rearrange("p (h d) -> p h d", d=DH)


class HeadNorm:

    def __init__(self, sb, sem, g, name, rows, w, bias, gamma, beta, eps, ps_p, ps_t):
        self.g, self.rows, self.w, self.bias, self.gamma, self.beta = g, rows, w, bias, gamma, beta
        self.eps, self.ps_p, self.ps_t = eps, ps_p, ps_t
        self.sq, self.n = ([sb(f"{name}_{n}{i}", [P, 2 * D]) for i in range(2)] for n in ("sq", "n"))
        self.var, self.sd, self.rstd = (
            [sb(f"{name}_{n}{i}", [P, 2 * H]) for i in range(2)] for n in ("var", "sd", "rstd"))
        self.s_proj, self.s_sq, self.s_var, self.s_sd, self.s_rstd, self.s_n, self.s_t, self.s_out = (
            sem(f"{name}_{n}") for n in ("proj", "sq", "var", "sd", "rstd", "n", "t", "out"))

    def project(self, pe, i, block):
        ps, r = self.ps_p[i.mod(4)], self.rows
        wait(pe, self.s_n, i.shift(-3).n)
        for a in range(2):
            pe.matmul(ps[0:r, a * D:(a + 1) * D], self.g.ones[0:1, 0:r], self.bias, start=True, stop=False)
            for c in range(DC):
                last = pe.matmul(ps[0:r, a * D:(a + 1) * D], block(a, c), self.w[:, c * D:(c + 1) * D],
                                 start=False, stop=(c == DC - 1))
        last.then_inc(self.s_proj, 1)

    def square(self, act, i):
        p, r = i.mod(2), self.rows
        act.wait_ge(self.s_proj, i.n + 1)
        wait(act, self.s_var, i.shift(-1).n)
        act.activation(self.sq[p][0:r, :], self.ps_p[i.mod(4)][0:r, :], ACT.Square, scale=DH ** -0.5).then_inc(self.s_sq, 1)

    def variance(self, dve, i):
        p, r = i.mod(2), self.rows
        dve.wait_ge(self.s_sq, i.n + 1)
        wait(dve, self.s_sd, i.shift(-1).n)
        dve.tensor_reduce(self.var[p][0:r, :], heads_of(self.sq[p][0:r, :]), AX.X, ALU.add).then_inc(self.s_var, 1)

    def root(self, act, i):
        p, r = i.mod(2), self.rows
        act.wait_ge(self.s_var, i.n + 1)
        wait(act, self.s_rstd, i.shift(-1).n)
        act.activation(self.sd[p][0:r, :], self.var[p][0:r, :], ACT.Sqrt, bias=self.eps[0:r, 0:1])\
            .then_inc(self.s_sd, 1)

    def scale(self, dve, i):
        p, r = i.mod(2), self.rows
        dve.wait_ge(self.s_sd, i.n + 1)
        dve.reciprocal(self.rstd[p][0:r, :], self.sd[p][0:r, :]).then_inc(self.s_rstd, 1)
        dve.wait_ge(self.s_rstd, i.n + 1)
        wait(dve, self.s_t, i.shift(-1).n)
        dve.tensor_tensor(heads_of(self.n[p][0:r, :]), heads_of(self.ps_p[i.mod(4)][0:r, :]),
                          self.rstd[p][0:r, :].unsqueeze(2).broadcast_to([r, 2 * H, DH]), ALU.mult)\
            .then_inc(self.s_n, 1)

    def transpose(self, pe, i):
        p, r = i.mod(2), self.rows
        pe.wait_ge(self.s_n, i.n + 1)
        wait(pe, self.s_out, i.n)
        for c in range(2 * DC):
            last = pe.transpose(self.ps_t[:, c * r:(c + 1) * r], self.n[p][0:r, c * P:(c + 1) * P],
                                self.g.ident[0:r, 0:r])
        last.then_inc(self.s_t, 1)

    def affine(self, act, i, out, s_passed):
        n = 2 * DC * self.rows
        wait_alone(act, self.s_t, i.n + 1, s_passed)
        act.activation(out[:, bass.ds(i.n * n, n)], self.ps_t[:, 0:n], ACT.Identity,
                       bias=self.beta, scale=self.gamma).then_inc(self.s_out, 1)


def qkv_phase(nc, g):
    ctx = ExitStack()
    with ctx:
        def sb(name, shape, dt=F32):
            return ctx.enter_context(nc.sbuf_tensor("qkv_" + name, shape, dt))

        sem = semaphores(nc, ctx, "qkv_")

        NKP, NQP, VW = NB // 2, NT // 2, H * (DH + 1)
        wq, wk, wv = (sb(n, [P, DC * D]) for n in ("wq", "wk", "wv"))
        bias = sb("bias", [1, 2 * D])
        wmean, bmean = sb("wmean", [P, 2, DC * H]), sb("bmean", [1, 2 * H])
        gb, scaled, eps, bv = sb("gb", [P, 4]), sb("scaled", [P, 2]), sb("eps", [P, 1]), sb("bv", [P, 2 * D])
        ctxT = sb("ctxT", [P, DC * NB * LK])
        x_in = [sb(f"x_in{i}", [P, 2 * D]) for i in range(4)]
        xn = [sb(f"xn{i}", [P, 2 * D]) for i in range(2)]
        xnT = [sb(f"xnT{i}", [P, 2 * D]) for i in range(2)]
        stats = [sb(f"stats{i}", [P, 12]) for i in range(2)]
        mv = [sb(f"mv{i}", [P, 4]) for i in range(2)]
        rstd = [sb(f"rstd{i}", [P, 2]) for i in range(2)]
        s_w, s_rest, s_ctx, s_wm, s_wc, s_gs, s_ones, s_v1, s_half = (sem(n) for n in (
            "s_w", "s_rest", "s_ctx", "s_wm", "s_wc", "s_gs", "s_ones", "s_v1", "s_half"))
        s_x = [sem(f"s_x{i}") for i in range(4)]
        v_mm, v_out, ln_stats, ln_mv, ln_eps, ln_rstd, x_norm, x_t, x_out = (sem(n) for n in (
            "v_mm", "v_out", "ln_stats", "ln_mv", "ln_eps", "ln_rstd", "x_norm", "x_t", "x_out"))
        passed = [sem(f"passed_{n}") for n in ("dve", "pool", "act")]
        ps_p, ps_t, ps_xt, ps_v = g.bank[0:4], g.bank[4], g.bank[5:7], g.bank[7]
        k = HeadNorm(sb, sem, g, "k", LK, wk, bias[0:1, 0:D], gb[:, 2:3], gb[:, 3:4], eps, ps_p, ps_t)
        q = HeadNorm(sb, sem, g, "q", P, wq, bias[0:1, D:2 * D], scaled[:, 0:1], scaled[:, 1:2], eps, ps_p, ps_t)
        block = ctx.enter_context(nc.Block())
        VAR, SCALE, OUT = 1, 2, 3
        XQ = NKP
        X, XT = XQ - 2, XQ - 1
        BODY, FIRST, TOTAL = 4, NKP + 4, XQ + NQP + OUT
        LAST = FIRST + (X + NQP - FIRST) // BODY * BODY

        def piece(s, skew):
            if s.loop is None and 0 <= s.off - skew < NKP:
                return k, s.shift(-skew)
            i = s.shift(-skew - XQ)
            return (q, i) if i.within(NQP) else None

        def pair(s, skew):
            i = s.shift(-skew)
            return i if i.within(NQP) else None

        @block.sync
        def _(sp):
            for dst, src in ((wk, g.ins["wk"]), (wq, g.ins["wq"]), (bias, g.ins["bkq"])):
                sp.dma_start(dst[:, :], src).then_inc(s_w, 16)
            for dst, src in ((gb, g.ins["gb"]), (wv, g.ins["wv"]), (bv, g.ins["bv"]), (g.ident, g.ins["ident"])):
                sp.dma_start(dst[:, :], src).then_inc(s_rest, 16)

            def load_x(s):
                wait(sp, x_norm, s.shift(-3).n)
                sp.dma_start(x_in[s.mod(4)][:, :].rearrange("p (a n) -> p a n", a=2),
                             g.ins["x"][bass.ds(s.n * 2 * P, 2 * P), :].rearrange("(a p) n -> p a n", p=P))\
                    .then_inc(s_x[s.mod(4)], 16)

            steps(sp, 4, NQP, NQP, 4, load_x)

        @block.gpsimd
        def _(pool):
            pool.memset(g.ones[:, :], 1.0).then_inc(s_ones, 1)
            pool.memset(eps[:, :], EPS).then_inc(s_half, 1)
            pool.memset(g.minus_half[:, :], -0.5).then_inc(s_half, 1)
            pool.wait_ge(s_half, 2)
            pool.memset(g.v_all[:, :], 1.0).then_inc(s_v1, 1)

            def invert(s):
                p = s.mod(2)
                wait_alone(pool, ln_mv, s.n + 1, passed[1])
                inverse_root(pool, rstd[p][:, :], mv[p][:, :].rearrange("p (a n) -> p a n", a=2)[:, :, 1],
                             g.minus_half[:, 0:2], ln_eps, ln_rstd, s)

            steps(pool, 2, NQP, NQP, 2, invert)

        @block.vector
        def _(dve):
            dve.wait_ge(s_w, 3 * 16)
            for j, (w, m) in enumerate(((wk[:, :], wmean[:, 0, :]), (bias[:, :], bmean[:, :]),
                                        (wq[:, :], wmean[:, 1, :]))):
                rows, heads = m.shape
                dve.tensor_reduce(m, heads_of(w), AX.X, ALU.add).then_inc(s_wm, 1)
                dve.wait_ge(s_wm, 2 * j + 1)
                dve.tensor_scalar(m, m, 1.0 / DH, None, ALU.mult).then_inc(s_wm, 1)
                dve.wait_ge(s_wm, 2 * j + 2)
                dve.tensor_tensor(heads_of(w), heads_of(w), m.unsqueeze(2).broadcast_to([rows, heads, DH]),
                                  ALU.subtract).then_inc(s_wc, 1)
            dve.wait_ge(s_rest, 4 * 16)
            dve.tensor_scalar(scaled[:, :], gb[:, 0:2], float(DH) ** -0.5, None, ALU.mult).then_inc(s_gs, 1)
            dve.wait_ge(s_v1, 1)

            def step(s):
                if (i := pair(s, XT)) is not None:
                    p = i.mod(2)
                    dve.wait_ge(ln_rstd, i.n + 1)
                    wait(dve, x_t, i.shift(-1).n)
                    for a in range(2):
                        last = dve.tensor_scalar(xn[p][:, a * D:(a + 1) * D], x_in[i.mod(4)][:, a * D:(a + 1) * D],
                                                 mv[p][:, 2 * a:2 * a + 1], rstd[p][:, a:a + 1],
                                                 ALU.subtract, ALU.mult)
                    last.then_inc(x_norm, 1)
                if (i := pair(s, X)) is not None:
                    p = i.mod(2)
                    dve.wait_ge(s_x[i.mod(4)], (i.div(4).n + 1) * 16)
                    for a in range(2):
                        last = dve.bn_stats(stats[p][:, 6 * a:6 * a + 6], x_in[i.mod(4)][:, a * D:(a + 1) * D])
                    last.then_inc(ln_stats, 1)
                    wait_alone(dve, ln_stats, i.n + 1, passed[0])
                    for a in range(2):
                        last = dve.bn_aggr(mv[p][:, 2 * a:2 * a + 2], stats[p][:, 6 * a:6 * a + 6])
                    last.then_inc(ln_mv, 1)
                if (at := piece(s, SCALE)) is not None:
                    at[0].scale(dve, at[1])
                if (at := piece(s, VAR)) is not None:
                    at[0].variance(dve, at[1])
                if s.loop is None and s.off < NKP:
                    i = s
                    dve.wait_ge(v_mm, i.n + 1)
                    dve.tensor_tensor(
                        g.v_all[0:LK, bass.ds(i.n * 2 * VW, 2 * VW)].rearrange("p (h d) -> p h d", d=DH + 1)[:, :, 0:DH],
                        heads_of(ps_v[0:LK, :]), heads_of(bv[0:LK, :]), ALU.add).then_inc(v_out, 1)

            steps(dve, FIRST, LAST, TOTAL, BODY, step)

        @block.scalar
        def _(act):
            act.dma_start(ctxT[:, :], g.ins["ctx"]).then_inc(s_ctx, 16)
            act.wait_ge(s_gs, 1)
            act.wait_ge(s_half, 2)

            def step(s):
                if (i := pair(s, XT)) is not None:
                    act.wait_ge(x_t, i.n + 1)
                    wait(act, q.s_proj, i.shift(-1).n)
                    act.activation(xnT[i.mod(2)][:, :], ps_xt[i.mod(2)][:, :], ACT.Copy).then_inc(x_out, 1)
                if (at := piece(s, VAR)) is not None:
                    at[0].root(act, at[1])
                if (at := piece(s, OUT)) is not None:
                    at[0].affine(act, at[1], g.kT_all if at[0] is k else g.qT_all, passed[2])
                if (at := piece(s, 0)) is not None:
                    at[0].square(act, at[1])

            steps(act, FIRST, LAST, TOTAL, BODY, step)

        @block.tensor
        def _(pe):
            pe.wait_ge(s_w, 3 * 16)
            pe.wait_ge(s_ctx, 16)
            pe.wait_ge(s_ones, 1)
            pe.wait_ge(s_wc, 3)
            pe.wait_ge(s_rest, 4 * 16)

            def step(s):
                if (i := pair(s, XT)) is not None:
                    p = i.mod(2)
                    pe.wait_ge(x_norm, i.n + 1)
                    wait(pe, x_out, i.shift(-1).n)
                    for c in range(2 * DC):
                        last = pe.transpose(ps_xt[p][:, c * P:(c + 1) * P], xn[p][:, c * P:(c + 1) * P], g.ident[:, :])
                    last.then_inc(x_t, 1)
                if (at := piece(s, 0)) is not None:
                    norm, i = at
                    if norm is k:
                        norm.project(pe, i, lambda a, c: ctxT[:, (c * NB + 2 * i.n + a) * LK:][:, 0:LK])
                        wait(pe, v_out, i.n)
                        for a in range(2):
                            for c in range(DC):
                                last = pe.matmul(ps_v[0:LK, a * D:(a + 1) * D],
                                                 ctxT[:, (c * NB + 2 * i.n + a) * LK:][:, 0:LK],
                                                 wv[:, c * D:(c + 1) * D], start=(c == 0), stop=(c == DC - 1))
                        last.then_inc(v_mm, 1)
                    else:
                        pe.wait_ge(x_out, i.n + 1)
                        if i.loop is None and i.off < 4:
                            pe.wait_ge(k.s_n, NKP - 3 + i.off)
                        norm.project(pe, i, lambda a, c: xnT[i.mod(2)][:, (a * DC + c) * P:(a * DC + c + 1) * P])
                if (at := piece(s, OUT)) is not None:
                    norm, i = at
                    if norm is q and i.loop is None and i.off == 0:
                        pe.wait_ge(k.s_out, NKP)
                    norm.transpose(pe, i)

            steps(pe, FIRST, LAST, TOTAL, BODY, step)


def top_of(dve, g, scores, top, ix, t, s_scores, s_top, s_ix, passed):
    wait_alone(dve, s_scores, t.n + 1, passed[0])
    dve.max(top[:, :], scores[:, :]).then_inc(s_top, 1)
    wait_alone(dve, s_top, t.n + 1, passed[0])
    dve.max_index(ix[:, :], top[:, :], scores[:, :]).then_inc(s_ix, 1)
    dve.tensor_copy(g.top_v[:, bass.ds(t.n * 8, 8)], top[:, :])
    wait_alone(dve, s_ix, t.n + 1, passed[0])
    dve.tensor_copy(g.top_i[:, bass.ds(t.n * 8, 8)], ix[:, :])


def attention0_phase(nc, g):
    ctx = ExitStack()
    with ctx:
        def sb(name, shape, dt=F32):
            return ctx.enter_context(nc.sbuf_tensor("at0_" + name, shape, dt))

        sem = semaphores(nc, ctx, "at0_")

        NU = NT * NG
        VW = H * (DH + 1)
        HW = HG * LK // 2
        wp = sb("wp", [P, DC * D])
        wr = sb("wr", [P, DC * E0])
        bp = sb("bp", [P, D])
        hmask = sb("hmask", [P, HG])
        q_s = [sb(f"q_s{i}", [P, D]) for i in range(2)]
        kblk = [sb(f"kblk{i}", [P, NG * HG * LK]) for i in range(2)]
        x_in = [sb(f"x_in{i}", [P, D]) for i in range(2)]
        xb = [sb(f"xb{i}", [P, D]) for i in range(2)]
        mx = [sb(f"mx{i}", [P, HG]) for i in range(2)]
        pr = [sb(f"pr{i}", [P, HG * LK]) for i in range(2)]
        prT = [sb(f"prT{i}", [P, HG * P]) for i in range(2)]
        rec = [sb(f"rec{i}", [P, H]) for i in range(2)]
        o = [sb(f"o{i}", [P, D]) for i in range(2)]
        oT = [sb(f"oT{i}", [P, D]) for i in range(2)]
        x1 = [sb(f"x1{i}", [P, D]) for i in range(2)]
        xn = [sb(f"xn{i}", [P, D]) for i in range(2)]
        xnT = [sb(f"xnT{i}", [P, D]) for i in range(2)]
        lg = [sb(f"lg{i}", [P, E0]) for i in range(2)]
        top = [sb(f"top{i}", [P, 8]) for i in range(2)]
        ix = [sb(f"ix{i}", [P, 8], U32) for i in range(2)]
        s_w, s_next = sem("s_w"), sem("s_next")
        s_x, x1_st, xn_st = ([sem(f"{n}{i}") for i in range(2)] for n in ("s_x", "x1_st", "xn_st"))
        k_ready, q_ready, xb_ready, s_mm, mx_ready, sub_done, exp_done, tp_mm, tp_out, pv_mm, rec_ready, o_norm = (
            sem(n) for n in ("k_ready", "q_ready", "xb_ready", "s_mm", "mx_ready", "sub_done", "exp_done", "tp_mm",
                             "tp_out", "pv_mm", "rec_ready", "o_norm"))
        o_t, o_out, wp_mm, x1_done, x_norm, x_t, x_out, r_mm, lg_done, m8_done, ix_done = (
            sem(n) for n in ("o_t", "o_out", "wp_mm", "x1_done", "x_norm", "x_t", "x_out", "r_mm", "lg_done",
                             "m8_done", "ix_done"))
        passed = [sem(f"passed_{n}") for n in ("dve", "pool", "act")]
        ln = LayerNorm(sb, sem, "ln", passed, g.minus_half)
        ps_s, ps_tp = g.pair[0], g.pair[1]
        ps_o, ps_ot, ps_wp, ps_x = g.bank[4:8]
        block = ctx.enter_context(nc.Block())
        T_O, T_WP, T_X, T_R = 5, 6, 8, 9
        FIRST, BODY, TOTAL = 16, 8, NU + T_R + 1
        LEAD = 2

        def tile_at(u, skew):
            s = u.shift(-skew)
            return s.div(2) if s.mod(2) == 0 and s.within(NU) else None

        @block.sync
        def _(sp):
            for dst, src in ((wp, g.ins["wp"]), (wr, g.ins["wr0"]), (bp, g.ins["bp"]), (hmask, g.ins["hmask"])):
                sp.dma_start(dst[:, :], src).then_inc(s_w, 16)
            for dst, src in ((g.tri, g.ins["tri"]), (g.iota, g.ins["iota"]), (g.iota16, g.ins["iota16"]),
                             (g.not_first, g.ins["not_first"]), (g.tokval, g.ins["tokval"])):
                sp.dma_start(dst[:, :], src).then_inc(s_next, 16)
            n = DC * 2 * M0
            for e in range(E0):
                sp.dma_start(g.w13[:, e * n:(e + 1) * n], g.ins["w13"][:, e * n:(e + 1) * n]).then_inc(s_next, 16)

            def tile(s):
                t = s
                if t.within(NT):
                    wait(sp, xb_ready, t.shift(-1).n)
                    sp.dma_start(x_in[t.mod(2)][:, :], g.ins["x"][bass.ds(t.n * P, P), :]).then_inc(s_x[t.mod(2)], 16)
                t = s.shift(-4)
                if t.within(NT):
                    p = t.mod(2)
                    sp.wait_ge(x1_done, t.n + 1)
                    sp.dma_start(g.x1[bass.ds(t.n * P, P), :], x1[p][:, :]).then_inc(x1_st[p], 16)
                    sp.wait_ge(x_norm, t.n + 1)
                    sp.dma_start(g.xn[bass.ds(t.n * P, P), :], xn[p][:, :]).then_inc(xn_st[p], 16)

            steps(sp, 6, NT, NT + 4, 2, tile)
            for p in range(2):
                sp.wait_ge(x1_st[p], NT // 2 * 16)
                sp.wait_ge(xn_st[p], NT // 2 * 16)
            sp.wait_ge(s_next, (5 + E0) * 16)

        @block.gpsimd
        def _(pool):
            pool.wait_ge(s_w, 64)

            def half(u):
                t = tile_at(u, 0)
                if t is not None:
                    p, b = t.mod(2), t.div(2)
                    if t.mod(2) == 0:
                        bp_ = b.mod(2)
                        wait_alone(pool, s_mm, b.shift(-1).n * 4, passed[1])
                        for gr in range(NG):
                            kT = g.kT_all[:, bass.ds(b.n * (NG * LK) + gr * LK, LK)]
                            pool.tensor_tensor(
                                kblk[bp_][:, gr * HG * LK:(gr + 1) * HG * LK].rearrange("p (h k) -> p h k", h=HG),
                                kT.unsqueeze(1).broadcast_to([P, HG, LK]),
                                hmask[:, :].unsqueeze(2).broadcast_to([P, HG, LK]), ALU.mult).then_inc(k_ready, 1)
                    wait_alone(pool, s_mm, t.shift(-1).n * 2, passed[1])
                    pool.tensor_copy(q_s[p][:, :], g.qT_all[:, bass.ds(t.n * D, D)]).then_inc(q_ready, 1)
                t = tile_at(u, 4 + LEAD)
                if t is not None:
                    p = t.mod(2)
                    pool.wait_ge(s_x[p], (t.div(2).n + 1) * 16)
                    wait(pool, x1_done, t.shift(-1).n)
                    pool.tensor_tensor(xb[p][:, :], x_in[p][:, :], bp[:, :], ALU.add).then_inc(xb_ready, 1)
                t = tile_at(u, T_WP + LEAD)
                if t is not None:
                    ln.invert(pool, t)

            steps(pool, FIRST, NU, TOTAL + LEAD, BODY, half)

        @block.vector
        def _(dve):
            def half(u):
                if u.within(NU):
                    p = u.mod(2)
                    s3 = ps_s[:, :, 0:HW].rearrange("p a (h k) -> p a h k", k=LK)
                    dve.wait_ge(s_mm, u.n + 1)
                    dve.tensor_reduce(mx[p][:, :].rearrange("p (a h) -> p a h", a=2), s3, AX.X, ALU.max)\
                        .then_inc(mx_ready, 1)
                    dve.wait_ge(mx_ready, u.n + 1)
                    wait(dve, tp_mm, u.shift(-1).n)
                    dve.tensor_tensor(
                        pr[p][:, :].rearrange("p (a h k) -> p a h k", a=2, k=LK), s3,
                        mx[p][:, :].rearrange("p (a h) -> p a h", a=2).unsqueeze(3).broadcast_to([P, 2, HG // 2, LK]),
                        ALU.subtract).then_inc(sub_done, 1)
                t = tile_at(u, 3)
                if t is not None:
                    p = t.mod(2)
                    ov = ps_o[:, 0:VW].rearrange("p (h d) -> p h d", h=H)
                    dve.wait_ge(pv_mm, t.n * 2 + 2)
                    dve.reciprocal(rec[p][:, :].unsqueeze(2), ov[:, :, DH:DH + 1]).then_inc(rec_ready, 1)
                    dve.wait_ge(rec_ready, t.n + 1)
                    wait(dve, o_t, t.shift(-1).n)
                    dve.tensor_tensor(heads_of(o[p][:, :]), ov[:, :, 0:DH],
                                      rec[p][:, :].unsqueeze(2).broadcast_to([P, H, DH]), ALU.mult).then_inc(o_norm, 1)
                t = tile_at(u, T_WP + 1)
                if t is not None:
                    p = t.mod(2)
                    wait(dve, xn_st[p], t.div(2).n * 16)
                    wait(dve, x_t, t.shift(-1).n)
                    ln.apply(dve, x1[p][:, :], xn[p][:, :], t).then_inc(x_norm, 1)
                t = tile_at(u, T_WP)
                if t is not None:
                    p = t.mod(2)
                    dve.wait_ge(wp_mm, t.n + 1)
                    dve.wait_ge(xb_ready, t.n + 1)
                    wait(dve, x1_st[p], t.div(2).n * 16)
                    dve.tensor_tensor(x1[p][:, :], ps_wp[:, 0:D], xb[p][:, :], ALU.add).then_inc(x1_done, 1)
                    dve.wait_ge(x1_done, t.n + 1)
                    ln.moments(dve, x1[p][:, :], t)
                t = tile_at(u, T_R)
                if t is not None:
                    p = t.mod(2)
                    dve.wait_ge(r_mm, t.n + 1)
                    dve.tensor_copy(lg[p][:, :], ps_x[:, D:D + E0]).then_inc(lg_done, 1)
                    top_of(dve, g, lg[p], top[p], ix[p], t, lg_done, m8_done, ix_done, passed)

            steps(dve, FIRST, NU, TOTAL, BODY, half)

        @block.scalar
        def _(act):
            def half(u):
                v = u.shift(-1)
                if v.within(NU):
                    p = v.mod(2)
                    act.wait_ge(tp_mm, v.n + 1)
                    wait(act, pv_mm, v.shift(-1).n)
                    act.activation(prT[p][0:LK, :].rearrange("p (a k) -> p a k", a=2), ps_tp[0:LK, :, :], ACT.Copy)\
                        .then_inc(tp_out, 1)
                if u.within(NU):
                    p = u.mod(2)
                    act.wait_ge(sub_done, u.n + 1)
                    act.activation(pr[p][:, :], pr[p][:, :], ACT.Exp).then_inc(exp_done, 1)
                t = tile_at(u, T_O)
                if t is not None:
                    p = t.mod(2)
                    act.wait_ge(o_t, t.n + 1)
                    wait(act, wp_mm, t.shift(-1).n)
                    act.activation(oT[p][:, :], ps_ot[:, 0:D], ACT.Copy).then_inc(o_out, 1)
                t = tile_at(u, T_X)
                if t is not None:
                    p = t.mod(2)
                    act.wait_ge(x_t, t.n + 1)
                    wait(act, r_mm, t.shift(-1).n)
                    act.activation(xnT[p][:, :], ps_x[:, 0:D], ACT.Copy).then_inc(x_out, 1)

            steps(act, FIRST, NU, TOTAL, BODY, half)

        @block.tensor
        def _(pe):
            pe.wait_ge(s_w, 64)

            def half(u):
                if u.within(NU):
                    gr, t = u.mod(2), u.div(2)
                    p, b = t.mod(2), t.div(2)
                    pe.wait_ge(k_ready, b.n * 2 + 2)
                    pe.wait_ge(q_ready, t.n + 1)
                    wait(pe, sub_done, u.n)
                    for a in range(2):
                        last = pe.matmul(ps_s[:, a, 0:HW], q_s[p][:, gr * P:(gr + 1) * P],
                                         kblk[b.mod(2)][:, (2 * gr + a) * HW:(2 * gr + a + 1) * HW],
                                         start=True, stop=True)
                    last.then_inc(s_mm, 1)
                v = u.shift(-1)
                if v.within(NU):
                    p = v.mod(2)
                    pe.wait_ge(exp_done, v.n + 1)
                    wait(pe, tp_out, v.n)
                    for h in range(HG):
                        last = pe.transpose(ps_tp[0:LK, h // 4, (h % 4) * P:(h % 4 + 1) * P],
                                            pr[p][:, h * LK:(h + 1) * LK], g.ident[:, :])
                    last.then_inc(tp_mm, 1)
                v = u.shift(-2)
                if v.within(NU):
                    p, gr, t = v.mod(2), v.mod(2), v.div(2)
                    b = t.div(2)
                    pe.wait_ge(tp_out, v.n + 1)
                    if gr == 0:
                        wait(pe, o_norm, t.n)
                    for h in range(HG):
                        c = (gr * HG + h) * (DH + 1)
                        last = pe.matmul(ps_o[:, c:c + DH + 1], prT[p][0:LK, h * P:(h + 1) * P],
                                         g.v_all[0:LK, bass.ds(b.n * VW + c, DH + 1)], start=True, stop=True)
                    last.then_inc(pv_mm, 1)
                t = tile_at(u, T_O)
                if t is not None:
                    p = t.mod(2)
                    pe.wait_ge(o_norm, t.n + 1)
                    wait(pe, o_out, t.n)
                    for c in range(DC):
                        last = pe.transpose(ps_ot[:, c * P:(c + 1) * P], o[p][:, c * P:(c + 1) * P], g.ident[:, :])
                    last.then_inc(o_t, 1)
                t = tile_at(u, T_WP)
                if t is not None:
                    p = t.mod(2)
                    pe.wait_ge(o_out, t.n + 1)
                    wait(pe, x1_done, t.n)
                    for c in range(DC):
                        last = pe.matmul(ps_wp[:, 0:D], oT[p][:, c * P:(c + 1) * P], wp[:, c * D:(c + 1) * D],
                                         start=(c == 0), stop=(c == DC - 1))
                    last.then_inc(wp_mm, 1)
                t = tile_at(u, T_R)
                if t is not None:
                    p = t.mod(2)
                    pe.wait_ge(x_out, t.n + 1)
                    for c in range(DC):
                        last = pe.matmul(ps_x[:, D:D + E0], xnT[p][:, c * P:(c + 1) * P], wr[:, c * E0:(c + 1) * E0],
                                         start=(c == 0), stop=(c == DC - 1))
                    last.then_inc(r_mm, 1)
                t = tile_at(u, T_X)
                if t is not None:
                    p = t.mod(2)
                    pe.wait_ge(x_norm, t.n + 1)
                    wait(pe, x_out, t.n)
                    wait(pe, lg_done, t.n)
                    for c in range(DC):
                        last = pe.transpose(ps_x[:, c * P:(c + 1) * P], xn[p][:, c * P:(c + 1) * P], g.ident[:, :])
                    last.then_inc(x_t, 1)

            steps(pe, FIRST, NU, TOTAL, BODY, half)


class Router:

    RING = 16

    def __init__(self, nc, ctx, sem, g, name, n_exp, k, n_slot_tiles, banks):
        self.g, self.E, self.K, self.NS = g, n_exp, k, n_slot_tiles

        def sb(n, shape, dt=F32):
            return ctx.enter_context(nc.sbuf_tensor(f"{name}_{n}", shape, dt))

        E, K, NS = n_exp, k, n_slot_tiles
        self.chosen = sb("chosen", [P, NT * K])
        self.onehot = sb("onehot", [P, NT * K * E], BF16)
        self.prod = sb("prod", [P, NT * K * E])
        self.pair = [sb(f"pair{i}", [P, NT * E], BF16) for i in range(2)]
        self.mask = sb("mask", [P, NT * E], BF16)
        self.tri16 = sb("tri16", [P, P], BF16)
        self.ones16 = sb("ones16", [P, P], BF16)
        self.zero16 = sb("zero16", [P, P], F16)
        self.tot = sb("tot", [P, E * NT])
        self.incl = sb("incl", [P, E * NT])
        self.first = sb("first", [P, NT * E])
        self.count_i = sb("count_i", [P, E], I32)
        self.tiles_i = sb("tiles_i", [P, E], I32)
        self.tiles = sb("tiles", [P, E])
        self.base = sb("base", [P, E])
        self.base_slot = sb("base_slot", [P, E])
        self.e_cmp = self.prod[0:1, :].bitcast(BF16)[:, 0:NS * E]
        self.e_sum = sb("e_sum", [1, NS])
        self.slot_f = sb("slot_f", [P, NT * K])
        self.lo_i = sb("lo_i", [P, NT * K], I32)
        self.hi_i = sb("hi_i", [P, NT * K], I32)
        self.lo = sb("lo", [P, NT * K])
        self.hi = sb("hi", [P, NT * K])
        self.at_lo = [sb(f"at_lo{i}", [P, P], F16) for i in range(self.RING)]
        self.at_hi = [sb(f"at_hi{i}", [P, NS], F16) for i in range(self.RING)]
        self.wsum = sb("wsum", [P, NT])
        self.wrec = sb("wrec", [P, NT])
        self.wexp = sb("wexp", [P, NT])
        self.done, self.s_mask, self.s_count, self.s_one, self.s_pair, self.s_table, self.s_wdiff, self.s_wexp = (
            sem(n) for n in ("done", "mask", "count", "one", "onehots", "table", "wdiff", "wexp"))
        self.ps_pos, self.ps_tot, self.ps_tab = banks

    def chunks(self):
        n = NT * self.E
        return [(i, min(n, i + 512)) for i in range(0, n, 512)]

    def tensor_counts(self, pe):
        pe.wait_ge(self.s_mask, 1)
        for j, (a, b) in enumerate(self.chunks()):
            pe.matmul(self.ps_pos[:, j, 0:b - a], self.tri16[:, :], self.mask[:, a:b], start=True, stop=True)
            last = pe.matmul(self.ps_tot[:, j, 0:b - a], self.ones16[:, :], self.mask[:, a:b], start=True, stop=True)
        last.then_inc(self.s_count, 1)

    def tensor_table(self, pe, c):
        pe.wait_ge(self.s_one, c.n + 1)
        i = c.mod(self.RING)
        pe.matmul(self.ps_tab[:, 0:self.NS], self.at_lo[i][:, :], self.at_hi[i][:, :],
                  start=False, stop=False).then_inc(self.s_pair, 1)

    def tensor_table_open(self, pe):
        pe.matmul(self.ps_tab[:, 0:self.NS], self.zero16[:, :], self.g.iota16[:, 0:self.NS], start=True, stop=False)

    def tensor_table_close(self, pe):
        pe.matmul(self.ps_tab[:, 0:self.NS], self.zero16[:, :], self.g.iota16[:, 0:self.NS], start=False, stop=True)\
            .then_inc(self.s_pair, 1)

    def vector(self, dve, weights):
        g, E, K, NS = self.g, self.E, self.K, self.NS
        links = [0]

        def link(ins):
            links[0] += 1
            ins.then_inc(self.done, 1)
            dve.wait_ge(self.done, links[0])

        top_i = g.top_i[:, :].rearrange("p (t k) -> p t k", k=8)[:, :, 0:K]
        tk = self.chosen[:, :].rearrange("p (t k) -> p t k", k=K)
        iota_e = g.iota[:, 0:E]
        onehot = self.onehot[:, :].rearrange("p (t k e) -> p t k e", k=K, e=E)
        dve.tensor_copy(self.tri16[:, :], g.tri[:, :])
        dve.tensor_copy(self.ones16[:, :], g.ones[:, :])
        dve.memset(self.zero16[:, :], 0.0)
        link(dve.tensor_copy(tk, top_i))
        link(dve.tensor_tensor(self.onehot[:, :].rearrange("p (c e) -> p c e", e=E),
                               iota_e.unsqueeze(1).broadcast_to([P, NT * K, E]),
                               self.chosen[:, :].unsqueeze(2).broadcast_to([P, NT * K, E]), ALU.is_equal))
        mask = self.mask[:, :].rearrange("p (t e) -> p t e", e=E)
        if K == 2:
            dve.tensor_tensor(mask, onehot[:, :, 0, :], onehot[:, :, 1, :], ALU.add).then_inc(self.s_mask, 1)
        else:
            halves = [x[:, :].rearrange("p (t e) -> p t e", e=E) for x in self.pair]
            dve.tensor_tensor(halves[0], onehot[:, :, 0, :], onehot[:, :, 1, :], ALU.add)
            link(dve.tensor_tensor(halves[1], onehot[:, :, 2, :], onehot[:, :, 3, :], ALU.add))
            dve.tensor_tensor(mask, halves[0], halves[1], ALU.add).then_inc(self.s_mask, 1)
        dve.wait_ge(self.s_count, 1)
        tot_et = self.tot[:, :].rearrange("p (e t) -> p t e", e=E)
        for j, (a, b) in enumerate(self.chunks()):
            last = dve.tensor_copy(tot_et[:, a // E:b // E, :],
                                   self.ps_tot[:, j, 0:b - a].rearrange("p (t e) -> p t e", e=E))
        link(last)
        link(dve.tensor_tensor_scan(self.incl[:, :], g.not_first[:, 0:E * NT], self.tot[:, :], 0.0, ALU.mult, ALU.add))
        incl3 = self.incl[:, :].rearrange("p (e t) -> p e t", t=NT)
        tot3 = self.tot[:, :].rearrange("p (e t) -> p e t", t=NT)
        link(dve.tensor_scalar(self.count_i[:, :].unsqueeze(2), incl3[:, :, NT - 1:NT], float(P - 1), None, ALU.add))
        link(dve.tensor_scalar(self.tiles_i[:, :], self.count_i[:, :], 7, None, ALU.arith_shift_right))
        link(dve.tensor_copy(self.tiles[:, :], self.tiles_i[:, :]))
        link(dve.tensor_tensor_scan(self.base[:, :], g.ones[:, 0:E], self.tiles[:, :], 0.0, ALU.mult, ALU.add))
        link(dve.tensor_tensor(self.base[:, :], self.base[:, :], self.tiles[:, :], ALU.subtract))
        link(dve.tensor_scalar(self.base_slot[:, :], self.base[:, :], float(P), None, ALU.mult))
        link(dve.tensor_tensor(incl3, incl3, tot3, ALU.subtract))
        link(dve.tensor_tensor(incl3, incl3, self.base_slot[:, :].unsqueeze(2).broadcast_to([P, E, NT]), ALU.add))
        first = self.first[:, :].rearrange("p (t e) -> p t e", e=E)
        incl_te = self.incl[:, :].rearrange("p (e t) -> p t e", t=NT)
        for j, (a, b) in enumerate(self.chunks()):
            last = dve.tensor_tensor(first[:, a // E:b // E, :],
                                     self.ps_pos[:, j, 0:b - a].rearrange("p (t e) -> p t e", e=E),
                                     incl_te[:, a // E:b // E, :], ALU.add)
        link(last)
        link(dve.tensor_tensor(self.prod[:, :].rearrange("p (t k e) -> p t k e", k=K, e=E), onehot,
                               first.unsqueeze(2).broadcast_to([P, NT, K, E]), ALU.mult))
        link(dve.tensor_reduce(self.slot_f[:, :], self.prod[:, :].rearrange("p (c e) -> p c e", e=E), AX.X, ALU.add))
        link(dve.tensor_copy(g.slot[:, 0:NT * K], self.slot_f[:, :]))
        dve.tensor_scalar(self.lo_i[:, :], g.slot[:, 0:NT * K], P - 1, None, ALU.bitwise_and)
        link(dve.tensor_scalar(self.hi_i[:, :], g.slot[:, 0:NT * K], 7, None, ALU.arith_shift_right))
        dve.tensor_copy(self.lo[:, :], self.lo_i[:, :])
        link(dve.tensor_copy(self.hi[:, :], self.hi_i[:, :]))

        def onehots(c):
            wait(dve, self.s_pair, c.shift(1 - self.RING).n)
            i = c.mod(self.RING)
            dve.tensor_scalar(self.at_lo[i][:, :], g.iota16[:, 0:P], self.lo[:, bass.ds(c.n, 1)], None,
                              ALU.is_equal)
            dve.tensor_scalar(self.at_hi[i][:, :], g.iota16[:, 0:NS], self.hi[:, bass.ds(c.n, 1)],
                              g.tokval[:, bass.ds(c.div(K).n, 1)], ALU.is_equal, ALU.mult).then_inc(self.s_one, 1)

        steps(dve, self.RING, NT * K, NT * K, self.RING, onehots)
        link(dve.tensor_tensor(self.e_cmp.rearrange("p (j e) -> p j e", e=E),
                               self.base[0:1, :].unsqueeze(1).broadcast_to([1, NS, E]),
                               g.iota[0:1, 0:NS].unsqueeze(2).broadcast_to([1, NS, E]), ALU.is_le))
        link(dve.tensor_reduce(self.e_sum[0:1, :], self.e_cmp.rearrange("p (j e) -> p j e", e=E), AX.X, ALU.add))
        link(dve.tensor_scalar(g.expert[0:1, 0:NS], self.e_sum[0:1, :], -1.0, None, ALU.add))
        weights(dve, link)
        dve.wait_ge(self.s_pair, NT * K + 1)
        dve.tensor_scalar(g.token[:, 0:NS], self.ps_tab[:, 0:NS], float(MID), None, ALU.add).then_inc(self.s_table, 1)


def route0_phase(nc, g):
    ctx = ExitStack()
    with ctx:
        sem = semaphores(nc, ctx, "r0_")
        r = Router(nc, ctx, sem, g, "r0", E0, K0, NS0, (g.pair[0], g.pair[1], g.bank[4]))
        s_w2 = sem("w2")
        block = ctx.enter_context(nc.Block())
        top = g.top_v[:, :].rearrange("p (t k) -> p t k", k=8)
        w = g.weight[:, 0:NT * K0].rearrange("p (t k) -> p t k", k=K0)

        @block.sync
        def _(sp):
            for e in range(E0):
                n = M0 // P * D
                sp.dma_start(g.w2[:, e * n:(e + 1) * n], g.ins["w2"][:, e * n:(e + 1) * n]).then_inc(s_w2, 16)
            sp.wait_ge(s_w2, 16 * E0)

        @block.vector
        def _(dve):
            def weights(dve, link):
                dve.tensor_tensor(r.wsum[:, :].unsqueeze(2), top[:, :, 1:2], top[:, :, 0:1], ALU.subtract)\
                    .then_inc(r.s_wdiff, 1)
                dve.wait_ge(r.s_wexp, 1)
                link(dve.tensor_scalar(r.wsum[:, :], r.wexp[:, :], 1.0, None, ALU.add))
                link(dve.reciprocal(w[:, :, 0:1], r.wsum[:, :].unsqueeze(2)))
                link(dve.tensor_tensor(w[:, :, 1:2], w[:, :, 0:1], r.wexp[:, :].unsqueeze(2), ALU.mult))

            r.vector(dve, weights)

        @block.scalar
        def _(act):
            act.wait_ge(r.s_wdiff, 1)
            act.activation(r.wexp[:, :], r.wsum[:, :], ACT.Exp).then_inc(r.s_wexp, 1)

        @block.tensor
        def _(pe):
            r.tensor_counts(pe)
            r.tensor_table_open(pe)
            steps(pe, r.RING, NT * K0, NT * K0, r.RING, lambda c: r.tensor_table(pe, c))
            r.tensor_table_close(pe)


def moe0_phase(nc, g):
    ctx = ExitStack()
    with ctx:
        def sb(name, shape, dt=F32):
            return ctx.enter_context(nc.sbuf_tensor("m0_" + name, shape, dt))

        sem = semaphores(nc, ctx, "m0_")

        MC = M0 // P
        idx = [sb(f"idx{i}", [P, 1], I32) for i in range(GB)]
        xg = [sb(f"xg{i}", [P, D]) for i in range(GB)]
        xT = [sb(f"xT{i}", [P, D]) for i in range(2)]
        sg = [sb(f"sg{i}", [P, M0]) for i in range(2)]
        h = [sb(f"h{i}", [P, M0]) for i in range(2)]
        hT = [sb(f"hT{i}", [P, M0]) for i in range(2)]
        y = [sb(f"y{i}", [P, D]) for i in range(2)]
        passed = sem("passed_pool")
        s_g = [sem(f"s_g{i}") for i in range(GB)]
        y_st = [sem(f"y_st{i}") for i in range(2)]
        idx_ready, x_t, x_out, gu_mm, silu_done, h_done, h_t, h_out, y_mm, y_out = (
            sem(n) for n in ("idx_ready", "x_t", "x_out", "gu_mm", "silu_done", "h_done", "h_t", "h_out", "y_mm",
                             "y_out"))
        ps_gu, ps_x, ps_ht, ps_y = g.pair[0:2], g.bank[4], g.bank[5], g.bank[6]
        block = ctx.enter_context(nc.Block())

        @block.gpsimd
        def _(pool):
            def gather(j):
                p = j.mod(GB)
                wait_alone(pool, x_t, j.shift(1 - GB).n, passed)
                pool.tensor_copy(idx[p][:, :], g.token[:, bass.ds(j.n, 1)]).then_inc(idx_ready, 1)
                wait_alone(pool, idx_ready, j.n + 1, passed)
                pool.indirect_dma_start(out=xg[p][:, :], out_offset=None, in_=g.xn,
                                        in_offset=bass.IndirectOffsetOnAxis(ap=idx[p][:, :], axis=0))\
                    .then_inc(s_g[p], 16)

            steps(pool, GB, NS0, NS0, GB, gather)

        @block.sync
        def _(sp):
            def store(j):
                p = j.mod(2)
                sp.wait_ge(y_out, j.n + 1)
                sp.dma_start(g.y0[bass.ds(j.n * P, P), :], y[p][:, :]).then_inc(y_st[p], 16)

            steps(sp, 2, NS0, NS0, 2, store)
            for p in range(2):
                sp.wait_ge(y_st[p], NS0 // 2 * 16)

        @block.scalar
        def _(act):
            def step(s):
                j = s
                if j.within(NS0):
                    p = j.mod(2)
                    act.wait_ge(x_t, j.n + 1)
                    wait(act, gu_mm, j.shift(-1).n)
                    act.activation(xT[p][:, :], ps_x[:, 0:D], ACT.Copy).then_inc(x_out, 1)
                j = s.shift(-1)
                if j.within(NS0):
                    p = j.mod(2)
                    act.wait_ge(gu_mm, j.n + 1)
                    wait(act, h_done, j.shift(-1).n)
                    act.activation(sg[p][:, :], ps_gu[p][:, 0, :], ACT.Silu).then_inc(silu_done, 1)
                j = s.shift(-2)
                if j.within(NS0):
                    p = j.mod(2)
                    act.wait_ge(h_t, j.n + 1)
                    wait(act, y_mm, j.shift(-1).n)
                    act.activation(hT[p][:, :], ps_ht[:, 0:M0], ACT.Copy).then_inc(h_out, 1)

            steps(act, 4, NS0, NS0 + 2, 2, step)

        @block.vector
        def _(dve):
            def step(s):
                j = s.shift(-1)
                if j.within(NS0):
                    p = j.mod(2)
                    dve.wait_ge(silu_done, j.n + 1)
                    wait(dve, h_t, j.shift(-1).n)
                    dve.tensor_tensor(h[p][:, :], ps_gu[p][:, 1, :], sg[p][:, :], ALU.mult).then_inc(h_done, 1)
                j = s.shift(-3)
                if j.within(NS0):
                    p = j.mod(2)
                    dve.wait_ge(y_mm, j.n + 1)
                    wait(dve, y_st[p], j.div(2).n * 16)
                    dve.tensor_copy(y[p][:, :], ps_y[:, 0:D]).then_inc(y_out, 1)

            steps(dve, 6, NS0, NS0 + 3, 2, step)

        @block.tensor
        def _(pe):
            e = [pe.alloc_register(f"m0_e{i}") for i in range(GB)]

            def step(s):
                j = s.shift(-1)
                if j.within(NS0):
                    pe.reg_load(e[j.mod(GB)], g.expert[0:1, bass.ds(j.n, 1)])
                j = s
                if j.within(NS0):
                    p = j.mod(GB)
                    pe.wait_ge(s_g[p], (j.div(GB).n + 1) * 16)
                    wait(pe, x_out, j.n)
                    for c in range(DC):
                        last = pe.transpose(ps_x[:, c * P:(c + 1) * P], xg[p][:, c * P:(c + 1) * P], g.ident[:, :])
                    last.then_inc(x_t, 1)
                j = s.shift(-1)
                if j.within(NS0):
                    p = j.mod(2)
                    ex = pe.snap(e[j.mod(GB)], min_val=0, max_val=E0 - 1)
                    pe.wait_ge(x_out, j.n + 1)
                    wait(pe, h_done, j.shift(-1).n)
                    for half in range(2):
                        for c in range(DC):
                            at = (c * 2 + half) * M0
                            last = pe.matmul(ps_gu[p][:, half, :], xT[p][:, c * P:(c + 1) * P],
                                             g.w13[:, bass.ds(ex * (DC * 2 * M0) + at, M0)],
                                             start=(c == 0), stop=(c == DC - 1))
                    last.then_inc(gu_mm, 1)
                j = s.shift(-2)
                if j.within(NS0):
                    p = j.mod(2)
                    pe.wait_ge(h_done, j.n + 1)
                    wait(pe, h_out, j.n)
                    for c in range(MC):
                        last = pe.transpose(ps_ht[:, c * P:(c + 1) * P], h[p][:, c * P:(c + 1) * P], g.ident[:, :])
                    last.then_inc(h_t, 1)
                j = s.shift(-3)
                if j.within(NS0):
                    p = j.mod(2)
                    ex = pe.snap(e[j.mod(GB)], min_val=0, max_val=E0 - 1)
                    pe.wait_ge(h_out, j.n + 1)
                    wait(pe, y_out, j.n)
                    for c in range(MC):
                        last = pe.matmul(ps_y[:, 0:D], hT[p][:, c * P:(c + 1) * P],
                                         g.w2[:, bass.ds(ex * (MC * D) + c * D, D)],
                                         start=(c == 0), stop=(c == MC - 1))
                    last.then_inc(y_mm, 1)

            steps(pe, 8, NS0, NS0 + 3, GB, step)


def attention1_phase(nc, g):
    ctx = ExitStack()
    with ctx:
        def sb(name, shape, dt=F32):
            return ctx.enter_context(nc.sbuf_tensor("at1_" + name, shape, dt))

        sem = semaphores(nc, ctx, "at1_")

        SCALE = float(D) ** -0.5
        wq, wk, wv, wo = (sb(n, [P, DC * D]) for n in ("wq", "wk", "wv", "wo"))
        wr = sb("wr", [P, DC * E1])
        qb, kb, qbs = (sb(n, [P, DC]) for n in ("qb", "kb", "qbs"))
        bv, bo, rb = sb("bv", [P, D]), sb("bo", [1, D]), sb("rb", [P, E1])
        ring = lambda name, shape, dt=F32, n=2: [sb(f"{name}{i}", shape, dt) for i in range(n)]
        idx = [ring(f"idx{k}_", [P, 1], I32, n=GB) for k in range(K0)]
        yg = [ring(f"yg{k}_", [P, D], n=GB) for k in range(K0)]
        x1, x2, x2r = (ring(n, [P, D]) for n in ("x1_", "x2_", "x2r"))
        xn = ring("xn", [P, D], n=4)
        ctx_s = ring("ctx", [P, DC * LK])
        kT = ring("kT", [P, DC * LK])
        v = ring("v", [P, D])
        xnT, qT = ring("xnT", [P, D]), ring("qT", [P, D])
        nmx, den, rec = ring("nmx", [P, 1]), ring("den", [P, 1]), ring("rec", [P, 1])
        pr, prT = ring("pr", [P, LK]), ring("prT", [P, P])
        o, oT = ring("o", [P, D]), ring("oT", [P, D])
        x3, xm, xmT = ring("x3_", [P, D]), ring("xm", [P, D]), ring("xmT", [P, D])
        lg, lmx, ez, sume, rsum, sc = (ring(n, [P, w]) for n, w in (
            ("lg", E1), ("lmx", 1), ("ez", E1), ("sume", 1), ("rsum", 1), ("sc", E1)))
        top, ix = ring("top", [P, 8]), ring("ix", [P, 8], U32)
        s_w, s_next, s_qbs = sem("s_w"), sem("s_next"), sem("s_qbs")
        passed = [sem(f"passed_{n}") for n in ("dve", "pool", "act")]
        s_passed_sp = sem("passed_sp")
        lna = LayerNorm(sb, sem, "lna", passed, g.minus_half)
        lnm = LayerNorm(sb, sem, "lnm", passed, g.minus_half)
        s_x1, s_x2r, s_ctx, x2_st, x3_st, xm_st = ([sem(f"{n}{i}") for i in range(2)] for n in (
            "s_x1", "s_x2r", "s_ctx", "x2_st", "x3_st", "xm_st"))
        s_y = [[sem(f"s_y{k}_{i}") for i in range(GB)] for k in range(K0)]
        (idx_ready, half_sum, x2_done, xn_done, x_t, x_out, q_mm, q_out, kv_mm, kT_out, v_out, s_mm,
         max_done, exp_done, rec_done, p_t, p_out, pv_mm, o_done, o_t, o_out, wo_mm, x3_done, xm_done, xm_t, xm_out,
         r_mm, lg_done, lmx_done, ez_done, rsum_done, sc_done, top_done, ix_done) = (sem(n) for n in (
             "idx_ready", "half_sum", "x2_done", "xn_done", "x_t", "x_out", "q_mm", "q_out",
             "kv_mm", "kT_out", "v_out", "s_mm", "max_done", "exp_done", "rec_done", "p_t", "p_out", "pv_mm", "o_done", "o_t",
             "o_out", "wo_mm", "x3_done", "xm_done", "xm_t", "xm_out", "r_mm", "lg_done", "lmx_done", "ez_done",
             "rsum_done", "sc_done", "top_done", "ix_done"))
        ps_x, ps_q, ps_s, ps_t, ps_o, ps_wo, ps_m, ps_kv = g.bank
        block = ctx.enter_context(nc.Block())
        SUM, XN, Q, S, PT, PV, OT, WO, XM, XMT, R, SC = 1, 2, 3, 4, 5, 6, 7, 8, 9, 10, 11, 12
        FIRST, BODY = 12, 4
        GU_FROM, GU_LOADS = 4, 8
        LEAD = 2

        def stage(s, skew):
            t = s.shift(-skew)
            return t if t.within(NT) else None

        def rows(t):
            return bass.ds(t.n * P, P)

        @block.sync
        def _(sp):
            for dst, src in ((wq, g.ins["wq1"]), (wk, g.ins["wk1"]), (wv, g.ins["wv1"]), (wo, g.ins["wo1"]), (wr, g.ins["wr1"]),
                             (qb, g.ins["bq1"]), (kb, g.ins["bk1"]), (bv, g.ins["bv1"]), (bo, g.ins["bo1"]), (rb, g.ins["rb1"])):
                sp.dma_start(dst[:, :], src).then_inc(s_w, 16)

            def step(s):
                if (t := stage(s, 0)) is not None:
                    p, b = t.mod(2), t.div(2)
                    wait(sp, x2_done, t.shift(-1).n)
                    sp.dma_start(x1[p][:, :], g.x1[rows(t), :]).then_inc(s_x1[p], 16)
                    if t.mod(2) == 0:
                        wait(sp, kv_mm, b.shift(-1).n)
                        sp.dma_start(ctx_s[b.mod(2)][:, :].rearrange("p (c k) -> p c k", c=DC),
                                 g.ins["ctx"].rearrange("p (c n) -> p c n", c=DC)[:, :, bass.ds(b.n * LK, LK)])\
                        .then_inc(s_ctx[b.mod(2)], 16)
                if (t := stage(s, SUM + 1)) is not None:
                    p = t.mod(2)
                    sp.wait_ge(x2_done, t.n + 1)
                    sp.dma_start(g.x2[rows(t), :], x2[p][:, :]).then_inc(x2_st[p], 16)
                if (t := stage(s, PV)) is not None:
                    p = t.mod(2)
                    wait_alone(sp, x2_st[p], (t.div(2).n + 1) * 16, s_passed_sp)
                    wait(sp, x3_done, t.shift(-1).n)
                    sp.dma_start(x2r[p][:, :], g.x2[rows(t), :]).then_inc(s_x2r[p], 16)
                if (t := stage(s, WO + 1)) is not None:
                    p = t.mod(2)
                    sp.wait_ge(x3_done, t.n + 1)
                    sp.dma_start(g.x3[rows(t), :], x3[p][:, :]).then_inc(x3_st[p], 16)
                if (t := stage(s, XM + 1)) is not None:
                    p = t.mod(2)
                    sp.wait_ge(xm_done, t.n + 1)
                    sp.dma_start(g.xn4[rows(t), :], xm[p][:, :]).then_inc(xm_st[p], 16)

            steps(sp, FIRST, NT, NT + XM + 2, BODY, step)
            for p in range(2):
                for st in (x2_st, x3_st, xm_st):
                    sp.wait_ge(st[p], NT // 2 * 16)
            sp.wait_ge(s_next, GU_LOADS * 16)

        @block.gpsimd
        def _(pool):
            pool.wait_ge(s_w, 160)

            def step(s):
                if (t := stage(s, WO + LEAD)) is not None:
                    lnm.invert(pool, t)
                if (t := stage(s, SUM + LEAD)) is not None:
                    lna.invert(pool, t)
                if (t := stage(s, 0)) is not None:
                    p = t.mod(GB)
                    wait_alone(pool, x2_done, t.shift(1 - GB).n, passed[1])
                    for k in range(K0):
                        pool.tensor_copy(idx[k][p][:, :], g.slot[:, bass.ds(t.n * K0 + k, 1)]).then_inc(idx_ready, 1)
                    wait_alone(pool, idx_ready, t.n * K0 + K0, passed[1])
                    for k in range(K0):
                        pool.indirect_dma_start(out=yg[k][p][:, :], out_offset=None, in_=g.y0,
                                                in_offset=bass.IndirectOffsetOnAxis(ap=idx[k][p][:, :], axis=0))\
                            .then_inc(s_y[k][p], 16)

            steps(pool, FIRST, NT, NT + WO + LEAD, BODY, step)

        @block.vector
        def _(dve):
            dve.wait_ge(s_w, 160)
            dve.tensor_scalar(qbs[:, :], qb[:, :], SCALE, None, ALU.mult).then_inc(s_qbs, 1)

            def step(s):
                if (t := stage(s, XM)) is not None:
                    p = t.mod(2)
                    wait(dve, xm_st[p], t.div(2).n * 16)
                    wait(dve, xm_t, t.shift(-1).n)
                    lnm.apply(dve, x3[p][:, :], xm[p][:, :], t).then_inc(xm_done, 1)
                if (t := stage(s, PV)) is not None:
                    p = t.mod(2)
                    dve.wait_ge(pv_mm, t.n + 1)
                    dve.wait_ge(rec_done, t.n + 1)
                    wait(dve, o_t, t.shift(-1).n)
                    dve.scalar_tensor_tensor(o[p][:, :], ps_o[:, 0:D], rec[p][:, :], xn[t.mod(4)][:, :],
                                             ALU.mult, ALU.add).then_inc(o_done, 1)
                if (t := stage(s, R)) is not None:
                    p = t.mod(2)
                    dve.wait_ge(r_mm, t.n + 1)
                    wait(dve, ez_done, t.shift(-1).n)
                    dve.tensor_tensor(lg[p][:, :], ps_m[:, D:D + E1], rb[:, :], ALU.add).then_inc(lg_done, 1)
                    dve.wait_ge(lg_done, t.n + 1)
                    dve.tensor_reduce(lmx[p][:, :], lg[p][:, :], AX.X, ALU.max, negate=True).then_inc(lmx_done, 1)
                if (t := stage(s, XN)) is not None:
                    wait(dve, x_t, t.shift(-3).n)
                    wait(dve, o_done, t.shift(-3).n)
                    lna.apply(dve, x2[t.mod(2)][:, :], xn[t.mod(4)][:, :], t).then_inc(xn_done, 1)
                if (t := stage(s, S)) is not None:
                    p = t.mod(2)
                    dve.wait_ge(s_mm, t.n + 1)
                    dve.tensor_reduce(nmx[p][:, :], ps_s[:, 0:LK], AX.X, ALU.max, negate=True).then_inc(max_done, 1)
                if (t := stage(s, WO)) is not None:
                    p = t.mod(2)
                    dve.wait_ge(wo_mm, t.n + 1)
                    dve.wait_ge(s_x2r[p], (t.div(2).n + 1) * 16)
                    wait(dve, x3_st[p], t.div(2).n * 16)
                    dve.tensor_tensor(x3[p][:, :], ps_wo[:, 0:D], x2r[p][:, :], ALU.add).then_inc(x3_done, 1)
                    dve.wait_ge(x3_done, t.n + 1)
                    lnm.moments(dve, x3[p][:, :], t)
                if (t := stage(s, Q)) is not None and t.mod(2) == 0:
                    b = t.div(2)
                    dve.wait_ge(kT_out, b.n * 2 + 2)
                    wait(dve, pv_mm, b.shift(-1).n * 2)
                    dve.tensor_tensor(v[b.mod(2)][0:LK, :], ps_kv[0:LK, D:2 * D], bv[0:LK, :], ALU.add)\
                        .then_inc(v_out, 1)
                if (t := stage(s, SC)) is not None:
                    p = t.mod(2)
                    dve.wait_ge(ez_done, t.n + 1)
                    dve.reciprocal(rsum[p][:, :], sume[p][:, :]).then_inc(rsum_done, 1)
                    dve.wait_ge(rsum_done, t.n + 1)
                    dve.tensor_scalar(sc[p][:, :], ez[p][:, :], rsum[p][:, :], None, ALU.mult).then_inc(sc_done, 1)
                    top_of(dve, g, sc[p], top[p], ix[p], t, sc_done, top_done, ix_done, passed)
                if (t := stage(s, SUM)) is not None:
                    p = t.mod(2)
                    dve.wait_ge(s_x1[p], (t.div(2).n + 1) * 16)
                    dve.wait_ge(s_y[0][t.mod(GB)], (t.div(GB).n + 1) * 16)
                    wait(dve, x2_st[p], t.div(2).n * 16)
                    dve.scalar_tensor_tensor(x2[p][:, :], yg[0][t.mod(GB)][:, :], g.weight[:, bass.ds(t.n * K0, 1)],
                                             x1[p][:, :], ALU.mult, ALU.add).then_inc(half_sum, 1)
                    dve.wait_ge(s_y[1][t.mod(GB)], (t.div(GB).n + 1) * 16)
                    dve.wait_ge(half_sum, t.n + 1)
                    dve.scalar_tensor_tensor(x2[p][:, :], yg[1][t.mod(GB)][:, :], g.weight[:, bass.ds(t.n * K0 + 1, 1)],
                                             x2[p][:, :], ALU.mult, ALU.add).then_inc(x2_done, 1)
                    dve.wait_ge(x2_done, t.n + 1)
                    lna.moments(dve, x2[p][:, :], t)
                if (t := stage(s, PT)) is not None:
                    p = t.mod(2)
                    dve.wait_ge(exp_done, t.n + 1)
                    dve.reciprocal(rec[p][:, :], den[p][:, :]).then_inc(rec_done, 1)

            steps(dve, FIRST, NT, NT + SC, BODY, step)

        @block.scalar
        def _(act):
            act.wait_ge(s_w, 160)
            act.wait_ge(s_qbs, 1)

            def step(s):
                if s.loop is None and GU_FROM <= s.off < GU_FROM + GU_LOADS:
                    n = E1 // GU_LOADS * DC * 2 * M1
                    e = s.off - GU_FROM
                    act.dma_start(g.gu[:, e * n:(e + 1) * n], g.ins["gu"][:, e * n:(e + 1) * n]).then_inc(s_next, 16)
                if (t := stage(s, Q)) is not None:
                    p, b = t.mod(2), t.div(2)
                    if t.mod(2) == 0:
                        act.wait_ge(kv_mm, b.n + 1)
                        wait(act, s_mm, b.shift(-1).n * 2)
                        for c in range(DC):
                            act.activation(kT[b.mod(2)][:, c * LK:(c + 1) * LK], ps_kv[:, c * LK:(c + 1) * LK],
                                           ACT.Identity, bias=kb[:, c:c + 1]).then_inc(kT_out, 1)
                    act.wait_ge(q_mm, t.n + 1)
                    wait(act, s_mm, t.shift(-1).n)
                    for c in range(DC):
                        act.activation(qT[p][:, c * P:(c + 1) * P], ps_q[:, c * P:(c + 1) * P], ACT.Identity,
                                       bias=qbs[:, c:c + 1], scale=SCALE).then_inc(q_out, 1)
                if (t := stage(s, R)) is not None:
                    p = t.mod(2)
                    act.wait_ge(lmx_done, t.n + 1)
                    wait(act, sc_done, t.shift(-1).n)
                    act.activation(ez[p][:, :], lg[p][:, :], ACT.Exp, bias=lmx[p][:, :],
                                   accum_out=sume[p][:, :]).then_inc(ez_done, 1)
                if (t := stage(s, S)) is not None:
                    p = t.mod(2)
                    act.wait_ge(max_done, t.n + 1)
                    wait(act, p_t, t.shift(-1).n)
                    wait(act, rec_done, t.shift(-1).n)
                    act.activation(pr[p][:, :], ps_s[:, 0:LK], ACT.Exp, bias=nmx[p][:, :],
                                   accum_out=den[p][:, :]).then_inc(exp_done, 1)
                if (t := stage(s, PT)) is not None:
                    p = t.mod(2)
                    act.wait_ge(p_t, t.n + 1)
                    wait(act, pv_mm, t.shift(-1).n)
                    act.activation(prT[p][0:LK, :], ps_t[0:LK, 0:P], ACT.Copy).then_inc(p_out, 1)
                if (t := stage(s, OT)) is not None:
                    p = t.mod(2)
                    act.wait_ge(o_t, t.n + 1)
                    wait(act, wo_mm, t.shift(-1).n)
                    act.activation(oT[p][:, :], ps_t[:, P:P + D], ACT.Copy).then_inc(o_out, 1)
                if (t := stage(s, XMT)) is not None:
                    p = t.mod(2)
                    wait_alone(act, xm_t, t.n + 1, passed[2])
                    act.activation(g.xn4T[:, :].rearrange("p (c n) -> p c n", c=DC)[:, :, rows(t)],
                                   ps_m[:, 0:D].rearrange("p (c n) -> p c n", c=DC), ACT.Copy)
                    wait(act, r_mm, t.shift(-1).n)
                    act.activation(xmT[p][:, :], ps_m[:, 0:D], ACT.Copy).then_inc(xm_out, 1)
                if (t := stage(s, XN)) is not None:
                    p = t.mod(2)
                    act.wait_ge(x_t, t.n + 1)
                    wait(act, q_mm, t.shift(-1).n)
                    act.activation(xnT[p][:, :], ps_x[:, 0:D], ACT.Copy).then_inc(x_out, 1)

            steps(act, FIRST, NT, NT + R + 1, BODY, step)

        @block.tensor
        def _(pe):
            pe.wait_ge(s_w, 160)

            def step(s):
                if (t := stage(s, PV)) is not None:
                    p, b = t.mod(2), t.div(2)
                    pe.wait_ge(p_out, t.n + 1)
                    pe.wait_ge(v_out, b.n + 1)
                    wait(pe, o_done, t.n)
                    pe.matmul(ps_o[:, 0:D], prT[p][0:LK, :], v[b.mod(2)][0:LK, :], start=True, stop=True)\
                        .then_inc(pv_mm, 1)
                if (t := stage(s, S)) is not None:
                    p, b = t.mod(2), t.div(2)
                    pe.wait_ge(q_out, t.n * 2 + 2)
                    pe.wait_ge(kT_out, b.n * 2 + 2)
                    wait(pe, exp_done, t.n)
                    for c in range(DC):
                        last = pe.matmul(ps_s[:, 0:LK], qT[p][:, c * P:(c + 1) * P],
                                         kT[b.mod(2)][:, c * LK:(c + 1) * LK], start=(c == 0), stop=(c == DC - 1))
                    last.then_inc(s_mm, 1)
                if (t := stage(s, R)) is not None:
                    p = t.mod(2)
                    pe.wait_ge(xm_out, t.n + 1)
                    for c in range(DC):
                        last = pe.matmul(ps_m[:, D:D + E1], xmT[p][:, c * P:(c + 1) * P], wr[:, c * E1:(c + 1) * E1],
                                         start=(c == 0), stop=(c == DC - 1))
                    last.then_inc(r_mm, 1)
                if (t := stage(s, WO)) is not None:
                    p = t.mod(2)
                    pe.wait_ge(o_out, t.n + 1)
                    wait(pe, x3_done, t.n)
                    pe.matmul(ps_wo[:, 0:D], g.ones[0:1, :], bo[0:1, :], start=True, stop=False)
                    for c in range(DC):
                        last = pe.matmul(ps_wo[:, 0:D], oT[p][:, c * P:(c + 1) * P], wo[:, c * D:(c + 1) * D],
                                         start=False, stop=(c == DC - 1))
                    last.then_inc(wo_mm, 1)
                if (t := stage(s, Q)) is not None:
                    p, b = t.mod(2), t.div(2)
                    if t.mod(2) == 0:
                        cs = ctx_s[b.mod(2)]
                        pe.wait_ge(s_ctx[b.mod(2)], (b.div(2).n + 1) * 16)
                        wait(pe, kT_out, b.n * 2)
                        wait(pe, v_out, b.n)
                        for m in range(DC):
                            for c in range(DC):
                                pe.matmul(ps_kv[:, m * LK:(m + 1) * LK], wk[:, c * D + m * P:c * D + (m + 1) * P],
                                          cs[:, c * LK:(c + 1) * LK], start=(c == 0), stop=(c == DC - 1))
                        for c in range(DC):
                            last = pe.matmul(ps_kv[0:LK, D:2 * D], cs[:, c * LK:(c + 1) * LK],
                                             wv[:, c * D:(c + 1) * D], start=(c == 0), stop=(c == DC - 1))
                        last.then_inc(kv_mm, 1)
                    pe.wait_ge(x_out, t.n + 1)
                    wait(pe, q_out, t.n * 2)
                    for m in range(DC):
                        for c in range(DC):
                            last = pe.matmul(ps_q[:, m * P:(m + 1) * P], wq[:, c * D + m * P:c * D + (m + 1) * P],
                                             xnT[p][:, c * P:(c + 1) * P], start=(c == 0), stop=(c == DC - 1))
                    last.then_inc(q_mm, 1)
                if (t := stage(s, PT)) is not None:
                    p = t.mod(2)
                    pe.wait_ge(exp_done, t.n + 1)
                    wait(pe, p_out, t.n)
                    wait(pe, o_out, t.shift(-2).n)
                    pe.transpose(ps_t[0:LK, 0:P], pr[p][:, :], g.ident[:, :]).then_inc(p_t, 1)
                if (t := stage(s, XN)) is not None:
                    p = t.mod(2)
                    pe.wait_ge(xn_done, t.n + 1)
                    wait(pe, x_out, t.n)
                    for c in range(DC):
                        last = pe.transpose(ps_x[:, c * P:(c + 1) * P], xn[t.mod(4)][:, c * P:(c + 1) * P], g.ident[:, :])
                    last.then_inc(x_t, 1)
                if (t := stage(s, OT)) is not None:
                    p = t.mod(2)
                    pe.wait_ge(o_done, t.n + 1)
                    wait(pe, o_out, t.n)
                    if (q := stage(s, PT)) is not None:
                        pe.wait_ge(p_out, q.n + 1)
                    for c in range(DC):
                        last = pe.transpose(ps_t[:, (c + 1) * P:(c + 2) * P], o[p][:, c * P:(c + 1) * P], g.ident[:, :])
                    last.then_inc(o_t, 1)
                if (t := stage(s, XMT)) is not None:
                    p = t.mod(2)
                    pe.wait_ge(xm_done, t.n + 1)
                    wait(pe, xm_out, t.n)
                    wait(pe, lg_done, t.n)
                    for c in range(DC):
                        last = pe.transpose(ps_m[:, c * P:(c + 1) * P], xm[p][:, c * P:(c + 1) * P], g.ident[:, :])
                    last.then_inc(xm_t, 1)

            steps(pe, FIRST, NT, NT + R + 1, BODY, step)


class SharedExpert:

    LAG = 5

    def __init__(self, nc, ctx, sem, g, name, first_block, blocks, banks, on_vector):
        def sb(n, shape, dt=F32):
            return ctx.enter_context(nc.sbuf_tensor(f"{name}_{n}", shape, dt))

        self.on_vector = on_vector
        self.g, self.units, self.t0 = g, 4 * blocks, 4 * first_block
        self.MC = MS // P
        self.sg, self.up = ([sb(f"{n}{i}", [P, MS]) for i in range(2)] for n in ("sg", "up"))
        self.h = [sb(f"h{i}", [P, 512]) for i in range(8)]
        self.ysb, self.x3, self.xs = ([sb(f"{n}{i}", [P, D]) for i in range(2)] for n in ("y", "x3", "xs"))
        self.g_mm, self.u_mm, self.sg_done, self.up_done, self.h_done, self.y_mm, self.y_out, self.xs_done = (
            sem(n) for n in ("g_mm", "u_mm", "sg_done", "up_done", "h_done", "y_mm", "y_out", "xs_done"))
        self.s_x3, self.xs_st = ([sem(f"{n}{i}") for i in range(2)] for n in ("s_x3", "xs_st"))
        self.ps_g, self.ps_u, self.ps_y = banks
        self.u_free, self.y_free = (self.h_done, self.xs_done) if on_vector else (self.up_done, self.y_out)

    def behind(self, c):
        t = c.shift(-self.LAG)
        return t if t.within(self.units) else None

    def tensor(self, pe, c):
        g = self.g
        if c.within(self.units):
            block = c.div(4)
            for ps, w, s_mm, s_free in ((self.ps_g, g.sg_w, self.g_mm, self.sg_done),
                                        (self.ps_u, g.su_w, self.u_mm, self.u_free)):
                wait(pe, s_free, c.n)
                for d in range(DC):
                    m = c.mod(4)
                    last = pe.matmul(ps[:, :], w[:, d * MS + m * P:d * MS + (m + 1) * P],
                                     g.xn4T[:, bass.ds(block.n * 512 + (d * NTOK + self.t0 * P), 512)],
                                     start=(d == 0), stop=(d == DC - 1))
                last.then_inc(s_mm, 1)
        if (t := self.behind(c)) is not None:
            pe.wait_ge(self.h_done, t.div(4).n * 4 + 4)
            wait(pe, self.y_free, t.n)
            for m in range(self.MC):
                q = t.mod(4)
                last = pe.matmul(self.ps_y[:, 0:D], self.h[4 * t.div(4).mod(2) + m][:, q * P:(q + 1) * P],
                                 g.sd_w[:, m * D:(m + 1) * D], start=(m == 0), stop=(m == self.MC - 1))
            last.then_inc(self.y_mm, 1)

    def silu(self, act, c):
        if c.within(self.units):
            p = c.mod(2)
            act.wait_ge(self.g_mm, c.n + 1)
            wait(act, self.h_done, c.shift(-1).n)
            act.activation(self.sg[p][:, :], self.ps_g[:, :], ACT.Silu).then_inc(self.sg_done, 1)

    def scalar(self, act, c):
        self.silu(act, c)
        if c.within(self.units):
            p = c.mod(2)
            act.wait_ge(self.u_mm, c.n + 1)
            act.activation(self.up[p][:, :], self.ps_u[:, :], ACT.Copy).then_inc(self.up_done, 1)
        if (t := self.behind(c)) is not None:
            p = t.mod(2)
            act.wait_ge(self.y_mm, t.n + 1)
            wait(act, self.xs_done, t.shift(-1).n)
            act.activation(self.ysb[p][:, :], self.ps_y[:, 0:D], ACT.Copy).then_inc(self.y_out, 1)

    def gpsimd(self, pool, c):
        if c.within(self.units):
            p = c.mod(2)
            wait(pool, self.y_mm, (c.div(4).n - 1) * 4)
            pool.wait_ge(self.sg_done, c.n + 1)
            pool.wait_ge(self.up_done, c.n + 1)
            pool.tensor_tensor(self.h[c.mod(8)][:, :], self.sg[p][:, :], self.up[p][:, :], ALU.mult)\
                .then_inc(self.h_done, 1)
        if (t := self.behind(c)) is not None:
            p = t.mod(2)
            pool.wait_ge(self.y_out, t.n + 1)
            pool.wait_ge(self.s_x3[p], (t.div(2).n + 1) * 16)
            wait(pool, self.xs_st[p], t.div(2).n * 16)
            pool.tensor_tensor(self.xs[p][:, :], self.x3[p][:, :], self.ysb[p][:, :], ALU.add).then_inc(self.xs_done, 1)

    def vector(self, dve, c, kept):
        if c.within(self.units):
            wait(dve, self.y_mm, (c.div(4).n - 1) * 4)
            dve.wait_ge(self.sg_done, c.n + 1)
            dve.wait_ge(self.u_mm, c.n + 1)
            dve.tensor_tensor(self.h[c.mod(8)][:, :], self.ps_u[:, :], self.sg[c.mod(2)][:, :], ALU.mult)\
                .then_inc(self.h_done, 1)
        if (t := self.behind(c)) is not None:
            p = t.mod(2)
            dve.wait_ge(self.y_mm, t.n + 1)
            dve.wait_ge(self.s_x3[p], (t.div(2).n + 1) * 16)
            dve.tensor_tensor(kept[:, bass.ds(t.n * D, D)], self.ps_y[:, 0:D], self.x3[p][:, :], ALU.add)\
                .then_inc(self.xs_done, 1)

    def load(self, eng, c):
        if (t := self.behind(c)) is not None:
            p = t.mod(2)
            wait(eng, self.xs_done, t.shift(-1).n)
            eng.dma_start(self.x3[p][:, :], self.g.x3[bass.ds((t.n + self.t0) * P, P), :]).then_inc(self.s_x3[p], 16)

    def sync(self, sp, c):
        g = self.g
        self.load(sp, c)
        if (t := self.behind(c)) is not None:
            p = t.mod(2)
            sp.wait_ge(self.xs_done, t.n + 1)
            sp.dma_start(g.xs[bass.ds((t.n + self.t0) * P, P), :], self.xs[p][:, :]).then_inc(self.xs_st[p], 16)

    def landed(self, sp):
        for p in range(2):
            sp.wait_ge(self.xs_st[p], self.units // 2 * 16)


def route1_phase(nc, g):
    ctx = ExitStack()
    with ctx:
        sem = semaphores(nc, ctx, "r1_")
        r = Router(nc, ctx, sem, g, "r1", E1, K1, NS1, (g.pair[0], g.pair[1], g.bank[4]))
        s_w = sem("w")
        sh = SharedExpert(nc, ctx, sem, g, "sh", 0, SHARED_FIRST, g.bank[5:8], False)
        block = ctx.enter_context(nc.Block())
        top = g.top_v[:, :].rearrange("p (t k) -> p t k", k=8)[:, :, 0:K1]
        w = g.weight[:, 0:NT * K1].rearrange("p (t k) -> p t k", k=K1)
        U, TAB = sh.units, 4
        PER = NT * K1 // (U - TAB)

        @block.sync
        def _(sp):
            for dst, src in ((g.sg_w, g.ins["sg"]), (g.su_w, g.ins["su"]), (g.sd_w, g.ins["sd"])):
                sp.dma_start(dst[:, :], src).then_inc(s_w, 16)
            few(U + sh.LAG, lambda c: sh.sync(sp, c))
            sh.landed(sp)

        @block.gpsimd
        def _(pool):
            few(U + sh.LAG, lambda c: sh.gpsimd(pool, c))

        @block.scalar
        def _(act):
            few(U + sh.LAG, lambda c: sh.scalar(act, c))

        @block.vector
        def _(dve):
            def weights(dve, link):
                link(dve.tensor_reduce(r.wsum[:, :], top, AX.X, ALU.add))
                link(dve.tensor_scalar(r.wsum[:, :], r.wsum[:, :], 1e-12, None, ALU.max))
                link(dve.reciprocal(r.wrec[:, :], r.wsum[:, :]))
                link(dve.tensor_tensor(w, top, r.wrec[:, :].unsqueeze(2).broadcast_to([P, NT, K1]), ALU.mult))

            r.vector(dve, weights)

        @block.tensor
        def _(pe):
            pe.wait_ge(s_w, 48)
            r.tensor_counts(pe)
            r.tensor_table_open(pe)

            def unit(c):
                sh.tensor(pe, c)
                if TAB <= c.off < U:
                    for i in range(PER):
                        r.tensor_table(pe, c.shift(-TAB).times(PER).shift(i))

            few(U + sh.LAG, unit)
            r.tensor_table_close(pe)


def moe1_phase(nc, g):
    ctx = ExitStack()
    with ctx:
        def sb(name, shape, dt=F32):
            return ctx.enter_context(nc.sbuf_tensor("m1_" + name, shape, dt))

        sem = semaphores(nc, ctx, "m1_")

        NJ = NS1 // 2
        idx = [[sb(f"idx{i}{k}", [P, 1], I32) for k in range(2)] for i in range(GB)]
        xg = [sb(f"xg{i}", [P, 2 * D]) for i in range(GB)]
        xT = [sb(f"xT{i}", [P, 2 * D]) for i in range(2)]
        sg = [sb(f"sg{i}", [P, 2 * M1]) for i in range(2)]
        h = [sb(f"h{i}", [P, 2 * M1]) for i in range(2)]
        hT = [sb(f"hT{i}", [P, 2 * P]) for i in range(2)]
        y = [sb(f"y{i}", [P, 2 * D]) for i in range(2)]
        passed, s_dn = sem("passed_pool"), sem("s_dn")
        s_g = [sem(f"s_g{i}") for i in range(GB)]
        y_st = [sem(f"y_st{i}") for i in range(2)]
        idx_ready, x_t, x_out, gu_mm, silu_done, h_done, h_t, h_out, y_mm, y_out = (
            sem(n) for n in ("idx_ready", "x_t", "x_out", "gu_mm", "silu_done", "h_done", "h_t", "h_out", "y_mm",
                             "y_out"))
        ps_x, ps_gu, ps_ht, ps_y = g.bank[0:2], g.bank[2:4], g.bank[4:6], g.bank[6:8]
        block = ctx.enter_context(nc.Block())

        @block.gpsimd
        def _(pool):
            def gather(j):
                p = j.mod(GB)
                wait_alone(pool, x_t, j.shift(1 - GB).n, passed)
                for k in range(2):
                    pool.tensor_copy(idx[p][k][:, :], g.token[:, bass.ds(j.n * 2 + k, 1)]).then_inc(idx_ready, 1)
                wait_alone(pool, idx_ready, j.n * 2 + 2, passed)
                for k in range(2):
                    pool.indirect_dma_start(out=xg[p][:, k * D:(k + 1) * D], out_offset=None, in_=g.xn4,
                                            in_offset=bass.IndirectOffsetOnAxis(ap=idx[p][k][:, :], axis=0))\
                        .then_inc(s_g[p], 16)

            steps(pool, GB, NJ, NJ, GB, gather)

        @block.sync
        def _(sp):
            sp.dma_start(g.dn[:, :], g.ins["dn"]).then_inc(s_dn, 16)

            def store(j):
                p = j.mod(2)
                sp.wait_ge(y_out, j.n + 1)
                sp.dma_start(g.y1[bass.ds(j.n * 2 * P, 2 * P), :].rearrange("(a p) n -> p a n", p=P),
                             y[p][:, :].rearrange("p (a n) -> p a n", a=2)).then_inc(y_st[p], 16)

            steps(sp, 2, NJ, NJ, 2, store)
            for p in range(2):
                sp.wait_ge(y_st[p], NJ // 2 * 16)

        def halves(ap):
            return ap.rearrange("p (a x n) -> p a x n", a=2, x=2)

        @block.scalar
        def _(act):
            def step(s):
                j = s
                if j.within(NJ):
                    p = j.mod(2)
                    act.wait_ge(x_t, j.n + 1)
                    wait(act, gu_mm, j.shift(-1).n)
                    act.activation(xT[p][:, :], ps_x[p][:, :], ACT.Copy).then_inc(x_out, 1)
                j = s.shift(-1)
                if j.within(NJ):
                    p = j.mod(2)
                    act.wait_ge(gu_mm, j.n + 1)
                    wait(act, h_done, j.shift(-1).n)
                    act.activation(sg[p][:, :].rearrange("p (a n) -> p a n", a=2), halves(ps_gu[p])[:, :, 0, :],
                                   ACT.Silu).then_inc(silu_done, 1)
                j = s.shift(-2)
                if j.within(NJ):
                    p = j.mod(2)
                    act.wait_ge(h_t, j.n + 1)
                    wait(act, y_mm, j.shift(-1).n)
                    act.activation(hT[p][:, :], ps_ht[p][:, 0:2 * P], ACT.Copy).then_inc(h_out, 1)

            steps(act, 4, NJ, NJ + 2, 2, step)

        @block.vector
        def _(dve):
            def step(s):
                j = s.shift(-1)
                if j.within(NJ):
                    p = j.mod(2)
                    dve.wait_ge(silu_done, j.n + 1)
                    wait(dve, h_t, j.shift(-1).n)
                    dve.tensor_tensor(h[p][:, :].rearrange("p (a n) -> p a n", a=2), halves(ps_gu[p])[:, :, 1, :],
                                      sg[p][:, :].rearrange("p (a n) -> p a n", a=2), ALU.mult).then_inc(h_done, 1)
                j = s.shift(-3)
                if j.within(NJ):
                    p = j.mod(2)
                    dve.wait_ge(y_mm, j.n + 1)
                    wait(dve, y_st[p], j.div(2).n * 16)
                    dve.tensor_copy(y[p][:, :], ps_y[p][:, :]).then_inc(y_out, 1)

            steps(dve, 6, NJ, NJ + 3, 2, step)

        @block.tensor
        def _(pe):
            e = [[pe.alloc_register(f"m1_e{i}{k}") for k in range(2)] for i in range(GB)]

            def step(s):
                j = s.shift(-1)
                if j.within(NJ):
                    for k in range(2):
                        pe.reg_load(e[j.mod(GB)][k], g.expert[0:1, bass.ds(j.n * 2 + k, 1)])
                j = s
                if j.within(NJ):
                    p, q = j.mod(2), j.mod(GB)
                    pe.wait_ge(s_g[q], (j.div(GB).n + 1) * 32)
                    wait(pe, x_out, j.shift(-1).n)
                    for c in range(2 * DC):
                        last = pe.transpose(ps_x[p][:, c * P:(c + 1) * P], xg[q][:, c * P:(c + 1) * P], g.ident[:, :])
                    last.then_inc(x_t, 1)
                j = s.shift(-1)
                if j.within(NJ):
                    p = j.mod(2)
                    ex = [pe.snap(e[j.mod(GB)][k], min_val=0, max_val=E1 - 1) for k in range(2)]
                    pe.wait_ge(x_out, j.n + 1)
                    wait(pe, h_done, j.shift(-1).n)
                    for k in range(2):
                        for c in range(DC):
                            at = (k * DC + c) * P
                            last = pe.matmul(ps_gu[p][:, k * 2 * M1:(k + 1) * 2 * M1], xT[p][:, at:at + P],
                                             g.gu[:, bass.ds(ex[k] * (DC * 2 * M1) + c * 2 * M1, 2 * M1)],
                                             start=(c == 0), stop=(c == DC - 1))
                    last.then_inc(gu_mm, 1)
                j = s.shift(-2)
                if j.within(NJ):
                    p = j.mod(2)
                    pe.wait_ge(h_done, j.n + 1)
                    wait(pe, h_out, j.shift(-1).n)
                    for k in range(2):
                        last = pe.transpose(ps_ht[p][:, k * P:(k + 1) * P], h[p][:, k * M1:(k + 1) * M1], g.ident[:, :])
                    last.then_inc(h_t, 1)
                j = s.shift(-3)
                if j.within(NJ):
                    p = j.mod(2)
                    if j.loop is None and j.off == 0:
                        pe.wait_ge(s_dn, 16)
                    ex = [pe.snap(e[j.mod(GB)][k], min_val=0, max_val=E1 - 1) for k in range(2)]
                    pe.wait_ge(h_out, j.n + 1)
                    wait(pe, y_out, j.shift(-1).n)
                    for k in range(2):
                        last = pe.matmul(ps_y[p][:, k * D:(k + 1) * D], hT[p][:, k * P:(k + 1) * P],
                                         g.dn[:, bass.ds(ex[k] * D, D)], start=True, stop=True)
                    last.then_inc(y_mm, 1)

            steps(pe, 8, NJ, NJ + 3, GB, step)


def sum_phase(nc, g):
    ctx = ExitStack()
    with ctx:
        def sb(name, shape, dt=F32):
            return ctx.enter_context(nc.sbuf_tensor("su_" + name, shape, dt))

        sem = semaphores(nc, ctx, "su_")

        STORED = SHARED_FIRST * 512 // P
        idx = [sb(f"idx{i}", [P, K1], I32) for i in range(GB)]
        yg = [[sb(f"yg{i}{k}", [P, D]) for k in range(K1)] for i in range(GB)]
        xs = [sb(f"xs{i}", [P, D]) for i in range(2)]
        kept = sb("kept", [P, (NT - STORED) * D])
        acc = [[sb(f"acc{i}{k}", [P, D]) for k in range(K1)] for i in range(2)]
        passed = sem("passed_pool")
        s_g = [sem(f"s_g{i}") for i in range(GB)]
        s_xs, st = ([sem(f"{n}{i}") for i in range(2)] for n in ("s_xs", "st"))
        idx_ready, part, done = sem("idx_ready"), sem("part"), sem("done")
        sh = SharedExpert(nc, ctx, sem, g, "sh2", SHARED_FIRST, NTOK // 512 - SHARED_FIRST, g.bank[5:8], True)
        UNITS = sh.units + sh.LAG
        block = ctx.enter_context(nc.Block())

        @block.gpsimd
        def _(pool):
            def gather(t):
                p = t.mod(GB)
                wait_alone(pool, done, t.shift(1 - GB).n, passed)
                pool.tensor_copy(idx[p][:, :], g.slot[:, bass.ds(t.n * K1, K1)]).then_inc(idx_ready, 1)
                wait_alone(pool, idx_ready, t.n + 1, passed)
                for k in range(K1):
                    pool.indirect_dma_start(out=yg[p][k][:, :], out_offset=None, in_=g.y1,
                                            in_offset=bass.IndirectOffsetOnAxis(ap=idx[p][:, k:k + 1], axis=0))\
                        .then_inc(s_g[p], 16)

            steps(pool, GB, NT, NT, GB, gather)

        @block.sync
        def _(sp):
            def load(t):
                wait(sp, done, t.shift(-1).n)
                sp.dma_start(xs[t.mod(2)][:, :], g.xs[bass.ds(t.n * P, P), :]).then_inc(s_xs[t.mod(2)], 16)

            def store(t):
                sp.wait_ge(done, t.n + 1)
                sp.dma_start(g.out[bass.ds(t.n * P, P), :], acc[t.mod(2)][K1 - 1][:, :]).then_inc(st[t.mod(2)], 16)

            def tile(s):
                load(s)
                t = s.shift(-1)
                if t.within(NT):
                    store(t)

            steps(sp, 2, STORED, STORED, 2, tile)
            steps(sp, 1, NT - STORED + 1, NT - STORED + 1, 2, lambda s: store(s.shift(STORED - 1)))
            for p in range(2):
                sp.wait_ge(st[p], NT // 2 * 16)

        @block.vector
        def _(dve):
            def tile(t):
                if t.loop is None and t.off < UNITS:
                    sh.vector(dve, t, kept)
                p = t.mod(2)
                if t.loop is None and t.off < STORED:
                    dve.wait_ge(s_xs[p], (t.div(2).n + 1) * 16)
                    residual = xs[p][:, :]
                else:
                    dve.wait_ge(sh.xs_done, t.shift(1 - STORED).n)
                    residual = kept[:, bass.ds(t.shift(-STORED).n * D, D)]
                dve.wait_ge(s_g[t.mod(GB)], (t.div(GB).n + 1) * 16 * K1)
                wait(dve, st[p], t.div(2).n * 16)
                for k in range(K1):
                    if k:
                        dve.wait_ge(part, t.n * (K1 - 1) + k)
                    dve.scalar_tensor_tensor(acc[p][k][:, :], yg[t.mod(GB)][k][:, :],
                                             g.weight[:, bass.ds(t.n * K1 + k, 1)],
                                             acc[p][k - 1][:, :] if k else residual, ALU.mult, ALU.add)\
                        .then_inc(part if k < K1 - 1 else done, 1)

            steps(dve, (UNITS + GB - 1) // GB * GB, NT, NT, GB, tile)

        @block.scalar
        def _(act):
            def unit(c):
                sh.load(act, c)
                sh.silu(act, c)

            few(UNITS, unit)

        @block.tensor
        def _(pe):
            few(UNITS, lambda c: sh.tensor(pe, c))


class Core:

    def __init__(self, ins, scratch, out):
        self.ins, self.out = ins, out
        self.x1, self.x2, self.x3, self.xs = (scratch[n] for n in ("x1", "x2", "x3", "xs"))
        self.xn, self.xn4, self.y0, self.y1 = (scratch[n] for n in ("xn", "xn4", "y0", "y1"))


def program(nc, dram_in, out, scratch):
    g = Core(dram_in, scratch, out)
    ctx = ExitStack()
    with ctx:
        def sb(name, shape, dt=F32):
            return ctx.enter_context(nc.sbuf_tensor(name, shape, dt))

        g.ident = sb("ident", [P, P])
        g.ones = sb("ones", [P, P])
        g.minus_half = sb("minus_half", [P, H])
        g.top_v = sb("top_v", [P, NT * 8])
        g.top_i = sb("top_i", [P, NT * 8], U32)
        g.tri = sb("tri", [P, P])
        g.iota = sb("iota", [P, NS1])
        g.iota16 = sb("iota16", [P, NS1], F16)
        g.not_first = sb("not_first", [P, E1 * NT])
        g.tokval = sb("tokval", [P, NT])
        g.slot = sb("slot", [P, NT * K1], I32)
        g.token = sb("token", [P, NS1], I32)
        g.expert = sb("expert", [1, NS1], I32)
        g.weight = sb("weight", [P, NT * K1])
        g.psum = ctx.enter_context(nc.psum_tensor("psum", [P, 8, 512], F32))
        g.bank = [g.psum[:, i, :] for i in range(8)]
        g.pair = [g.psum[:, 2 * i:2 * i + 2, :] for i in range(4)]
        with ExitStack() as l0:
            g.w13 = l0.enter_context(nc.sbuf_tensor("w13", [P, E0 * DC * 2 * M0], F32))
            with ExitStack() as attn:
                g.kT_all = attn.enter_context(nc.sbuf_tensor("kT_all", [P, NB * NG * LK], F32))
                g.v_all = attn.enter_context(nc.sbuf_tensor("v_all", [P, NB * H * (DH + 1)], F32))
                g.qT_all = attn.enter_context(nc.sbuf_tensor("qT_all", [P, NT * D], F32))
                qkv_phase(nc, g)
                attention0_phase(nc, g)
            g.w2 = l0.enter_context(nc.sbuf_tensor("w2", [P, E0 * M0 // P * D], F32))
            route0_phase(nc, g)
            moe0_phase(nc, g)
        with ExitStack() as l1:
            def sb1(name, n):
                return l1.enter_context(nc.sbuf_tensor(name, [P, n], F32))

            g.xn4T = sb1("xn4T", DC * NTOK)
            g.sg_w, g.su_w, g.sd_w = sb1("sg_w", DC * MS), sb1("su_w", DC * MS), sb1("sd_w", MS // P * D)
            with ExitStack() as routed:
                g.gu = routed.enter_context(nc.sbuf_tensor("gu", [P, E1 * DC * 2 * M1], F32))
                attention1_phase(nc, g)
                route1_phase(nc, g)
                g.dn = routed.enter_context(nc.sbuf_tensor("dn", [P, E1 * D], F32))
                moe1_phase(nc, g)
            sum_phase(nc, g)


def kernel(**inputs):
    import concourse.bacc as bacc
    from concourse.bass_utils import run_bass_kernel_spmd

    a = {k: np.asarray(v) for k, v in inputs.items()}

    def cols(w):
        return w.T.reshape(-1, P, w.shape[0]).transpose(1, 0, 2).reshape(P, -1)

    def row(b, n=P):
        return np.broadcast_to(b, (n, b.shape[0]))

    f = np.float32
    eye = np.eye(P, dtype=f)
    arrays = {
        "x": a["x"].reshape(NTOK, D),
        "ctx": a["ctx_1024"].reshape(NB, LK, DC, P).transpose(3, 2, 0, 1).reshape(P, DC * NB * LK),
        "wq": cols(a["L0_xattn_Wq"]),
        "wk": cols(a["L0_xattn_Wk"]),
        "wv": cols(a["L0_xattn_Wv"]),
        "bv": row(np.tile(a["L0_xattn_bv"], 2)),
        "wp": cols(a["L0_xattn_Wp"]),
        "bp": row(a["L0_xattn_bp"]),
        "gb": np.stack([np.tile(a["L0_xattn_" + n], HG) for n in ("q_gamma", "q_beta", "k_gamma", "k_beta")], 1),
        "bkq": np.concatenate([a["L0_xattn_bk"], a["L0_xattn_bq"]])[None, :],
        "wr0": cols(a["L0_ffn_moe_router"].T),
        "ident": eye,
        "tri": np.triu(np.ones((P, P), f), 1),
        "iota": np.broadcast_to(np.arange(NS1, dtype=f), (P, NS1)),
        "iota16": np.broadcast_to(np.arange(NS1, dtype=np.float16), (P, NS1)),
        "not_first": np.broadcast_to((np.arange(E1 * NT) % NT > 0).astype(f), (P, E1 * NT)),
        "tokval": np.arange(NT, dtype=f)[None, :] * P + np.arange(P, dtype=f)[:, None] - MID,
        "w13": a["L0_ffn_moe_w13"].reshape(E0, DC, P, 2 * M0).transpose(2, 0, 1, 3).reshape(P, -1),
        "wq1": cols(a["L1_xattn_Wq"]),
        "wk1": cols(a["L1_xattn_Wk"]),
        "wv1": cols(a["L1_xattn_Wv"]),
        "wo1": cols(a["L1_xattn_Wo"]),
        "wr1": cols(a["L1_ffn_router_w"]),
        "bq1": a["L1_xattn_bq"].reshape(DC, P).T,
        "bk1": a["L1_xattn_bk"].reshape(DC, P).T,
        "bv1": row(a["L1_xattn_bv"]),
        "bo1": row(a["L1_xattn_bo"], 1),
        "rb1": row(a["L1_ffn_router_bias"]),
        "gu": np.stack([a["L1_ffn_gate_w"], a["L1_ffn_up_w"]]).reshape(2, E1, M1, DC, P)
        .transpose(4, 1, 3, 0, 2).reshape(P, -1),
        "dn": a["L1_ffn_down_w"].transpose(2, 0, 1).reshape(P, -1),
        "sg": cols(a["L1_ffn_sgate_w"]),
        "su": cols(a["L1_ffn_sup_w"]),
        "sd": cols(a["L1_ffn_sdown_w"]),
        "w2": a["L0_ffn_moe_w2"].reshape(E0, M0 // P, P, D).transpose(2, 0, 1, 3).reshape(P, -1),
        "hmask": np.repeat(np.eye(HG, dtype=f), DH, axis=0),
    }
    arrays = {k: np.ascontiguousarray(v) for k, v in arrays.items()}
    nc = bacc.Bacc("TRN2", target_bir_lowering=False, num_devices=1)
    dram_in = {n: nc.dram_tensor("in_" + n, v.shape, mybir.dt.from_np(v.dtype), kind="ExternalInput").ap()
               for n, v in arrays.items()}
    out = nc.dram_tensor("out", (NTOK, D), F32, kind="ExternalOutput").ap()
    scratch = {n: nc.dram_tensor("t_" + n, s, F32, kind="Internal").ap() for n, s in (
        ("x1", (NTOK, D)), ("xn", (NTOK, D)), ("y0", (NS0 * P, D)), ("y1", (NS1 * P, D)), ("x2", (NTOK, D)), ("x3", (NTOK, D)), ("xn4", (NTOK, D)), ("xs", (NTOK, D)))}
    program(nc, dram_in, out, scratch)
    res = run_bass_kernel_spmd(nc, [{"in_" + n: v for n, v in arrays.items()}], core_ids=[0])
    return res.results[0]["out"].reshape(NB, SQ, D)
```

```python
import numpy as np
from contextlib import ExitStack

import concourse.bass as bass
from concourse import mybir

F32 = mybir.dt.float32
F32R = mybir.dt.float32r
F16 = mybir.dt.float16
BF16 = mybir.dt.bfloat16
I32 = mybir.dt.int32
U32 = mybir.dt.uint32
ALU = mybir.AluOpType
ACT = mybir.ActivationFunctionType
AX = mybir.AxisListType

P = 128
D = 256
DC = D // P
NB, SQ, LK = 16, 256, 77
NTOK = NB * SQ
NT = NTOK // P
H, DH = 16, 16
HG = 8
NG = H // HG
EPS = 1e-5
E0, K0, M0 = 8, 2, 512
E1, K1, M1 = 32, 4, 128
MS = 512
NS0 = NTOK * K0 // P + E0
NS1 = NTOK * K1 // P + E1
MID = NTOK // 2
SHARED_FIRST = 3
GB = 4


class At:

    def __init__(self, loop, mul, off):
        self.loop, self.mul, self.off = loop, mul, off

    @property
    def n(self):
        return self.off if self.loop is None else self.loop * self.mul + self.off

    def shift(self, d):
        return At(self.loop, self.mul, self.off + d)

    def times(self, k):
        return At(self.loop, self.mul * k, self.off * k)

    def div(self, k):
        return At(self.loop, self.mul // k, self.off // k)

    def mod(self, k):
        return self.off % k

    def within(self, count):
        return self.loop is not None or 0 <= self.off < count


def steps(eng, first, last, total, body, step):
    for s in range(first):
        step(At(None, 0, s))
    with eng.Fori(0, (last - first) // body) as i:
        for u in range(body):
            step(At(i, body, first + u))
    for s in range(last, total):
        step(At(None, 0, s))


def few(total, step):
    for s in range(total):
        step(At(None, 0, s))


def wait(eng, sem, count):
    if isinstance(count, int) and count <= 0:
        return
    eng.wait_ge(sem, count)


def semaphores(nc, ctx, prefix):
    taken = []

    def clear():
        nc.clear_and_free_semaphores(taken)
        nc.all_engine_barrier()

    def sem(name):
        taken.append(nc.alloc_semaphore(prefix + name))
        return taken[-1]

    ctx.callback(clear)
    return sem


def wait_alone(eng, sem, count, s_passed):
    if isinstance(count, int) and count <= 0:
        return
    eng.wait_ge(sem, count)
    eng.sem_inc(s_passed, 1)


def inverse_root(pool, out, var, minus_half, s_eps, s_rstd, t):
    pool.tensor_scalar(out, var, EPS, None, ALU.add).then_inc(s_eps, 1)
    pool.wait_ge(s_eps, t.n + 1)
    pool.tensor_tensor(out, out, minus_half, ALU.pow).then_inc(s_rstd, 1)


class LayerNorm:

    def __init__(self, sb, sem, name, s_passed, minus_half):
        self.minus_half, self.s_eps = minus_half, sem(f"{name}_eps")
        self.stats = [sb(f"{name}_stats{i}", [P, 6]) for i in range(2)]
        self.mv = [sb(f"{name}_mv{i}", [P, 2]) for i in range(2)]
        self.rstd = [sb(f"{name}_rstd{i}", [P, 1]) for i in range(2)]
        self.s_stats, self.s_mv, self.s_rstd = (sem(f"{name}_{n}") for n in ("stats", "mv", "rstd"))
        self.s_passed = s_passed

    def moments(self, dve, x, t):
        self.halves(dve, x, t)
        self.join(dve, t)

    def halves(self, dve, x, t):
        dve.bn_stats(self.stats[t.mod(2)][:, :], x).then_inc(self.s_stats, 1)

    def join(self, dve, t):
        p = t.mod(2)
        wait_alone(dve, self.s_stats, t.n + 1, self.s_passed[0])
        dve.bn_aggr(self.mv[p][:, :], self.stats[p][:, :]).then_inc(self.s_mv, 1)

    def invert(self, pool, t):
        p = t.mod(2)
        wait_alone(pool, self.s_mv, t.n + 1, self.s_passed[1])
        inverse_root(pool, self.rstd[p][:, :], self.mv[p][:, 1:2], self.minus_half[:, 0:1], self.s_eps, self.s_rstd, t)

    def apply(self, dve, x, out, t):
        p = t.mod(2)
        dve.wait_ge(self.s_rstd, t.n + 1)
        return dve.tensor_scalar(out, x, self.mv[p][:, 0:1], self.rstd[p][:, :], ALU.subtract, ALU.mult)


def heads_of(ap):
    return ap.rearrange("p (h d) -> p h d", d=DH)


class HeadNorm:

    def __init__(self, sb, sem, g, name, rows, w, bias, gamma, beta, eps, ps_p, ps_t):
        self.g, self.rows, self.w, self.bias, self.gamma, self.beta = g, rows, w, bias, gamma, beta
        self.eps, self.ps_p, self.ps_t = eps, ps_p, ps_t
        self.sq, self.n = ([sb(f"{name}_{n}{i}", [P, 2 * D]) for i in range(2)] for n in ("sq", "n"))
        self.var, self.sd, self.rstd = (
            [sb(f"{name}_{n}{i}", [P, 2 * H]) for i in range(2)] for n in ("var", "sd", "rstd"))
        self.s_proj, self.s_sq, self.s_var, self.s_sd, self.s_rstd, self.s_n, self.s_t, self.s_out = (
            sem(f"{name}_{n}") for n in ("proj", "sq", "var", "sd", "rstd", "n", "t", "out"))

    def project(self, pe, i, block):
        ps, r = self.ps_p[i.mod(4)], self.rows
        wait(pe, self.s_n, i.shift(-3).n)
        for a in range(2):
            pe.matmul(ps[0:r, a * D:(a + 1) * D], self.g.ones[0:1, 0:r], self.bias, start=True, stop=False)
            for c in range(DC):
                last = pe.matmul(ps[0:r, a * D:(a + 1) * D], block(a, c), self.w[:, c * D:(c + 1) * D],
                                 start=False, stop=(c == DC - 1))
        last.then_inc(self.s_proj, 1)

    def square(self, act, i):
        p, r = i.mod(2), self.rows
        act.wait_ge(self.s_proj, i.n + 1)
        wait(act, self.s_var, i.shift(-1).n)
        act.activation(self.sq[p][0:r, :], self.ps_p[i.mod(4)][0:r, :], ACT.Square, scale=DH ** -0.5).then_inc(self.s_sq, 1)

    def variance(self, dve, i):
        p, r = i.mod(2), self.rows
        dve.wait_ge(self.s_sq, i.n + 1)
        wait(dve, self.s_sd, i.shift(-1).n)
        dve.tensor_reduce(self.var[p][0:r, :], heads_of(self.sq[p][0:r, :]), AX.X, ALU.add).then_inc(self.s_var, 1)

    def root(self, act, i):
        p, r = i.mod(2), self.rows
        act.wait_ge(self.s_var, i.n + 1)
        wait(act, self.s_rstd, i.shift(-1).n)
        act.activation(self.sd[p][0:r, :], self.var[p][0:r, :], ACT.Sqrt, bias=self.eps[0:r, 0:1])\
            .then_inc(self.s_sd, 1)

    def scale(self, dve, i):
        p, r = i.mod(2), self.rows
        dve.wait_ge(self.s_sd, i.n + 1)
        dve.reciprocal(self.rstd[p][0:r, :], self.sd[p][0:r, :]).then_inc(self.s_rstd, 1)
        dve.wait_ge(self.s_rstd, i.n + 1)
        wait(dve, self.s_t, i.shift(-1).n)
        dve.tensor_tensor(heads_of(self.n[p][0:r, :]), heads_of(self.ps_p[i.mod(4)][0:r, :]),
                          self.rstd[p][0:r, :].unsqueeze(2).broadcast_to([r, 2 * H, DH]), ALU.mult)\
            .then_inc(self.s_n, 1)

    def transpose(self, pe, i):
        p, r = i.mod(2), self.rows
        pe.wait_ge(self.s_n, i.n + 1)
        wait(pe, self.s_out, i.n)
        for c in range(2 * DC):
            last = pe.transpose(self.ps_t[:, c * r:(c + 1) * r], self.n[p][0:r, c * P:(c + 1) * P],
                                self.g.ident[0:r, 0:r])
        last.then_inc(self.s_t, 1)

    def affine(self, act, i, out, s_passed):
        n = 2 * DC * self.rows
        wait_alone(act, self.s_t, i.n + 1, s_passed)
        act.activation(out[:, bass.ds(i.n * n, n)], self.ps_t[:, 0:n], ACT.Identity,
                       bias=self.beta, scale=self.gamma).then_inc(self.s_out, 1)


def qkv_phase(nc, g):
    ctx = ExitStack()
    with ctx:
        def sb(name, shape, dt=F32):
            return ctx.enter_context(nc.sbuf_tensor("qkv_" + name, shape, dt))

        sem = semaphores(nc, ctx, "qkv_")

        NKP, NQP, VW = NB // 2, NT // 2, H * (DH + 1)
        wq, wk, wv = (sb(n, [P, DC * D]) for n in ("wq", "wk", "wv"))
        bias = sb("bias", [1, 2 * D])
        wmean, bmean = sb("wmean", [P, 2, DC * H]), sb("bmean", [1, 2 * H])
        gb, scaled, eps, bv = sb("gb", [P, 4]), sb("scaled", [P, 2]), sb("eps", [P, 1]), sb("bv", [P, 2 * D])
        ctxT = g.w13[:, 0:CONTEXT_COLS]
        x_in = [g.w13[:, CONTEXT_COLS + i * 2 * D:CONTEXT_COLS + (i + 1) * 2 * D] for i in range(4)]
        xn = [sb(f"xn{i}", [P, 2 * D]) for i in range(2)]
        xnT = [sb(f"xnT{i}", [P, 2 * D]) for i in range(2)]
        stats = [sb(f"stats{i}", [P, 12]) for i in range(2)]
        mv = [sb(f"mv{i}", [P, 4]) for i in range(2)]
        rstd = [sb(f"rstd{i}", [P, 2]) for i in range(2)]
        s_w, s_rest, s_ctx, s_wm, s_wc, s_gs, s_ones, s_v1, s_half = (sem(n) for n in (
            "s_w", "s_rest", "s_ctx", "s_wm", "s_wc", "s_gs", "s_ones", "s_v1", "s_half"))
        s_x = [sem(f"s_x{i}") for i in range(4)]
        v_mm, v_out, ln_stats, ln_mv, ln_eps, ln_rstd, x_norm, x_t, x_out = (sem(n) for n in (
            "v_mm", "v_out", "ln_stats", "ln_mv", "ln_eps", "ln_rstd", "x_norm", "x_t", "x_out"))
        passed = [sem(f"passed_{n}") for n in ("dve", "pool", "act")]
        ps_p, ps_t, ps_xt, ps_v = g.bank[0:4], g.bank[4], g.bank[5:7], g.bank[7]
        k = HeadNorm(sb, sem, g, "k", LK, wk, bias[0:1, 0:D], gb[:, 2:3], gb[:, 3:4], eps, ps_p, ps_t)
        q = HeadNorm(sb, sem, g, "q", P, wq, bias[0:1, D:2 * D], scaled[:, 0:1], scaled[:, 1:2], eps, ps_p, ps_t)
        block = ctx.enter_context(nc.Block())
        VAR, SCALE, OUT = 1, 2, 3
        XQ = NKP
        X, XT = XQ - 2, XQ - 1
        BODY, FIRST, TOTAL = 4, NKP + 4, XQ + NQP + OUT
        LAST = FIRST + (X + NQP - FIRST) // BODY * BODY

        def piece(s, skew):
            if s.loop is None and 0 <= s.off - skew < NKP:
                return k, s.shift(-skew)
            i = s.shift(-skew - XQ)
            return (q, i) if i.within(NQP) else None

        def pair(s, skew):
            i = s.shift(-skew)
            return i if i.within(NQP) else None

        @block.sync
        def _(sp):
            for dst, src in ((wk, g.ins["wk"]), (wq, g.ins["wq"]), (bias, g.ins["bkq"])):
                sp.dma_start(dst[:, :], src).then_inc(s_w, 16)
            for dst, src in ((gb, g.ins["gb"]), (wv, g.ins["wv"]), (bv, g.ins["bv"]), (g.ident, g.ins["ident"])):
                sp.dma_start(dst[:, :], src).then_inc(s_rest, 16)

            def load_x(s):
                wait(sp, x_norm, s.shift(-3).n)
                sp.dma_start(x_in[s.mod(4)][:, :].rearrange("p (a n) -> p a n", a=2),
                             g.ins["x"][bass.ds(s.n * 2 * P, 2 * P), :].rearrange("(a p) n -> p a n", p=P))\
                    .then_inc(s_x[s.mod(4)], 16)

            steps(sp, 4, NQP, NQP, 4, load_x)

        @block.gpsimd
        def _(pool):
            pool.memset(g.ones[:, :], 1.0).then_inc(s_ones, 1)
            pool.memset(eps[:, :], EPS).then_inc(s_half, 1)
            pool.memset(g.minus_half[:, :], -0.5).then_inc(s_half, 1)
            pool.wait_ge(s_half, 2)
            pool.memset(g.v_all[:, :], 1.0).then_inc(s_v1, 1)

            def invert(s):
                p = s.mod(2)
                wait_alone(pool, ln_mv, s.n + 1, passed[1])
                inverse_root(pool, rstd[p][:, :], mv[p][:, :].rearrange("p (a n) -> p a n", a=2)[:, :, 1],
                             g.minus_half[:, 0:2], ln_eps, ln_rstd, s)

            steps(pool, 2, NQP, NQP, 2, invert)

        @block.vector
        def _(dve):
            dve.wait_ge(s_w, 3 * 16)
            for j, (w, m) in enumerate(((wk[:, :], wmean[:, 0, :]), (bias[:, :], bmean[:, :]),
                                        (wq[:, :], wmean[:, 1, :]))):
                rows, heads = m.shape
                dve.tensor_reduce(m, heads_of(w), AX.X, ALU.add).then_inc(s_wm, 1)
                dve.wait_ge(s_wm, 2 * j + 1)
                dve.tensor_scalar(m, m, 1.0 / DH, None, ALU.mult).then_inc(s_wm, 1)
                dve.wait_ge(s_wm, 2 * j + 2)
                dve.tensor_tensor(heads_of(w), heads_of(w), m.unsqueeze(2).broadcast_to([rows, heads, DH]),
                                  ALU.subtract).then_inc(s_wc, 1)
            dve.wait_ge(s_rest, 4 * 16)
            dve.tensor_scalar(scaled[:, :], gb[:, 0:2], float(DH) ** -0.5, None, ALU.mult).then_inc(s_gs, 1)
            dve.wait_ge(s_v1, 1)

            def step(s):
                if (i := pair(s, XT)) is not None:
                    p = i.mod(2)
                    dve.wait_ge(ln_rstd, i.n + 1)
                    wait(dve, x_t, i.shift(-1).n)
                    for a in range(2):
                        last = dve.tensor_scalar(xn[p][:, a * D:(a + 1) * D], x_in[i.mod(4)][:, a * D:(a + 1) * D],
                                                 mv[p][:, 2 * a:2 * a + 1], rstd[p][:, a:a + 1],
                                                 ALU.subtract, ALU.mult)
                    last.then_inc(x_norm, 1)
                if (i := pair(s, X)) is not None:
                    p = i.mod(2)
                    dve.wait_ge(s_x[i.mod(4)], (i.div(4).n + 1) * 16)
                    for a in range(2):
                        last = dve.bn_stats(stats[p][:, 6 * a:6 * a + 6], x_in[i.mod(4)][:, a * D:(a + 1) * D])
                    last.then_inc(ln_stats, 1)
                    wait_alone(dve, ln_stats, i.n + 1, passed[0])
                    for a in range(2):
                        last = dve.bn_aggr(mv[p][:, 2 * a:2 * a + 2], stats[p][:, 6 * a:6 * a + 6])
                    last.then_inc(ln_mv, 1)
                if (at := piece(s, SCALE)) is not None:
                    at[0].scale(dve, at[1])
                if (at := piece(s, VAR)) is not None:
                    at[0].variance(dve, at[1])
                if s.loop is None and s.off < NKP:
                    i = s
                    dve.wait_ge(v_mm, i.n + 1)
                    dve.tensor_tensor(
                        g.v_all[0:LK, bass.ds(i.n * 2 * VW, 2 * VW)].rearrange("p (h d) -> p h d", d=DH + 1)[:, :, 0:DH],
                        heads_of(ps_v[0:LK, :]), heads_of(bv[0:LK, :]), ALU.add).then_inc(v_out, 1)

            steps(dve, FIRST, LAST, TOTAL, BODY, step)

        @block.scalar
        def _(act):
            act.dma_start(ctxT[:, :], g.ins["ctx"]).then_inc(s_ctx, 16)
            act.wait_ge(s_gs, 1)
            act.wait_ge(s_half, 2)

            def step(s):
                if (i := pair(s, XT)) is not None:
                    act.wait_ge(x_t, i.n + 1)
                    wait(act, q.s_proj, i.shift(-1).n)
                    act.activation(xnT[i.mod(2)][:, :], ps_xt[i.mod(2)][:, :], ACT.Copy).then_inc(x_out, 1)
                if (at := piece(s, VAR)) is not None:
                    at[0].root(act, at[1])
                if (at := piece(s, OUT)) is not None:
                    at[0].affine(act, at[1], g.kT_all if at[0] is k else g.qT_all, passed[2])
                if (at := piece(s, 0)) is not None:
                    at[0].square(act, at[1])

            steps(act, FIRST, LAST, TOTAL, BODY, step)

        @block.tensor
        def _(pe):
            pe.wait_ge(s_w, 3 * 16)
            pe.wait_ge(s_ctx, 16)
            pe.wait_ge(s_ones, 1)
            pe.wait_ge(s_wc, 3)
            pe.wait_ge(s_rest, 4 * 16)

            def step(s):
                if (i := pair(s, XT)) is not None:
                    p = i.mod(2)
                    pe.wait_ge(x_norm, i.n + 1)
                    wait(pe, x_out, i.shift(-1).n)
                    for c in range(2 * DC):
                        last = pe.transpose(ps_xt[p][:, c * P:(c + 1) * P], xn[p][:, c * P:(c + 1) * P], g.ident[:, :])
                    last.then_inc(x_t, 1)
                if (at := piece(s, 0)) is not None:
                    norm, i = at
                    if norm is k:
                        norm.project(pe, i, lambda a, c: ctxT[:, (c * NB + 2 * i.n + a) * LK:][:, 0:LK])
                        wait(pe, v_out, i.n)
                        for a in range(2):
                            for c in range(DC):
                                last = pe.matmul(ps_v[0:LK, a * D:(a + 1) * D],
                                                 ctxT[:, (c * NB + 2 * i.n + a) * LK:][:, 0:LK],
                                                 wv[:, c * D:(c + 1) * D], start=(c == 0), stop=(c == DC - 1))
                        last.then_inc(v_mm, 1)
                    else:
                        pe.wait_ge(x_out, i.n + 1)
                        if i.loop is None and i.off < 4:
                            pe.wait_ge(k.s_n, NKP - 3 + i.off)
                        norm.project(pe, i, lambda a, c: xnT[i.mod(2)][:, (a * DC + c) * P:(a * DC + c + 1) * P])
                if (at := piece(s, OUT)) is not None:
                    norm, i = at
                    if norm is q and i.loop is None and i.off == 0:
                        pe.wait_ge(k.s_out, NKP)
                    norm.transpose(pe, i)

            steps(pe, FIRST, LAST, TOTAL, BODY, step)


def top_of(dve, g, scores, top, ix, t, s_scores, s_top, s_ix, passed):
    wait_alone(dve, s_scores, t.n + 1, passed[0])
    dve.max(top[:, :], scores[:, :]).then_inc(s_top, 1)
    wait_alone(dve, s_top, t.n + 1, passed[0])
    dve.max_index(ix[:, :], top[:, :], scores[:, :]).then_inc(s_ix, 1)
    dve.tensor_copy(g.top_v[:, bass.ds(t.n * 8, 8)], top[:, :])
    wait_alone(dve, s_ix, t.n + 1, passed[0])
    dve.tensor_copy(g.top_i[:, bass.ds(t.n * 8, 8)], ix[:, :])


def attention0_phase(nc, g):
    ctx = ExitStack()
    with ctx:
        def sb(name, shape, dt=F32):
            return ctx.enter_context(nc.sbuf_tensor("at0_" + name, shape, dt))

        sem = semaphores(nc, ctx, "at0_")

        NU = NT * NG
        VW = H * (DH + 1)
        HW = HG * LK // 2
        wp = sb("wp", [P, DC * D])
        wr = sb("wr", [P, DC * E0])
        bp = sb("bp", [P, D])
        hmask = sb("hmask", [P, HG])
        q_s = [sb(f"q_s{i}", [P, D]) for i in range(2)]
        kblk = [sb(f"kblk{i}", [P, NG * HG * LK]) for i in range(2)]
        x_in = [sb(f"x_in{i}", [P, D]) for i in range(2)]
        xb = [sb(f"xb{i}", [P, D]) for i in range(2)]
        mx = [sb(f"mx{i}", [P, HG]) for i in range(2)]
        pr = [sb(f"pr{i}", [P, HG * LK]) for i in range(2)]
        prT = [sb(f"prT{i}", [P, HG * P]) for i in range(2)]
        rec = [sb(f"rec{i}", [P, H]) for i in range(2)]
        o = [sb(f"o{i}", [P, D]) for i in range(2)]
        oT = [sb(f"oT{i}", [P, D]) for i in range(2)]
        x1 = [sb(f"x1{i}", [P, D]) for i in range(2)]
        xn = [sb(f"xn{i}", [P, D]) for i in range(2)]
        xnT = [sb(f"xnT{i}", [P, D]) for i in range(2)]
        lg = [sb(f"lg{i}", [P, E0]) for i in range(2)]
        top = [sb(f"top{i}", [P, 8]) for i in range(2)]
        ix = [sb(f"ix{i}", [P, 8], U32) for i in range(2)]
        s_w, s_next = sem("s_w"), sem("s_next")
        s_x, x1_st, xn_st = ([sem(f"{n}{i}") for i in range(2)] for n in ("s_x", "x1_st", "xn_st"))
        k_ready, q_ready, xb_ready, s_mm, mx_ready, sub_done, exp_done, tp_mm, tp_out, pv_mm, rec_ready, o_norm = (
            sem(n) for n in ("k_ready", "q_ready", "xb_ready", "s_mm", "mx_ready", "sub_done", "exp_done", "tp_mm",
                             "tp_out", "pv_mm", "rec_ready", "o_norm"))
        o_t, o_out, wp_mm, x1_done, x_norm, x_t, x_out, r_mm, lg_done, m8_done, ix_done = (
            sem(n) for n in ("o_t", "o_out", "wp_mm", "x1_done", "x_norm", "x_t", "x_out", "r_mm", "lg_done",
                             "m8_done", "ix_done"))
        passed = [sem(f"passed_{n}") for n in ("dve", "pool", "act")]
        ln = LayerNorm(sb, sem, "ln", passed, g.minus_half)
        ps_s, ps_tp = g.pair[0], g.pair[1]
        ps_o, ps_ot, ps_wp, ps_x = g.bank[4:8]
        block = ctx.enter_context(nc.Block())
        T_O, T_WP, T_X, T_R = 5, 6, 8, 9
        FIRST, BODY, TOTAL = 16, 8, NU + T_R + 1
        LEAD = 2

        def tile_at(u, skew):
            s = u.shift(-skew)
            return s.div(2) if s.mod(2) == 0 and s.within(NU) else None

        @block.sync
        def _(sp):
            for dst, src in ((wp, g.ins["wp"]), (wr, g.ins["wr0"]), (bp, g.ins["bp"]), (hmask, g.ins["hmask"])):
                sp.dma_start(dst[:, :], src).then_inc(s_w, 16)
            for dst, src in ((g.tri, g.ins["tri"]), (g.iota, g.ins["iota"]), (g.iota16, g.ins["iota16"]),
                             (g.not_first, g.ins["not_first"][:, 0:E0 * NT]), (g.tokval, g.ins["tokval"])):
                sp.dma_start(dst[:, :], src).then_inc(s_next, 16)
            for dst, src in ((g.ctxT, g.ins["ctx"]), (g.wk1, g.ins["wk1"]), (g.wv1, g.ins["wv1"]),
                             (g.bk1, g.ins["bk1"]), (g.bv1, g.ins["bv1"])):
                sp.dma_start(dst[:, :], src).then_inc(s_next, 16)
            n = DC * 2 * M0
            for e in range(E0):
                sp.dma_start(g.w13[:, e * n:(e + 1) * n], g.ins["w13"][:, e * n:(e + 1) * n]).then_inc(s_next, 16)

            def tile(s):
                t = s
                if t.within(NT):
                    wait(sp, xb_ready, t.shift(-1).n)
                    sp.dma_start(x_in[t.mod(2)][:, :], g.ins["x"][bass.ds(t.n * P, P), :]).then_inc(s_x[t.mod(2)], 16)
                t = s.shift(-4)
                if t.within(NT):
                    p = t.mod(2)
                    sp.wait_ge(x1_done, t.n + 1)
                    sp.dma_start(g.x1[bass.ds(t.n * P, P), :], x1[p][:, :]).then_inc(x1_st[p], 16)
                    sp.wait_ge(x_norm, t.n + 1)
                    sp.dma_start(g.xn[bass.ds(t.n * P, P), :], xn[p][:, :]).then_inc(xn_st[p], 16)

            steps(sp, 6, NT, NT + 4, 2, tile)
            for p in range(2):
                sp.wait_ge(x1_st[p], NT // 2 * 16)
                sp.wait_ge(xn_st[p], NT // 2 * 16)
            sp.wait_ge(s_next, (10 + E0) * 16)

        @block.gpsimd
        def _(pool):
            pool.wait_ge(s_w, 64)

            def half(u):
                t = tile_at(u, 0)
                if t is not None:
                    p, b = t.mod(2), t.div(2)
                    if t.mod(2) == 0:
                        bp_ = b.mod(2)
                        wait_alone(pool, s_mm, b.shift(-1).n * 4, passed[1])
                        for gr in range(NG):
                            kT = g.kT_all[:, bass.ds(b.n * (NG * LK) + gr * LK, LK)]
                            pool.tensor_tensor(
                                kblk[bp_][:, gr * HG * LK:(gr + 1) * HG * LK].rearrange("p (h k) -> p h k", h=HG),
                                kT.unsqueeze(1).broadcast_to([P, HG, LK]),
                                hmask[:, :].unsqueeze(2).broadcast_to([P, HG, LK]), ALU.mult).then_inc(k_ready, 1)
                    wait_alone(pool, s_mm, t.shift(-1).n * 2, passed[1])
                    pool.tensor_copy(q_s[p][:, :], g.qT_all[:, bass.ds(t.n * D, D)]).then_inc(q_ready, 1)
                t = tile_at(u, 4 + LEAD)
                if t is not None:
                    p = t.mod(2)
                    pool.wait_ge(s_x[p], (t.div(2).n + 1) * 16)
                    wait(pool, x1_done, t.shift(-1).n)
                    pool.tensor_tensor(xb[p][:, :], x_in[p][:, :], bp[:, :], ALU.add).then_inc(xb_ready, 1)
                t = tile_at(u, T_WP + LEAD)
                if t is not None:
                    ln.invert(pool, t)

            steps(pool, FIRST, NU, TOTAL + LEAD, BODY, half)

        @block.vector
        def _(dve):
            def half(u):
                if u.within(NU):
                    p = u.mod(2)
                    s3 = ps_s[:, :, 0:HW].rearrange("p a (h k) -> p a h k", k=LK)
                    dve.wait_ge(s_mm, u.n + 1)
                    dve.tensor_reduce(mx[p][:, :].rearrange("p (a h) -> p a h", a=2), s3, AX.X, ALU.max)\
                        .then_inc(mx_ready, 1)
                    dve.wait_ge(mx_ready, u.n + 1)
                    wait(dve, tp_mm, u.shift(-1).n)
                    dve.tensor_tensor(
                        pr[p][:, :].rearrange("p (a h k) -> p a h k", a=2, k=LK), s3,
                        mx[p][:, :].rearrange("p (a h) -> p a h", a=2).unsqueeze(3).broadcast_to([P, 2, HG // 2, LK]),
                        ALU.subtract).then_inc(sub_done, 1)
                t = tile_at(u, 3)
                if t is not None:
                    p = t.mod(2)
                    ov = ps_o[:, 0:VW].rearrange("p (h d) -> p h d", h=H)
                    dve.wait_ge(pv_mm, t.n * 2 + 2)
                    dve.reciprocal(rec[p][:, :].unsqueeze(2), ov[:, :, DH:DH + 1]).then_inc(rec_ready, 1)
                    dve.wait_ge(rec_ready, t.n + 1)
                    wait(dve, o_t, t.shift(-1).n)
                    dve.tensor_tensor(heads_of(o[p][:, :]), ov[:, :, 0:DH],
                                      rec[p][:, :].unsqueeze(2).broadcast_to([P, H, DH]), ALU.mult).then_inc(o_norm, 1)
                t = tile_at(u, T_WP + 1)
                if t is not None:
                    p = t.mod(2)
                    wait(dve, xn_st[p], t.div(2).n * 16)
                    wait(dve, x_t, t.shift(-1).n)
                    ln.apply(dve, x1[p][:, :], xn[p][:, :], t).then_inc(x_norm, 1)
                t = tile_at(u, T_WP)
                if t is not None:
                    p = t.mod(2)
                    dve.wait_ge(wp_mm, t.n + 1)
                    dve.wait_ge(xb_ready, t.n + 1)
                    wait(dve, x1_st[p], t.div(2).n * 16)
                    dve.tensor_tensor(x1[p][:, :], ps_wp[:, 0:D], xb[p][:, :], ALU.add).then_inc(x1_done, 1)
                    dve.wait_ge(x1_done, t.n + 1)
                    ln.moments(dve, x1[p][:, :], t)
                t = tile_at(u, T_R)
                if t is not None:
                    p = t.mod(2)
                    dve.wait_ge(r_mm, t.n + 1)
                    dve.tensor_copy(lg[p][:, :], ps_x[:, D:D + E0]).then_inc(lg_done, 1)
                    top_of(dve, g, lg[p], top[p], ix[p], t, lg_done, m8_done, ix_done, passed)

            steps(dve, FIRST, NU, TOTAL, BODY, half)

        @block.scalar
        def _(act):
            def half(u):
                v = u.shift(-1)
                if v.within(NU):
                    p = v.mod(2)
                    act.wait_ge(tp_mm, v.n + 1)
                    wait(act, pv_mm, v.shift(-1).n)
                    act.activation(prT[p][0:LK, :].rearrange("p (a k) -> p a k", a=2), ps_tp[0:LK, :, :], ACT.Copy)\
                        .then_inc(tp_out, 1)
                if u.within(NU):
                    p = u.mod(2)
                    act.wait_ge(sub_done, u.n + 1)
                    act.activation(pr[p][:, :], pr[p][:, :], ACT.Exp).then_inc(exp_done, 1)
                t = tile_at(u, T_O)
                if t is not None:
                    p = t.mod(2)
                    act.wait_ge(o_t, t.n + 1)
                    wait(act, wp_mm, t.shift(-1).n)
                    act.activation(oT[p][:, :], ps_ot[:, 0:D], ACT.Copy).then_inc(o_out, 1)
                t = tile_at(u, T_X)
                if t is not None:
                    p = t.mod(2)
                    act.wait_ge(x_t, t.n + 1)
                    wait(act, r_mm, t.shift(-1).n)
                    act.activation(xnT[p][:, :], ps_x[:, 0:D], ACT.Copy).then_inc(x_out, 1)

            steps(act, FIRST, NU, TOTAL, BODY, half)

        @block.tensor
        def _(pe):
            pe.wait_ge(s_w, 64)

            def half(u):
                if u.within(NU):
                    gr, t = u.mod(2), u.div(2)
                    p, b = t.mod(2), t.div(2)
                    pe.wait_ge(k_ready, b.n * 2 + 2)
                    pe.wait_ge(q_ready, t.n + 1)
                    wait(pe, sub_done, u.n)
                    for a in range(2):
                        last = pe.matmul(ps_s[:, a, 0:HW], q_s[p][:, gr * P:(gr + 1) * P],
                                         kblk[b.mod(2)][:, (2 * gr + a) * HW:(2 * gr + a + 1) * HW],
                                         start=True, stop=True)
                    last.then_inc(s_mm, 1)
                v = u.shift(-1)
                if v.within(NU):
                    p = v.mod(2)
                    pe.wait_ge(exp_done, v.n + 1)
                    wait(pe, tp_out, v.n)
                    for h in range(HG):
                        last = pe.transpose(ps_tp[0:LK, h // 4, (h % 4) * P:(h % 4 + 1) * P],
                                            pr[p][:, h * LK:(h + 1) * LK], g.ident[:, :])
                    last.then_inc(tp_mm, 1)
                v = u.shift(-2)
                if v.within(NU):
                    p, gr, t = v.mod(2), v.mod(2), v.div(2)
                    b = t.div(2)
                    pe.wait_ge(tp_out, v.n + 1)
                    if gr == 0:
                        wait(pe, o_norm, t.n)
                    for h in range(HG):
                        c = (gr * HG + h) * (DH + 1)
                        last = pe.matmul(ps_o[:, c:c + DH + 1], prT[p][0:LK, h * P:(h + 1) * P],
                                         g.v_all[0:LK, bass.ds(b.n * VW + c, DH + 1)], start=True, stop=True)
                    last.then_inc(pv_mm, 1)
                t = tile_at(u, T_O)
                if t is not None:
                    p = t.mod(2)
                    pe.wait_ge(o_norm, t.n + 1)
                    wait(pe, o_out, t.n)
                    for c in range(DC):
                        last = pe.transpose(ps_ot[:, c * P:(c + 1) * P], o[p][:, c * P:(c + 1) * P], g.ident[:, :])
                    last.then_inc(o_t, 1)
                t = tile_at(u, T_WP)
                if t is not None:
                    p = t.mod(2)
                    pe.wait_ge(o_out, t.n + 1)
                    wait(pe, x1_done, t.n)
                    for c in range(DC):
                        last = pe.matmul(ps_wp[:, 0:D], oT[p][:, c * P:(c + 1) * P], wp[:, c * D:(c + 1) * D],
                                         start=(c == 0), stop=(c == DC - 1))
                    last.then_inc(wp_mm, 1)
                t = tile_at(u, T_R)
                if t is not None:
                    p = t.mod(2)
                    pe.wait_ge(x_out, t.n + 1)
                    for c in range(DC):
                        last = pe.matmul(ps_x[:, D:D + E0], xnT[p][:, c * P:(c + 1) * P], wr[:, c * E0:(c + 1) * E0],
                                         start=(c == 0), stop=(c == DC - 1))
                    last.then_inc(r_mm, 1)
                t = tile_at(u, T_X)
                if t is not None:
                    p = t.mod(2)
                    pe.wait_ge(x_norm, t.n + 1)
                    wait(pe, x_out, t.n)
                    wait(pe, lg_done, t.n)
                    for c in range(DC):
                        last = pe.transpose(ps_x[:, c * P:(c + 1) * P], xn[p][:, c * P:(c + 1) * P], g.ident[:, :])
                    last.then_inc(x_t, 1)

            steps(pe, FIRST, NU, TOTAL, BODY, half)


class Router:

    def __init__(self, nc, ctx, sem, g, name, n_exp, k, n_slot_tiles, banks, space, ring):
        self.g, self.E, self.K, self.NS = g, n_exp, k, n_slot_tiles

        def sb(n, shape, dt=F32):
            return ctx.enter_context(nc.sbuf_tensor(f"{name}_{n}", shape, dt))

        E, K, NS = n_exp, k, n_slot_tiles
        self.RING = ring
        self.chosen = sb("chosen", [P, NT * K])
        self.onehot = sb("onehot", [P, NT * K * E], BF16)
        n = NT * E
        self.prod, self.tot, self.incl = (space[:, a * n:b * n] for a, b in ((0, K), (K, K + 1), (K + 1, K + 2)))
        self.mask = space[:, (K + 2) * n:].bitcast(BF16)[:, 0:n]
        self.pair = [self.prod[:, :].bitcast(BF16)[:, i * NT * E:(i + 1) * NT * E] for i in range(2)]
        self.tri16 = sb("tri16", [P, P], BF16)
        self.ones16 = sb("ones16", [P, P], BF16)
        self.zero16 = sb("zero16", [P, P], F16)
        self.first = sb("first", [P, NT * E])
        self.count_i = sb("count_i", [P, E], I32)
        self.tiles_i = sb("tiles_i", [P, E], I32)
        self.tiles = sb("tiles", [P, E])
        self.base = sb("base", [P, E])
        self.base_slot = sb("base_slot", [P, E])
        self.own = sb("own", [P, E])
        self.base_col = sb("base_col", [P, 1])
        self.begun = sb("begun", [P, NS], BF16)
        self.slot_f = sb("slot_f", [P, NT * K])
        self.lo_i = sb("lo_i", [P, NT * K], I32)
        self.hi_i = sb("hi_i", [P, NT * K], I32)
        self.lo = sb("lo", [P, NT * K])
        self.hi = sb("hi", [P, NT * K])
        self.at_lo = [sb(f"at_lo{i}", [P, P], F16) for i in range(self.RING)]
        self.at_hi = [sb(f"at_hi{i}", [P, NS], F16) for i in range(self.RING)]
        self.wsum = sb("wsum", [P, NT])
        self.wrec = sb("wrec", [P, NT])
        self.wexp = sb("wexp", [P, NT])
        self.s_begun, self.s_expert = sem("begun"), sem("expert")
        self.done, self.s_mask, self.s_count, self.s_one, self.s_pair, self.s_table, self.s_wdiff, self.s_wexp = (
            sem(n) for n in ("done", "mask", "count", "one", "onehots", "table", "wdiff", "wexp"))
        self.ps_pos, self.ps_tot, self.ps_tab = banks

    def chunks(self):
        n = NT * self.E
        return [(i, min(n, i + 512)) for i in range(0, n, 512)]

    def tensor_counts(self, pe):
        pe.wait_ge(self.s_mask, 1)
        for j, (a, b) in enumerate(self.chunks()):
            pe.matmul(self.ps_pos[:, j, 0:b - a], self.tri16[:, :], self.mask[:, a:b], start=True, stop=True)
            last = pe.matmul(self.ps_tot[:, j, 0:b - a], self.ones16[:, :], self.mask[:, a:b], start=True, stop=True)
        last.then_inc(self.s_count, 1)

    def tensor_table(self, pe, c):
        pe.wait_ge(self.s_one, c.n + 1)
        i = c.mod(self.RING)
        pe.matmul(self.ps_tab[:, 0:self.NS], self.at_lo[i][:, :], self.at_hi[i][:, :],
                  start=False, stop=False).then_inc(self.s_pair, 1)

    def tensor_table_open(self, pe):
        pe.wait_ge(self.s_begun, 1)
        pe.matmul(self.ps_pos[:, 0, 0:self.NS], self.ones16[0:self.E, :], self.begun[0:self.E, :],
                  start=True, stop=True).then_inc(self.s_expert, 1)
        pe.matmul(self.ps_tab[:, 0:self.NS], self.zero16[:, :], self.g.iota16[:, 0:self.NS], start=True, stop=False)

    def tensor_table_close(self, pe):
        pe.matmul(self.ps_tab[:, 0:self.NS], self.zero16[:, :], self.g.iota16[:, 0:self.NS], start=False, stop=True)\
            .then_inc(self.s_pair, 1)

    def vector(self, dve, weights):
        g, E, K, NS = self.g, self.E, self.K, self.NS
        links = [0]

        def link(ins):
            links[0] += 1
            ins.then_inc(self.done, 1)
            dve.wait_ge(self.done, links[0])

        top_i = g.top_i[:, :].rearrange("p (t k) -> p t k", k=8)[:, :, 0:K]
        tk = self.chosen[:, :].rearrange("p (t k) -> p t k", k=K)
        iota_e = g.iota[:, 0:E]
        onehot = self.onehot[:, :].rearrange("p (t k e) -> p t k e", k=K, e=E)
        dve.tensor_copy(self.tri16[:, :], g.tri[:, :])
        dve.tensor_copy(self.ones16[:, :], g.ones[:, :])
        dve.memset(self.zero16[:, :], 0.0)
        link(dve.tensor_copy(tk, top_i))
        link(dve.tensor_tensor(self.onehot[:, :].rearrange("p (c e) -> p c e", e=E),
                               iota_e.unsqueeze(1).broadcast_to([P, NT * K, E]),
                               self.chosen[:, :].unsqueeze(2).broadcast_to([P, NT * K, E]), ALU.is_equal))
        mask = self.mask[:, :].rearrange("p (t e) -> p t e", e=E)
        if K == 2:
            dve.tensor_tensor(mask, onehot[:, :, 0, :], onehot[:, :, 1, :], ALU.add).then_inc(self.s_mask, 1)
        else:
            halves = [x.rearrange("p (t e) -> p t e", e=E) for x in self.pair]
            dve.tensor_tensor(halves[0], onehot[:, :, 0, :], onehot[:, :, 1, :], ALU.add)
            link(dve.tensor_tensor(halves[1], onehot[:, :, 2, :], onehot[:, :, 3, :], ALU.add))
            dve.tensor_tensor(mask, halves[0], halves[1], ALU.add).then_inc(self.s_mask, 1)
        dve.wait_ge(self.s_count, 1)
        tot_et = self.tot[:, :].rearrange("p (e t) -> p t e", e=E)
        for j, (a, b) in enumerate(self.chunks()):
            last = dve.tensor_copy(tot_et[:, a // E:b // E, :],
                                   self.ps_tot[:, j, 0:b - a].rearrange("p (t e) -> p t e", e=E))
        link(last)
        link(dve.tensor_tensor_scan(self.incl[:, :], g.not_first[:, 0:E * NT], self.tot[:, :], 0.0, ALU.mult, ALU.add))
        incl3 = self.incl[:, :].rearrange("p (e t) -> p e t", t=NT)
        tot3 = self.tot[:, :].rearrange("p (e t) -> p e t", t=NT)
        link(dve.tensor_scalar(self.count_i[:, :].unsqueeze(2), incl3[:, :, NT - 1:NT], float(P - 1), None, ALU.add))
        link(dve.tensor_scalar(self.tiles_i[:, :], self.count_i[:, :], 7, None, ALU.arith_shift_right))
        link(dve.tensor_copy(self.tiles[:, :], self.tiles_i[:, :]))
        link(dve.tensor_tensor_scan(self.base[:, :], g.ones[:, 0:E], self.tiles[:, :], 0.0, ALU.mult, ALU.add))
        link(dve.tensor_tensor(self.base[:, :], self.base[:, :], self.tiles[:, :], ALU.subtract))
        link(dve.tensor_scalar(self.base_slot[:, :], self.base[:, :], float(P), None, ALU.mult))
        link(dve.tensor_tensor(incl3, incl3, tot3, ALU.subtract))
        link(dve.tensor_tensor(incl3, incl3, self.base_slot[:, :].unsqueeze(2).broadcast_to([P, E, NT]), ALU.add))
        first = self.first[:, :].rearrange("p (t e) -> p t e", e=E)
        incl_te = self.incl[:, :].rearrange("p (e t) -> p t e", t=NT)
        for j, (a, b) in enumerate(self.chunks()):
            last = dve.tensor_tensor(first[:, a // E:b // E, :],
                                     self.ps_pos[:, j, 0:b - a].rearrange("p (t e) -> p t e", e=E),
                                     incl_te[:, a // E:b // E, :], ALU.add)
        link(last)
        link(dve.tensor_tensor(self.prod[:, :].rearrange("p (t k e) -> p t k e", k=K, e=E), onehot,
                               first.unsqueeze(2).broadcast_to([P, NT, K, E]), ALU.mult))
        link(dve.tensor_reduce(self.slot_f[:, :], self.prod[:, :].rearrange("p (c e) -> p c e", e=E), AX.X, ALU.add))
        link(dve.tensor_copy(g.slot[:, 0:NT * K], self.slot_f[:, :]))
        dve.tensor_scalar(self.lo_i[:, :], g.slot[:, 0:NT * K], P - 1, None, ALU.bitwise_and)
        link(dve.tensor_scalar(self.hi_i[:, :], g.slot[:, 0:NT * K], 7, None, ALU.arith_shift_right))
        dve.tensor_copy(self.lo[:, :], self.lo_i[:, :])
        link(dve.tensor_copy(self.hi[:, :], self.hi_i[:, :]))

        link(dve.tensor_tensor(self.own[0:E, :], self.base[0:E, :], g.ident[0:E, 0:E], ALU.mult))
        link(dve.tensor_reduce(self.base_col[0:E, :], self.own[0:E, :], AX.X, ALU.add))
        dve.tensor_scalar(self.begun[0:E, :], g.iota[0:E, 0:NS], self.base_col[0:E, :], None, ALU.is_ge)\
            .then_inc(self.s_begun, 1)

        def onehots(c):
            wait(dve, self.s_pair, c.shift(1 - self.RING).n)
            i = c.mod(self.RING)
            dve.tensor_scalar(self.at_lo[i][:, :], g.iota16[:, 0:P], self.lo[:, bass.ds(c.n, 1)], None,
                              ALU.is_equal)
            dve.tensor_scalar(self.at_hi[i][:, :], g.iota16[:, 0:NS], self.hi[:, bass.ds(c.n, 1)],
                              g.tokval[:, bass.ds(c.div(K).n, 1)], ALU.is_equal, ALU.mult).then_inc(self.s_one, 1)

        steps(dve, self.RING, NT * K, NT * K, self.RING, onehots)
        dve.wait_ge(self.s_expert, 1)
        link(dve.tensor_scalar(g.expert[0:1, 0:NS], self.ps_pos[0:1, 0, 0:NS], -1.0, None, ALU.add))
        weights(dve, link)
        dve.wait_ge(self.s_pair, NT * K + 1)
        dve.tensor_scalar(g.token[:, 0:NS], self.ps_tab[:, 0:NS], float(MID), None, ALU.add).then_inc(self.s_table, 1)


W2_COLS = M0 // P * D
CONTEXT_COLS = DC * NB * LK
W2_LATE = -(-(CONTEXT_COLS + 2 * DC * D + D) // W2_COLS)
ROUTE0_SPACE = NT * E0 * (K0 + 3)
W2_FIRST = W2_LATE + -(-ROUTE0_SPACE // W2_COLS)


def load_w2(sp, g, first, end, s_w2):
    for e in range(first, end):
        at = slice(e * W2_COLS, (e + 1) * W2_COLS)
        sp.dma_start(g.w2[:, at], g.ins["w2"][:, at]).then_inc(s_w2, 16)


class KeysValues:

    KB = 4

    def __init__(self, nc, ctx, sem, g, banks_k, bank_v):
        self.g, self.banks_k, self.bank_v = g, banks_k, bank_v
        self.ctxT, self.wk, self.wv, self.kb, self.bv = g.ctxT, g.wk1, g.wv1, g.bk1, g.bv1
        self.k_mm, self.k_out, self.v_mm, self.v_out = (
            sem("kv_" + n) for n in ("k_mm", "k_out", "v_mm", "v_out"))
        self.pieces = [(m, b) for m in range(DC) for b in range(0, NB, self.KB)]

    def keys(self, pe, first, end):
        g, n = self.g, self.KB * LK
        for i in range(first, end):
            m, b = self.pieces[i]
            wait(pe, self.k_out, i - 1)
            for c in range(DC):
                last = pe.matmul(self.banks_k[i % 2][:, 0:n], self.wk[:, c * D + m * P:c * D + (m + 1) * P],
                                 self.ctxT[:, (c * NB + b) * LK:(c * NB + b) * LK + n],
                                 start=(c == 0), stop=(c == DC - 1))
            last.then_inc(self.k_mm, 1)

    def values(self, pe, i):
        g = self.g
        wait(pe, self.v_out, i)
        for a in range(2):
            out = self.bank_v[0:LK, a * D:(a + 1) * D]
            pe.matmul(out, g.ones[0:1, 0:LK], self.bv[0:1, :], start=True, stop=False)
            for c in range(DC):
                at = (c * NB + 2 * i + a) * LK
                last = pe.matmul(out, self.ctxT[:, at:at + LK], self.wv[:, c * D:(c + 1) * D],
                                 start=False, stop=(c == DC - 1))
        last.then_inc(self.v_mm, 1)

    def scalar(self, act, event):
        g, n, i = self.g, self.KB * LK, event - len(self.pieces)
        if i < 0:
            m, b = self.pieces[event]
            act.wait_ge(self.k_mm, event + 1)
            act.activation(g.kT1[:, (m * NB + b) * LK:(m * NB + b) * LK + n], self.banks_k[event % 2][:, 0:n],
                           ACT.Identity, bias=self.kb[:, m:m + 1]).then_inc(self.k_out, 1)
        else:
            act.wait_ge(self.v_mm, i + 1)
            act.activation(g.v1[0:LK, 2 * i * D:2 * (i + 1) * D], self.bank_v[0:LK, :], ACT.Copy)\
                .then_inc(self.v_out, 1)


class Split:

    def __init__(self, sem, w, low, chunks):
        self.w, self.low, self.n = w, low, w.shape[1] // chunks
        self.chunks = chunks
        self.s_high, self.s_low, self.s_done = sem("sp_high"), sem("sp_low"), sem("sp_done")

    def part(self, ap, i):
        return ap[:, i * self.n:(i + 1) * self.n]

    def scalar(self, act, event):
        if event < self.chunks:
            act.activation(self.part(self.low, event), self.part(self.w, event), ACT.Copy).then_inc(self.s_high, 1)
        i = event - 2
        if 0 <= i < self.chunks:
            act.wait_ge(self.s_low, i + 1)
            act.activation(self.part(self.w, i).bitcast(F32R), self.part(self.w, i), ACT.Copy).then_inc(self.s_done, 1)

    def gpsimd(self, pool):
        for i in range(self.chunks):
            pool.wait_ge(self.s_high, i + 1)
            low = self.part(self.low, i)
            pool.tensor_tensor(low, self.part(self.w, i), low, ALU.subtract).then_inc(self.s_low, 1)


def route0_phase(nc, g):
    ctx = ExitStack()
    with ctx:
        sem = semaphores(nc, ctx, "r0_")
        space = g.w2[:, W2_LATE * W2_COLS:W2_LATE * W2_COLS + ROUTE0_SPACE]
        r = Router(nc, ctx, sem, g, "r0", E0, K0, NS0, (g.pair[0], g.pair[1], g.bank[4]), space, 8)
        kv = KeysValues(nc, ctx, sem, g, g.bank[5:7], g.bank[7])
        events = len(kv.pieces) + NB // 2
        split = Split(sem, g.w13[:, :], g.w13_low[:, :], events)
        s_w2 = sem("w2")
        block = ctx.enter_context(nc.Block())
        top = g.top_v[:, :].rearrange("p (t k) -> p t k", k=8)
        w = g.weight[:, 0:NT * K0].rearrange("p (t k) -> p t k", k=K0)

        @block.sync
        def _(sp):
            load_w2(sp, g, W2_FIRST, E0, s_w2)
            sp.wait_ge(r.s_begun, 1)
            load_w2(sp, g, W2_LATE, W2_FIRST, s_w2)
            sp.wait_ge(s_w2, 16 * (E0 - W2_LATE))

        @block.vector
        def _(dve):
            def weights(dve, link):
                dve.tensor_tensor(r.wsum[:, :].unsqueeze(2), top[:, :, 1:2], top[:, :, 0:1], ALU.subtract)\
                    .then_inc(r.s_wdiff, 1)
                dve.wait_ge(r.s_wexp, 1)
                link(dve.tensor_scalar(r.wsum[:, :], r.wexp[:, :], 1.0, None, ALU.add))
                link(dve.reciprocal(w[:, :, 0:1], r.wsum[:, :].unsqueeze(2)))
                link(dve.tensor_tensor(w[:, :, 1:2], w[:, :, 0:1], r.wexp[:, :].unsqueeze(2), ALU.mult))

            r.vector(dve, weights)

        @block.scalar
        def _(act):
            for event in range(events + 2):
                split.scalar(act, event)
                if event < events:
                    kv.scalar(act, event)
            act.wait_ge(r.s_wdiff, 1)
            act.activation(r.wexp[:, :], r.wsum[:, :], ACT.Exp).then_inc(r.s_wexp, 1)

        @block.gpsimd
        def _(pool):
            split.gpsimd(pool)

        @block.tensor
        def _(pe):
            EARLY, PAIRS = 3, NT * K0
            kv.keys(pe, 0, EARLY)
            r.tensor_counts(pe)
            kv.keys(pe, EARLY, len(kv.pieces))
            r.tensor_table_open(pe)
            for i in range(PAIRS):
                r.tensor_table(pe, At(None, 0, i))
                if (i + 1) % (2 * PAIRS // NB) == 0:
                    kv.values(pe, i // (2 * PAIRS // NB))
            r.tensor_table_close(pe)


def moe0_phase(nc, g):
    ctx = ExitStack()
    with ctx:
        def sb(name, shape, dt=F32):
            return ctx.enter_context(nc.sbuf_tensor("m0_" + name, shape, dt))

        sem = semaphores(nc, ctx, "m0_")

        MC = M0 // P
        idx = [sb(f"idx{i}", [P, 1], I32) for i in range(GB)]
        xg = [sb(f"xg{i}", [P, D]) for i in range(GB - 1)] + [g.kv[:, DC * NB * LK + NB * D:DC * NB * LK + NB * D + D]]
        y = [g.top_v, g.top_i[:, :].bitcast(F32)]
        xT_high, xT_low = ([sb(f"xT_{n}{i}", [P, D], F32R) for i in range(2)] for n in ("high", "low"))
        w13_high = g.w13[:, :].bitcast(F32R)
        h = [sb(f"h{i}", [P, M0]) for i in range(2)]
        hT = sb("hT", [P, M0])
        passed, s_w2 = sem("passed_pool"), sem("w2")
        s_g = [sem(f"s_g{i}") for i in range(GB)]
        y_st = [sem(f"y_st{i}") for i in range(2)]
        idx_ready, x_t, high_out, low_out, gu_mm, silu_done, h_done, h_t, h_out, y_mm, y_out = (
            sem(n) for n in ("idx_ready", "x_t", "high_out", "low_out", "gu_mm", "silu_done", "h_done", "h_t", "h_out", "y_mm",
                             "y_out"))
        ps_gu, ps_x, ps_ht, ps_y = g.pair[0:2], g.bank[4], g.bank[5], g.bank[6]
        block = ctx.enter_context(nc.Block())

        @block.gpsimd
        def _(pool):
            def gather(j):
                p = j.mod(GB)
                wait_alone(pool, x_t, j.shift(1 - GB).n, passed)
                pool.tensor_copy(idx[p][:, :], g.token[:, bass.ds(j.n, 1)]).then_inc(idx_ready, 1)
                wait_alone(pool, idx_ready, j.n + 1, passed)
                pool.indirect_dma_start(out=xg[p][:, :], out_offset=None, in_=g.xn,
                                        in_offset=bass.IndirectOffsetOnAxis(ap=idx[p][:, :], axis=0))\
                    .then_inc(s_g[p], 16)

            steps(pool, GB, NS0, NS0, GB, gather)

        @block.sync
        def _(sp):
            sp.wait_ge(x_t, 1)
            load_w2(sp, g, 0, W2_LATE, s_w2)

            def store(j):
                p = j.mod(2)
                sp.wait_ge(y_out, j.n + 1)
                sp.dma_start(g.y0[bass.ds(j.n * P, P), :], y[p][:, :]).then_inc(y_st[p], 16)

            steps(sp, 2, NS0, NS0, 2, store)
            for p in range(2):
                sp.wait_ge(y_st[p], NS0 // 2 * 16)

        @block.scalar
        def _(act):
            def step(s):
                j = s
                if j.within(NS0):
                    p = j.mod(2)
                    act.wait_ge(x_t, j.n + 1)
                    wait(act, gu_mm, j.shift(-1).n)
                    act.activation(xT_high[p][:, :], ps_x[:, 0:D], ACT.Copy).then_inc(high_out, 1)
                j = s.shift(-1)
                if j.within(NS0):
                    p = j.mod(2)
                    act.wait_ge(gu_mm, j.n + 1)
                    wait(act, h_t, j.shift(-1).n)
                    act.activation(h[p][:, :], ps_gu[p][:, 0, :], ACT.Silu).then_inc(silu_done, 1)
                j = s.shift(-2)
                if j.within(NS0):
                    act.wait_ge(h_t, j.n + 1)
                    wait(act, y_mm, j.n)
                    act.activation(hT[:, :], ps_ht[:, 0:M0], ACT.Copy).then_inc(h_out, 1)

            steps(act, 4, NS0, NS0 + 2, 2, step)

        @block.vector
        def _(dve):
            def step(s):
                j = s
                if j.within(NS0):
                    p = j.mod(2)
                    dve.wait_ge(high_out, j.n + 1)
                    wait(dve, gu_mm, j.shift(-1).n)
                    dve.tensor_tensor(xT_low[p][:, :], ps_x[:, 0:D], xT_high[p][:, :], ALU.subtract)\
                        .then_inc(low_out, 1)
                j = s.shift(-1)
                if j.within(NS0):
                    p = j.mod(2)
                    dve.wait_ge(silu_done, j.n + 1)
                    dve.tensor_tensor(h[p][:, :], ps_gu[p][:, 1, :], h[p][:, :], ALU.mult).then_inc(h_done, 1)
                j = s.shift(-3)
                if j.within(NS0):
                    p = j.mod(2)
                    dve.wait_ge(y_mm, j.n + 1)
                    wait(dve, y_st[p], j.div(2).n * 16)
                    dve.tensor_copy(y[p][:, :], ps_y[:, 0:D]).then_inc(y_out, 1)

            steps(dve, 6, NS0, NS0 + 3, 2, step)

        @block.tensor
        def _(pe):
            e = [pe.alloc_register(f"m0_e{i}") for i in range(GB)]

            def step(s):
                j = s.shift(-1)
                if j.within(NS0):
                    pe.reg_load(e[j.mod(GB)], g.expert[0:1, bass.ds(j.n, 1)])
                j = s
                if j.within(NS0):
                    p = j.mod(GB)
                    pe.wait_ge(s_g[p], (j.div(GB).n + 1) * 16)
                    wait(pe, low_out, j.n)
                    for c in range(DC):
                        last = pe.transpose(ps_x[:, c * P:(c + 1) * P], xg[p][:, c * P:(c + 1) * P], g.ident[:, :])
                    last.then_inc(x_t, 1)
                j = s.shift(-1)
                if j.within(NS0):
                    p = j.mod(2)
                    ex = pe.snap(e[j.mod(GB)], min_val=0, max_val=E0 - 1)
                    pe.wait_ge(low_out, j.n + 1)
                    wait(pe, h_done, j.shift(-1).n)
                    for half in range(2):
                        for c in range(DC):
                            tile = slice(c * P, (c + 1) * P)
                            at = bass.ds(ex * (DC * 2 * M0) + (c * 2 + half) * M0, M0)
                            for x, w in ((xT_high, w13_high), (xT_high, g.w13_low), (xT_low, w13_high)):
                                last = pe.matmul(ps_gu[p][:, half, :], x[p][:, tile], w[:, at],
                                                 start=(c == 0 and w is w13_high and x is xT_high),
                                                 stop=(c == DC - 1 and x is xT_low))
                    last.then_inc(gu_mm, 1)
                j = s.shift(-2)
                if j.within(NS0):
                    p = j.mod(2)
                    pe.wait_ge(h_done, j.n + 1)
                    wait(pe, h_out, j.n)
                    for c in range(MC):
                        last = pe.transpose(ps_ht[:, c * P:(c + 1) * P], h[p][:, c * P:(c + 1) * P], g.ident[:, :])
                    last.then_inc(h_t, 1)
                j = s.shift(-3)
                if j.within(NS0):
                    p = j.mod(2)
                    ex = pe.snap(e[j.mod(GB)], min_val=0, max_val=E0 - 1)
                    if j.loop is None and j.off == 0:
                        pe.wait_ge(s_w2, 16 * W2_LATE)
                    pe.wait_ge(h_out, j.n + 1)
                    wait(pe, y_out, j.n)
                    for c in range(MC):
                        last = pe.matmul(ps_y[:, 0:D], hT[:, c * P:(c + 1) * P],
                                         g.w2[:, bass.ds(ex * (MC * D) + c * D, D)],
                                         start=(c == 0), stop=(c == MC - 1))
                    last.then_inc(y_mm, 1)

            steps(pe, 8, NS0, NS0 + 3, GB, step)


def attention1_phase(nc, g):
    ctx = ExitStack()
    with ctx:
        def sb(name, shape, dt=F32):
            return ctx.enter_context(nc.sbuf_tensor("at1_" + name, shape, dt))

        sem = semaphores(nc, ctx, "at1_")

        SCALE = float(D) ** -0.5
        wq, wo = (sb(n, [P, DC * D]) for n in ("wq", "wo"))
        wr = sb("wr", [P, DC * E1])
        qb, qbs = sb("qb", [P, DC]), sb("qbs", [P, DC])
        bo, rb = sb("bo", [1, D]), sb("rb", [P, E1])
        ring = lambda name, shape, dt=F32, n=2: [sb(f"{name}{i}", shape, dt) for i in range(n)]
        idx = [ring(f"idx{k}_", [P, 1], I32, n=GB) for k in range(K0)]
        yg = [ring(f"yg{k}_", [P, D], n=GB) for k in range(K0)]
        x1, x2, x2r = (ring(n, [P, D]) for n in ("x1_", "x2_", "x2r"))
        xn = ring("xn", [P, D], n=4)
        xnT, qT = ring("xnT", [P, D]), ring("qT", [P, D])
        nmx, den, rec = ring("nmx", [P, 1]), ring("den", [P, 1]), ring("rec", [P, 1])
        pr, prT = ring("pr", [P, LK]), ring("prT", [P, P])
        o, oT = ring("o", [P, D]), ring("oT", [P, D])
        x3, xm, xmT = ring("x3_", [P, D]), ring("xm", [P, D]), ring("xmT", [P, D])
        s_w, s_next, s_qbs = sem("s_w"), sem("s_next"), sem("s_qbs")
        passed = [sem(f"passed_{n}") for n in ("dve", "pool", "act")]
        s_passed_sp = sem("passed_sp")
        lna = LayerNorm(sb, sem, "lna", passed, g.minus_half)
        lnm = LayerNorm(sb, sem, "lnm", passed, g.minus_half)
        s_x1, s_x2r, x2_st, x3_st, xm_st = ([sem(f"{n}{i}") for i in range(2)] for n in (
            "s_x1", "s_x2r", "x2_st", "x3_st", "xm_st"))
        s_y = [[sem(f"s_y{k}_{i}") for i in range(GB)] for k in range(K0)]
        (idx_ready, half_sum, x2_done, xn_done, x_t, x_out, q_mm, q_out, s_mm,
         max_done, exp_done, rec_done, p_t, p_out, pv_mm, o_done, o_t, o_out, wo_mm, x3_done, xm_done, xm_t, xm_out,
         r_mm, lg_done) = (sem(n) for n in (
             "idx_ready", "half_sum", "x2_done", "xn_done", "x_t", "x_out", "q_mm", "q_out",
             "s_mm", "max_done", "exp_done", "rec_done", "p_t", "p_out", "pv_mm", "o_done", "o_t",
             "o_out", "wo_mm", "x3_done", "xm_done", "xm_t", "xm_out", "r_mm", "lg_done"))
        ps_x, ps_q, ps_s, ps_t, ps_o, ps_wo, ps_m, _ = g.bank
        block = ctx.enter_context(nc.Block())
        SUM, XN, Q, S, PT, PV, OT, WO, XM, XMT, R = 1, 2, 3, 4, 5, 6, 7, 8, 9, 10, 11
        FIRST, BODY = 12, 4
        GU_FROM, GU_LOADS = 4, 8
        LEAD = 2

        def stage(s, skew):
            t = s.shift(-skew)
            return t if t.within(NT) else None

        def rows(t):
            return bass.ds(t.n * P, P)

        @block.sync
        def _(sp):
            for dst, src in ((wq, g.ins["wq1"]), (wo, g.ins["wo1"]), (wr, g.ins["wr1"]), (qb, g.ins["bq1"]),
                             (bo, g.ins["bo1"]), (rb, g.ins["rb1"])):
                sp.dma_start(dst[:, :], src).then_inc(s_w, 16)

            def step(s):
                if (t := stage(s, 0)) is not None:
                    p = t.mod(2)
                    wait(sp, x2_done, t.shift(-1).n)
                    sp.dma_start(x1[p][:, :], g.x1[rows(t), :]).then_inc(s_x1[p], 16)
                if (t := stage(s, SUM + 1)) is not None:
                    p = t.mod(2)
                    sp.wait_ge(x2_done, t.n + 1)
                    sp.dma_start(g.x2[rows(t), :], x2[p][:, :]).then_inc(x2_st[p], 16)
                if (t := stage(s, PV)) is not None:
                    p = t.mod(2)
                    wait_alone(sp, x2_st[p], (t.div(2).n + 1) * 16, s_passed_sp)
                    wait(sp, x3_done, t.shift(-1).n)
                    sp.dma_start(x2r[p][:, :], g.x2[rows(t), :]).then_inc(s_x2r[p], 16)
                if (t := stage(s, WO + 1)) is not None:
                    p = t.mod(2)
                    sp.wait_ge(x3_done, t.n + 1)
                    sp.dma_start(g.x3[rows(t), :], x3[p][:, :]).then_inc(x3_st[p], 16)
                if (t := stage(s, XM + 1)) is not None:
                    p = t.mod(2)
                    sp.wait_ge(xm_done, t.n + 1)
                    sp.dma_start(g.xn4[rows(t), :], xm[p][:, :]).then_inc(xm_st[p], 16)

            steps(sp, FIRST, NT, NT + XM + 2, BODY, step)
            for p in range(2):
                for st in (x2_st, x3_st, xm_st):
                    sp.wait_ge(st[p], NT // 2 * 16)
            sp.wait_ge(s_next, GU_LOADS * 16)

        @block.gpsimd
        def _(pool):
            def step(s):
                if (t := stage(s, WO + LEAD)) is not None:
                    lnm.invert(pool, t)
                if (t := stage(s, SUM + LEAD)) is not None:
                    lna.invert(pool, t)
                if (t := stage(s, 0)) is not None:
                    p = t.mod(GB)
                    wait_alone(pool, x2_done, t.shift(1 - GB).n, passed[1])
                    for k in range(K0):
                        pool.tensor_copy(idx[k][p][:, :], g.slot[:, bass.ds(t.n * K0 + k, 1)]).then_inc(idx_ready, 1)
                    wait_alone(pool, idx_ready, t.n * K0 + K0, passed[1])
                    for k in range(K0):
                        pool.indirect_dma_start(out=yg[k][p][:, :], out_offset=None, in_=g.y0,
                                                in_offset=bass.IndirectOffsetOnAxis(ap=idx[k][p][:, :], axis=0))\
                            .then_inc(s_y[k][p], 16)

            steps(pool, FIRST, NT, NT + WO + LEAD, BODY, step)

        @block.vector
        def _(dve):
            dve.wait_ge(s_w, 6 * 16)
            dve.tensor_scalar(qbs[:, :], qb[:, :], SCALE, None, ALU.mult).then_inc(s_qbs, 1)

            def sums(s):
                out, into, rec_of = stage(s, WO), stage(s, SUM), stage(s, PT)
                if (t := out) is not None:
                    p = t.mod(2)
                    dve.wait_ge(wo_mm, t.n + 1)
                    dve.wait_ge(s_x2r[p], (t.div(2).n + 1) * 16)
                    wait(dve, x3_st[p], t.div(2).n * 16)
                    dve.tensor_tensor(x3[p][:, :], ps_wo[:, 0:D], x2r[p][:, :], ALU.add).then_inc(x3_done, 1)
                if (t := into) is not None:
                    p, q = t.mod(2), t.mod(GB)
                    dve.wait_ge(s_x1[p], (t.div(2).n + 1) * 16)
                    dve.wait_ge(s_y[0][q], (t.div(GB).n + 1) * 16)
                    wait(dve, x2_st[p], t.div(2).n * 16)
                    dve.scalar_tensor_tensor(x2[p][:, :], yg[0][q][:, :], g.weight[:, bass.ds(t.n * K0, 1)],
                                             x1[p][:, :], ALU.mult, ALU.add).then_inc(half_sum, 1)
                if (t := out) is not None:
                    dve.wait_ge(x3_done, t.n + 1)
                    lnm.halves(dve, x3[t.mod(2)][:, :], t)
                if (t := into) is not None:
                    p, q = t.mod(2), t.mod(GB)
                    dve.wait_ge(s_y[1][q], (t.div(GB).n + 1) * 16)
                    dve.wait_ge(half_sum, t.n + 1)
                    dve.scalar_tensor_tensor(x2[p][:, :], yg[1][q][:, :], g.weight[:, bass.ds(t.n * K0 + 1, 1)],
                                             x2[p][:, :], ALU.mult, ALU.add).then_inc(x2_done, 1)
                if (t := out) is not None:
                    lnm.join(dve, t)
                if (t := rec_of) is not None:
                    p = t.mod(2)
                    dve.wait_ge(exp_done, t.n + 1)
                    dve.reciprocal(rec[p][:, :], den[p][:, :]).then_inc(rec_done, 1)
                if (t := into) is not None:
                    dve.wait_ge(x2_done, t.n + 1)
                    lna.moments(dve, x2[t.mod(2)][:, :], t)

            def step(s):
                if (t := stage(s, PV)) is not None:
                    p = t.mod(2)
                    dve.wait_ge(pv_mm, t.n + 1)
                    dve.wait_ge(rec_done, t.n + 1)
                    wait(dve, o_t, t.shift(-1).n)
                    dve.scalar_tensor_tensor(o[p][:, :], ps_o[:, 0:D], rec[p][:, :], xn[t.mod(4)][:, :],
                                             ALU.mult, ALU.add).then_inc(o_done, 1)
                if (t := stage(s, XN)) is not None:
                    wait(dve, x_t, t.shift(-3).n)
                    wait(dve, o_done, t.shift(-3).n)
                    lna.apply(dve, x2[t.mod(2)][:, :], xn[t.mod(4)][:, :], t).then_inc(xn_done, 1)
                if (t := stage(s, R)) is not None:
                    p = t.mod(2)
                    dve.wait_ge(r_mm, t.n + 1)
                    dve.tensor_tensor(g.logits[:, bass.ds(t.n * E1, E1)], ps_m[:, D:D + E1], rb[:, :], ALU.add)\
                        .then_inc(lg_done, 1)
                if (t := stage(s, XM)) is not None:
                    p = t.mod(2)
                    wait(dve, xm_st[p], t.div(2).n * 16)
                    wait(dve, xm_t, t.shift(-1).n)
                    lnm.apply(dve, x3[p][:, :], xm[p][:, :], t).then_inc(xm_done, 1)
                if (t := stage(s, S)) is not None:
                    p = t.mod(2)
                    dve.wait_ge(s_mm, t.n + 1)
                    dve.tensor_reduce(nmx[p][:, :], ps_s[:, 0:LK], AX.X, ALU.max, negate=True).then_inc(max_done, 1)
                if (t := stage(s, WO)) is not None or stage(s, SUM) is not None:
                    sums(s)

            steps(dve, FIRST, NT, NT + R + 1, BODY, step)

        @block.scalar
        def _(act):
            act.wait_ge(s_w, 6 * 16)
            act.wait_ge(s_qbs, 1)

            def step(s):
                if s.loop is None and GU_FROM <= s.off < GU_FROM + GU_LOADS:
                    n = E1 // GU_LOADS * DC * 2 * M1
                    e = s.off - GU_FROM
                    act.dma_start(g.gu[:, e * n:(e + 1) * n], g.ins["gu"][:, e * n:(e + 1) * n]).then_inc(s_next, 16)
                if (t := stage(s, Q)) is not None:
                    p = t.mod(2)
                    act.wait_ge(q_mm, t.n + 1)
                    wait(act, s_mm, t.shift(-1).n)
                    for c in range(DC):
                        act.activation(qT[p][:, c * P:(c + 1) * P], ps_q[:, c * P:(c + 1) * P], ACT.Identity,
                                       bias=qbs[:, c:c + 1], scale=SCALE).then_inc(q_out, 1)
                if (t := stage(s, PT)) is not None:
                    p = t.mod(2)
                    act.wait_ge(p_t, t.n + 1)
                    wait(act, pv_mm, t.shift(-1).n)
                    act.activation(prT[p][0:LK, :], ps_t[0:LK, 0:P], ACT.Copy).then_inc(p_out, 1)
                if (t := stage(s, XN)) is not None:
                    p = t.mod(2)
                    act.wait_ge(x_t, t.n + 1)
                    wait(act, q_mm, t.shift(-1).n)
                    act.activation(xnT[p][:, :], ps_x[:, 0:D], ACT.Copy).then_inc(x_out, 1)
                if (t := stage(s, S)) is not None:
                    p = t.mod(2)
                    act.wait_ge(max_done, t.n + 1)
                    wait(act, p_t, t.shift(-1).n)
                    wait(act, rec_done, t.shift(-1).n)
                    act.activation(pr[p][:, :], ps_s[:, 0:LK], ACT.Exp, bias=nmx[p][:, :],
                                   accum_out=den[p][:, :]).then_inc(exp_done, 1)
                if (t := stage(s, OT)) is not None:
                    p = t.mod(2)
                    act.wait_ge(o_t, t.n + 1)
                    wait(act, wo_mm, t.shift(-1).n)
                    act.activation(oT[p][:, :], ps_t[:, P:P + D], ACT.Copy).then_inc(o_out, 1)
                if (t := stage(s, XMT)) is not None:
                    p = t.mod(2)
                    wait_alone(act, xm_t, t.n + 1, passed[2])
                    act.activation(g.xn4T[:, :].rearrange("p (c n) -> p c n", c=DC)[:, :, rows(t)],
                                   ps_m[:, 0:D].rearrange("p (c n) -> p c n", c=DC), ACT.Copy)
                    wait(act, r_mm, t.shift(-1).n)
                    act.activation(xmT[p][:, :], ps_m[:, 0:D], ACT.Copy).then_inc(xm_out, 1)

            steps(act, FIRST, NT, NT + R + 1, BODY, step)

        @block.tensor
        def _(pe):
            pe.wait_ge(s_w, 6 * 16)

            def step(s):
                if (t := stage(s, PV)) is not None:
                    p, b = t.mod(2), t.div(2)
                    pe.wait_ge(p_out, t.n + 1)
                    wait(pe, o_done, t.n)
                    pe.matmul(ps_o[:, 0:D], prT[p][0:LK, :], g.v1[0:LK, bass.ds(b.n * D, D)], start=True, stop=True)\
                        .then_inc(pv_mm, 1)
                if (t := stage(s, Q)) is not None:
                    p = t.mod(2)
                    pe.wait_ge(x_out, t.n + 1)
                    wait(pe, q_out, t.n * 2)
                    for m in range(DC):
                        for c in range(DC):
                            last = pe.matmul(ps_q[:, m * P:(m + 1) * P], wq[:, c * D + m * P:c * D + (m + 1) * P],
                                             xnT[p][:, c * P:(c + 1) * P], start=(c == 0), stop=(c == DC - 1))
                    last.then_inc(q_mm, 1)
                if (t := stage(s, R)) is not None:
                    p = t.mod(2)
                    pe.wait_ge(xm_out, t.n + 1)
                    for c in range(DC):
                        last = pe.matmul(ps_m[:, D:D + E1], xmT[p][:, c * P:(c + 1) * P], wr[:, c * E1:(c + 1) * E1],
                                         start=(c == 0), stop=(c == DC - 1))
                    last.then_inc(r_mm, 1)
                if (t := stage(s, WO)) is not None:
                    p = t.mod(2)
                    pe.wait_ge(o_out, t.n + 1)
                    wait(pe, x3_done, t.n)
                    pe.matmul(ps_wo[:, 0:D], g.ones[0:1, :], bo[0:1, :], start=True, stop=False)
                    for c in range(DC):
                        last = pe.matmul(ps_wo[:, 0:D], oT[p][:, c * P:(c + 1) * P], wo[:, c * D:(c + 1) * D],
                                         start=False, stop=(c == DC - 1))
                    last.then_inc(wo_mm, 1)
                if (t := stage(s, PT)) is not None:
                    p = t.mod(2)
                    pe.wait_ge(exp_done, t.n + 1)
                    wait(pe, p_out, t.n)
                    wait(pe, o_out, t.shift(-2).n)
                    pe.transpose(ps_t[0:LK, 0:P], pr[p][:, :], g.ident[:, :]).then_inc(p_t, 1)
                if (t := stage(s, S)) is not None:
                    p, b = t.mod(2), t.div(2)
                    pe.wait_ge(q_out, t.n * 2 + 2)
                    wait(pe, exp_done, t.n)
                    for c in range(DC):
                        last = pe.matmul(ps_s[:, 0:LK], qT[p][:, c * P:(c + 1) * P],
                                         g.kT1[:, bass.ds(b.n * LK + c * NB * LK, LK)], start=(c == 0), stop=(c == DC - 1))
                    last.then_inc(s_mm, 1)
                if (t := stage(s, XMT)) is not None:
                    p = t.mod(2)
                    pe.wait_ge(xm_done, t.n + 1)
                    wait(pe, xm_out, t.n)
                    wait(pe, lg_done, t.n)
                    for c in range(DC):
                        last = pe.transpose(ps_m[:, c * P:(c + 1) * P], xm[p][:, c * P:(c + 1) * P], g.ident[:, :])
                    last.then_inc(xm_t, 1)
                if (t := stage(s, XN)) is not None:
                    p = t.mod(2)
                    pe.wait_ge(xn_done, t.n + 1)
                    wait(pe, x_out, t.n)
                    for c in range(DC):
                        last = pe.transpose(ps_x[:, c * P:(c + 1) * P], xn[t.mod(4)][:, c * P:(c + 1) * P], g.ident[:, :])
                    last.then_inc(x_t, 1)
                if (t := stage(s, OT)) is not None:
                    p = t.mod(2)
                    pe.wait_ge(o_done, t.n + 1)
                    wait(pe, o_out, t.n)
                    if (q := stage(s, PT)) is not None:
                        pe.wait_ge(p_out, q.n + 1)
                    for c in range(DC):
                        last = pe.transpose(ps_t[:, (c + 1) * P:(c + 2) * P], o[p][:, c * P:(c + 1) * P], g.ident[:, :])
                    last.then_inc(o_t, 1)

            steps(pe, FIRST, NT, NT + R + 1, BODY, step)


class SharedExpert:

    LAG = 5

    def __init__(self, nc, ctx, sem, g, name, first_block, blocks, banks, on_vector):
        def sb(n, shape, dt=F32):
            return ctx.enter_context(nc.sbuf_tensor(f"{name}_{n}", shape, dt))

        self.on_vector = on_vector
        self.g, self.units, self.t0 = g, 4 * blocks, 4 * first_block
        self.MC = MS // P
        self.sg, self.up = ([sb(f"{n}{i}", [P, MS]) for i in range(2)] for n in ("sg", "up"))
        self.h = [sb(f"h{i}", [P, 512]) for i in range(8)]
        self.ysb, self.x3, self.xs = ([sb(f"{n}{i}", [P, D]) for i in range(2)] for n in ("y", "x3", "xs"))
        self.g_mm, self.u_mm, self.sg_done, self.up_done, self.h_done, self.y_mm, self.y_out, self.xs_done = (
            sem(n) for n in ("g_mm", "u_mm", "sg_done", "up_done", "h_done", "y_mm", "y_out", "xs_done"))
        self.s_x3, self.xs_st = ([sem(f"{n}{i}") for i in range(2)] for n in ("s_x3", "xs_st"))
        self.ps_g, self.ps_u, self.ps_y = banks
        self.u_free, self.y_free = (self.h_done, self.xs_done) if on_vector else (self.up_done, self.y_out)

    def behind(self, c):
        t = c.shift(-self.LAG)
        return t if t.within(self.units) else None

    def tensor(self, pe, c):
        g = self.g
        if c.within(self.units):
            block = c.div(4)
            for ps, w, s_mm, s_free in ((self.ps_g, g.sg_w, self.g_mm, self.sg_done),
                                        (self.ps_u, g.su_w, self.u_mm, self.u_free)):
                wait(pe, s_free, c.n)
                for d in range(DC):
                    m = c.mod(4)
                    last = pe.matmul(ps[:, :], w[:, d * MS + m * P:d * MS + (m + 1) * P],
                                     g.xn4T[:, bass.ds(block.n * 512 + (d * NTOK + self.t0 * P), 512)],
                                     start=(d == 0), stop=(d == DC - 1))
                last.then_inc(s_mm, 1)
        if (t := self.behind(c)) is not None:
            pe.wait_ge(self.h_done, t.div(4).n * 4 + 4)
            wait(pe, self.y_free, t.n)
            for m in range(self.MC):
                q = t.mod(4)
                last = pe.matmul(self.ps_y[:, 0:D], self.h[4 * t.div(4).mod(2) + m][:, q * P:(q + 1) * P],
                                 g.sd_w[:, m * D:(m + 1) * D], start=(m == 0), stop=(m == self.MC - 1))
            last.then_inc(self.y_mm, 1)

    def silu(self, act, c):
        if c.within(self.units):
            p = c.mod(2)
            act.wait_ge(self.g_mm, c.n + 1)
            wait(act, self.h_done, c.shift(-1).n)
            act.activation(self.sg[p][:, :], self.ps_g[:, :], ACT.Silu).then_inc(self.sg_done, 1)

    def scalar(self, act, c):
        self.silu(act, c)
        if c.within(self.units):
            p = c.mod(2)
            act.wait_ge(self.u_mm, c.n + 1)
            act.activation(self.up[p][:, :], self.ps_u[:, :], ACT.Copy).then_inc(self.up_done, 1)
        if (t := self.behind(c)) is not None:
            p = t.mod(2)
            act.wait_ge(self.y_mm, t.n + 1)
            wait(act, self.xs_done, t.shift(-1).n)
            act.activation(self.ysb[p][:, :], self.ps_y[:, 0:D], ACT.Copy).then_inc(self.y_out, 1)

    def gpsimd(self, pool, c):
        if c.within(self.units):
            p = c.mod(2)
            wait(pool, self.y_mm, (c.div(4).n - 1) * 4)
            pool.wait_ge(self.sg_done, c.n + 1)
            pool.wait_ge(self.up_done, c.n + 1)
            pool.tensor_tensor(self.h[c.mod(8)][:, :], self.sg[p][:, :], self.up[p][:, :], ALU.mult)\
                .then_inc(self.h_done, 1)
        if (t := self.behind(c)) is not None:
            p = t.mod(2)
            pool.wait_ge(self.y_out, t.n + 1)
            pool.wait_ge(self.s_x3[p], (t.div(2).n + 1) * 16)
            wait(pool, self.xs_st[p], t.div(2).n * 16)
            pool.tensor_tensor(self.xs[p][:, :], self.x3[p][:, :], self.ysb[p][:, :], ALU.add).then_inc(self.xs_done, 1)

    def vector(self, dve, c, kept):
        if c.within(self.units):
            wait(dve, self.y_mm, (c.div(4).n - 1) * 4)
            dve.wait_ge(self.sg_done, c.n + 1)
            dve.wait_ge(self.u_mm, c.n + 1)
            dve.tensor_tensor(self.h[c.mod(8)][:, :], self.ps_u[:, :], self.sg[c.mod(2)][:, :], ALU.mult)\
                .then_inc(self.h_done, 1)
        if (t := self.behind(c)) is not None:
            p = t.mod(2)
            dve.wait_ge(self.y_mm, t.n + 1)
            dve.wait_ge(self.s_x3[p], (t.div(2).n + 1) * 16)
            dve.tensor_tensor(kept[:, bass.ds(t.n * D, D)], self.ps_y[:, 0:D], self.x3[p][:, :], ALU.add)\
                .then_inc(self.xs_done, 1)

    def load(self, eng, c):
        if (t := self.behind(c)) is not None:
            p = t.mod(2)
            wait(eng, self.xs_done, t.shift(-1).n)
            eng.dma_start(self.x3[p][:, :], self.g.x3[bass.ds((t.n + self.t0) * P, P), :]).then_inc(self.s_x3[p], 16)

    def sync(self, sp, c):
        g = self.g
        self.load(sp, c)
        if (t := self.behind(c)) is not None:
            p = t.mod(2)
            sp.wait_ge(self.xs_done, t.n + 1)
            sp.dma_start(g.xs[bass.ds((t.n + self.t0) * P, P), :], self.xs[p][:, :]).then_inc(self.xs_st[p], 16)

    def landed(self, sp):
        for p in range(2):
            sp.wait_ge(self.xs_st[p], self.units // 2 * 16)


def route1_phase(nc, g):
    ctx = ExitStack()
    with ctx:
        sem = semaphores(nc, ctx, "r1_")
        r = Router(nc, ctx, sem, g, "r1", E1, K1, NS1, (g.pair[0], g.pair[1], g.bank[4]), g.kv[:, :], 16)
        g.not_first = ctx.enter_context(nc.sbuf_tensor("r1_not_first", [P, E1 * NT], F32))
        s_not_first, s_w, s_soft, s_shift, s_exp, s_top = (
            sem(n) for n in ("not_first", "w", "soft", "shift", "exp", "top"))
        shift, total = (ctx.enter_context(nc.sbuf_tensor(f"r1_{n}", [P, NT], F32)) for n in ("shift", "total"))
        sh = SharedExpert(nc, ctx, sem, g, "sh", 0, SHARED_FIRST, g.bank[5:8], False)
        block = ctx.enter_context(nc.Block())
        top = g.top_v[:, :].rearrange("p (t k) -> p t k", k=8)[:, :, 0:K1]
        w = g.weight[:, 0:NT * K1].rearrange("p (t k) -> p t k", k=K1)
        U, COUNTS, TAB, PER = sh.units, 3, 8, 16

        @block.sync
        def _(sp):
            for dst, src in ((g.sg_w, g.ins["sg"]), (g.su_w, g.ins["su"]), (g.sd_w, g.ins["sd"])):
                sp.dma_start(dst[:, :], src).then_inc(s_w, 16)
            sp.dma_start(g.not_first[:, :], g.ins["not_first"]).then_inc(s_not_first, 16)
            few(U + sh.LAG, lambda c: sh.sync(sp, c))
            sh.landed(sp)

        @block.gpsimd
        def _(pool):
            few(U + sh.LAG, lambda c: sh.gpsimd(pool, c))

        @block.scalar
        def _(act):
            act.wait_ge(s_shift, 1)
            act.activation(g.logits[:, :], g.logits[:, :], ACT.Exp).then_inc(s_exp, 1)
            few(U + sh.LAG, lambda c: sh.scalar(act, c))

        @block.vector
        def _(dve):
            by_tile = g.logits[:, :].rearrange("p (t e) -> p t e", e=E1)
            over_experts = lambda v: v[:, :].unsqueeze(2).broadcast_to([P, NT, E1])
            dve.tensor_reduce(shift[:, :], by_tile, AX.X, ALU.max).then_inc(s_soft, 1)
            dve.wait_ge(s_soft, 1)
            dve.tensor_tensor(by_tile, by_tile, over_experts(shift), ALU.subtract).then_inc(s_shift, 1)
            dve.wait_ge(s_exp, 1)
            dve.tensor_reduce(total[:, :], by_tile, AX.X, ALU.add).then_inc(s_soft, 1)
            dve.wait_ge(s_soft, 2)
            dve.reciprocal(total[:, :], total[:, :]).then_inc(s_soft, 1)
            dve.wait_ge(s_soft, 3)
            dve.tensor_tensor(by_tile, by_tile, over_experts(total), ALU.mult).then_inc(s_soft, 1)
            dve.wait_ge(s_soft, 4)
            for t in range(NT):
                last = dve.max(g.top_v[:, t * 8:(t + 1) * 8], g.logits[:, t * E1:(t + 1) * E1])
            last.then_inc(s_top, 1)
            dve.wait_ge(s_top, 1)
            for t in range(NT):
                last = dve.max_index(g.top_i[:, t * 8:(t + 1) * 8], g.top_v[:, t * 8:(t + 1) * 8],
                                     g.logits[:, t * E1:(t + 1) * E1])
            last.then_inc(s_top, 1)
            dve.wait_ge(s_top, 2)

            def weights(dve, link):
                link(dve.tensor_reduce(r.wsum[:, :], top, AX.X, ALU.add))
                link(dve.tensor_scalar(r.wsum[:, :], r.wsum[:, :], 1e-12, None, ALU.max))
                link(dve.reciprocal(r.wrec[:, :], r.wsum[:, :]))
                link(dve.tensor_tensor(w, top, r.wrec[:, :].unsqueeze(2).broadcast_to([P, NT, K1]), ALU.mult))

            dve.wait_ge(s_not_first, 16)
            r.vector(dve, weights)

        @block.tensor
        def _(pe):
            pe.wait_ge(s_w, 48)

            def unit(c):
                sh.tensor(pe, c)
                if c.off == COUNTS:
                    r.tensor_counts(pe)
                if c.off == TAB - 1:
                    r.tensor_table_open(pe)
                if TAB <= c.off < TAB + NT * K1 // PER:
                    for i in range(PER):
                        r.tensor_table(pe, c.shift(-TAB).times(PER).shift(i))

            few(U + sh.LAG, unit)
            r.tensor_table_close(pe)


def moe1_phase(nc, g):
    ctx = ExitStack()
    with ctx:
        def sb(name, shape, dt=F32):
            return ctx.enter_context(nc.sbuf_tensor("m1_" + name, shape, dt))

        sem = semaphores(nc, ctx, "m1_")

        NJ = NS1 // 2
        DOWN, HELD, DN_LOADS = 7, 8, 8
        idx = [[sb(f"idx{i}{k}", [P, 1], I32) for k in range(2)] for i in range(GB)]
        xg = [sb(f"xg{i}", [P, 2 * D]) for i in range(GB)]
        xT = [sb(f"xT{i}", [P, 2 * D]) for i in range(2)]
        sg = [sb(f"sg{i}", [P, 2 * M1]) for i in range(2)]
        h = [sb(f"h{i}", [P, 2 * M1]) for i in range(2)]
        hT = [sb(f"hT{i}", [P, 2 * P]) for i in range(HELD)]
        y = [sb(f"y{i}", [P, 2 * D]) for i in range(2)]
        passed, s_dn = sem("passed_pool"), sem("s_dn")
        s_g = [sem(f"s_g{i}") for i in range(GB)]
        y_st = [sem(f"y_st{i}") for i in range(2)]
        idx_ready, x_t, x_out, gu_mm, silu_done, h_done, h_t, h_out, y_mm, y_out = (
            sem(n) for n in ("idx_ready", "x_t", "x_out", "gu_mm", "silu_done", "h_done", "h_t", "h_out", "y_mm",
                             "y_out"))
        ps_x, ps_gu, ps_ht, ps_y = g.bank[0:2], g.bank[2:4], g.bank[4:6], g.bank[6:8]
        block = ctx.enter_context(nc.Block())

        @block.gpsimd
        def _(pool):
            def gather(j):
                p = j.mod(GB)
                wait_alone(pool, x_t, j.shift(1 - GB).n, passed)
                for k in range(2):
                    pool.tensor_copy(idx[p][k][:, :], g.token[:, bass.ds(j.n * 2 + k, 1)]).then_inc(idx_ready, 1)
                wait_alone(pool, idx_ready, j.n * 2 + 2, passed)
                for k in range(2):
                    pool.indirect_dma_start(out=xg[p][:, k * D:(k + 1) * D], out_offset=None, in_=g.xn4,
                                            in_offset=bass.IndirectOffsetOnAxis(ap=idx[p][k][:, :], axis=0))\
                        .then_inc(s_g[p], 16)

            steps(pool, GB, NJ, NJ, GB, gather)

        @block.sync
        def _(sp):
            n = E1 * D // DN_LOADS
            for i in range(DN_LOADS):
                sp.wait_ge(x_t, i // 2 + 1)
                sp.dma_start(g.dn[:, i * n:(i + 1) * n], g.ins["dn"][:, i * n:(i + 1) * n]).then_inc(s_dn, 16)

            def store(j):
                p = j.mod(2)
                sp.wait_ge(y_out, j.n + 1)
                sp.dma_start(g.y1[bass.ds(j.n * 2 * P, 2 * P), :].rearrange("(a p) n -> p a n", p=P),
                             y[p][:, :].rearrange("p (a n) -> p a n", a=2)).then_inc(y_st[p], 16)

            steps(sp, 2, NJ, NJ, 2, store)
            for p in range(2):
                sp.wait_ge(y_st[p], NJ // 2 * 16)

        def halves(ap):
            return ap.rearrange("p (a x n) -> p a x n", a=2, x=2)

        @block.scalar
        def _(act):
            def step(s):
                j = s
                if j.within(NJ):
                    p = j.mod(2)
                    act.wait_ge(x_t, j.n + 1)
                    wait(act, gu_mm, j.shift(-1).n)
                    act.activation(xT[p][:, :], ps_x[p][:, :], ACT.Copy).then_inc(x_out, 1)
                j = s.shift(-1)
                if j.within(NJ):
                    p = j.mod(2)
                    act.wait_ge(gu_mm, j.n + 1)
                    wait(act, h_done, j.shift(-1).n)
                    act.activation(sg[p][:, :].rearrange("p (a n) -> p a n", a=2), halves(ps_gu[p])[:, :, 0, :],
                                   ACT.Silu).then_inc(silu_done, 1)
                j = s.shift(-2)
                if j.within(NJ):
                    p = j.mod(2)
                    act.wait_ge(h_t, j.n + 1)
                    wait(act, y_mm, j.shift(1 - HELD).n)
                    act.activation(hT[j.mod(HELD)][:, :], ps_ht[p][:, 0:2 * P], ACT.Copy).then_inc(h_out, 1)

            steps(act, 2 * HELD, NJ, NJ + 2, HELD, step)

        @block.vector
        def _(dve):
            def step(s):
                j = s.shift(-1)
                if j.within(NJ):
                    p = j.mod(2)
                    dve.wait_ge(silu_done, j.n + 1)
                    wait(dve, h_t, j.shift(-1).n)
                    dve.tensor_tensor(h[p][:, :].rearrange("p (a n) -> p a n", a=2), halves(ps_gu[p])[:, :, 1, :],
                                      sg[p][:, :].rearrange("p (a n) -> p a n", a=2), ALU.mult).then_inc(h_done, 1)
                j = s.shift(-DOWN)
                if j.within(NJ):
                    p = j.mod(2)
                    dve.wait_ge(y_mm, j.n + 1)
                    wait(dve, y_st[p], j.div(2).n * 16)
                    dve.tensor_copy(y[p][:, :], ps_y[p][:, :]).then_inc(y_out, 1)

            steps(dve, DOWN + 3, NJ, NJ + DOWN, 2, step)

        @block.tensor
        def _(pe):
            e = [[pe.alloc_register(f"m1_e{i}{k}") for k in range(2)] for i in range(HELD)]

            def step(s):
                j = s.shift(-1)
                if j.within(NJ):
                    for k in range(2):
                        pe.reg_load(e[j.mod(HELD)][k], g.expert[0:1, bass.ds(j.n * 2 + k, 1)])
                j = s
                if j.within(NJ):
                    p, q = j.mod(2), j.mod(GB)
                    pe.wait_ge(s_g[q], (j.div(GB).n + 1) * 32)
                    wait(pe, x_out, j.shift(-1).n)
                    for c in range(2 * DC):
                        last = pe.transpose(ps_x[p][:, c * P:(c + 1) * P], xg[q][:, c * P:(c + 1) * P], g.ident[:, :])
                    last.then_inc(x_t, 1)
                j = s.shift(-1)
                if j.within(NJ):
                    p = j.mod(2)
                    ex = [pe.snap(e[j.mod(HELD)][k], min_val=0, max_val=E1 - 1) for k in range(2)]
                    pe.wait_ge(x_out, j.n + 1)
                    wait(pe, h_done, j.shift(-1).n)
                    for k in range(2):
                        for c in range(DC):
                            at = (k * DC + c) * P
                            last = pe.matmul(ps_gu[p][:, k * 2 * M1:(k + 1) * 2 * M1], xT[p][:, at:at + P],
                                             g.gu[:, bass.ds(ex[k] * (DC * 2 * M1) + c * 2 * M1, 2 * M1)],
                                             start=(c == 0), stop=(c == DC - 1))
                    last.then_inc(gu_mm, 1)
                j = s.shift(-2)
                if j.within(NJ):
                    p = j.mod(2)
                    pe.wait_ge(h_done, j.n + 1)
                    wait(pe, h_out, j.shift(-1).n)
                    for k in range(2):
                        last = pe.transpose(ps_ht[p][:, k * P:(k + 1) * P], h[p][:, k * M1:(k + 1) * M1], g.ident[:, :])
                    last.then_inc(h_t, 1)
                j = s.shift(-DOWN)
                if j.within(NJ):
                    p = j.mod(2)
                    if j.loop is None and j.off == 0:
                        pe.wait_ge(s_dn, 16 * DN_LOADS)
                    ex = [pe.snap(e[j.mod(HELD)][k], min_val=0, max_val=E1 - 1) for k in range(2)]
                    pe.wait_ge(h_out, j.n + 1)
                    wait(pe, y_out, j.shift(-1).n)
                    for k in range(2):
                        last = pe.matmul(ps_y[p][:, k * D:(k + 1) * D], hT[j.mod(HELD)][:, k * P:(k + 1) * P],
                                         g.dn[:, bass.ds(ex[k] * D, D)], start=True, stop=True)
                    last.then_inc(y_mm, 1)

            steps(pe, 2 * HELD, NJ, NJ + DOWN, HELD, step)


def sum_phase(nc, g):
    ctx = ExitStack()
    with ctx:
        def sb(name, shape, dt=F32):
            return ctx.enter_context(nc.sbuf_tensor("su_" + name, shape, dt))

        sem = semaphores(nc, ctx, "su_")

        STORED = SHARED_FIRST * 512 // P
        idx = [sb(f"idx{i}", [P, K1], I32) for i in range(GB)]
        yg = [[sb(f"yg{i}{k}", [P, D]) for k in range(K1)] for i in range(GB)]
        xs = [sb(f"xs{i}", [P, D]) for i in range(2)]
        kept = sb("kept", [P, (NT - STORED) * D])
        acc = [[sb(f"acc{i}{k}", [P, D]) for k in range(K1)] for i in range(2)]
        passed = sem("passed_pool")
        s_g = [sem(f"s_g{i}") for i in range(GB)]
        s_xs, st = ([sem(f"{n}{i}") for i in range(2)] for n in ("s_xs", "st"))
        idx_ready, part, done = sem("idx_ready"), sem("part"), sem("done")
        sh = SharedExpert(nc, ctx, sem, g, "sh2", SHARED_FIRST, NTOK // 512 - SHARED_FIRST, g.bank[5:8], True)
        UNITS = sh.units + sh.LAG
        block = ctx.enter_context(nc.Block())

        @block.gpsimd
        def _(pool):
            def gather(t):
                p = t.mod(GB)
                wait_alone(pool, done, t.shift(1 - GB).n, passed)
                pool.tensor_copy(idx[p][:, :], g.slot[:, bass.ds(t.n * K1, K1)]).then_inc(idx_ready, 1)
                wait_alone(pool, idx_ready, t.n + 1, passed)
                for k in range(K1):
                    pool.indirect_dma_start(out=yg[p][k][:, :], out_offset=None, in_=g.y1,
                                            in_offset=bass.IndirectOffsetOnAxis(ap=idx[p][:, k:k + 1], axis=0))\
                        .then_inc(s_g[p], 16)

            steps(pool, GB, NT, NT, GB, gather)

        @block.sync
        def _(sp):
            def load(t):
                wait(sp, done, t.shift(-1).n)
                sp.dma_start(xs[t.mod(2)][:, :], g.xs[bass.ds(t.n * P, P), :]).then_inc(s_xs[t.mod(2)], 16)

            def store(t):
                sp.wait_ge(done, t.n + 1)
                sp.dma_start(g.out[bass.ds(t.n * P, P), :], acc[t.mod(2)][K1 - 1][:, :]).then_inc(st[t.mod(2)], 16)

            def tile(s):
                load(s)
                t = s.shift(-1)
                if t.within(NT):
                    store(t)

            steps(sp, 2, STORED, STORED, 2, tile)
            steps(sp, 1, NT - STORED + 1, NT - STORED + 1, 2, lambda s: store(s.shift(STORED - 1)))
            for p in range(2):
                sp.wait_ge(st[p], NT // 2 * 16)

        @block.vector
        def _(dve):
            def tile(t):
                if t.loop is None and t.off < UNITS:
                    sh.vector(dve, t, kept)
                p = t.mod(2)
                if t.loop is None and t.off < STORED:
                    dve.wait_ge(s_xs[p], (t.div(2).n + 1) * 16)
                    residual = xs[p][:, :]
                else:
                    dve.wait_ge(sh.xs_done, t.shift(1 - STORED).n)
                    residual = kept[:, bass.ds(t.shift(-STORED).n * D, D)]
                dve.wait_ge(s_g[t.mod(GB)], (t.div(GB).n + 1) * 16 * K1)
                wait(dve, st[p], t.div(2).n * 16)
                for k in range(K1):
                    if k:
                        dve.wait_ge(part, t.n * (K1 - 1) + k)
                    dve.scalar_tensor_tensor(acc[p][k][:, :], yg[t.mod(GB)][k][:, :],
                                             g.weight[:, bass.ds(t.n * K1 + k, 1)],
                                             acc[p][k - 1][:, :] if k else residual, ALU.mult, ALU.add)\
                        .then_inc(part if k < K1 - 1 else done, 1)

            steps(dve, (UNITS + GB - 1) // GB * GB, NT, NT, GB, tile)

        @block.scalar
        def _(act):
            def unit(c):
                sh.load(act, c)
                sh.silu(act, c)

            few(UNITS, unit)

        @block.tensor
        def _(pe):
            few(UNITS, lambda c: sh.tensor(pe, c))


class Core:

    def __init__(self, ins, scratch, out):
        self.ins, self.out = ins, out
        self.x1, self.x2, self.x3, self.xs = (scratch[n] for n in ("x1", "x2", "x3", "xs"))
        self.xn, self.xn4, self.y0, self.y1 = (scratch[n] for n in ("xn", "xn4", "y0", "y1"))


def program(nc, dram_in, out, scratch):
    g = Core(dram_in, scratch, out)
    ctx = ExitStack()
    with ctx:
        def sb(name, shape, dt=F32):
            return ctx.enter_context(nc.sbuf_tensor(name, shape, dt))

        g.ident = sb("ident", [P, P])
        g.ones = sb("ones", [P, P])
        g.minus_half = sb("minus_half", [P, H])
        g.top_v = sb("top_v", [P, NT * 8])
        g.top_i = sb("top_i", [P, NT * 8], U32)
        g.tri = sb("tri", [P, P])
        g.iota = sb("iota", [P, NS1])
        g.iota16 = sb("iota16", [P, NS1], F16)
        g.tokval = sb("tokval", [P, NT])
        g.slot = sb("slot", [P, NT * K1], I32)
        g.token = sb("token", [P, NS1], I32)
        g.expert = sb("expert", [1, NS1], I32)
        g.weight = sb("weight", [P, NT * K1])
        g.psum = ctx.enter_context(nc.psum_tensor("psum", [P, 8, 512], F32))
        g.bank = [g.psum[:, i, :] for i in range(8)]
        g.pair = [g.psum[:, 2 * i:2 * i + 2, :] for i in range(4)]
        g.kv = sb("kv", [P, NB * NG * LK + NB * H * (DH + 1)])
        g.kT_all, g.v_all = g.kv[:, 0:NB * NG * LK], g.kv[:, NB * NG * LK:]
        g.kT1, g.v1 = g.kv[:, 0:DC * NB * LK], g.kv[:, DC * NB * LK:DC * NB * LK + NB * D]
        with ExitStack() as l0:
            g.w13 = l0.enter_context(nc.sbuf_tensor("w13", [P, E0 * DC * 2 * M0], F32))
            g.not_first = l0.enter_context(nc.sbuf_tensor("not_first", [P, E0 * NT], F32))
            g.w2 = l0.enter_context(nc.sbuf_tensor("w2", [P, E0 * W2_COLS], F32))
            g.ctxT = g.w2[:, 0:CONTEXT_COLS]
            g.wk1, g.wv1 = (g.w2[:, CONTEXT_COLS + i * DC * D:CONTEXT_COLS + (i + 1) * DC * D] for i in range(2))
            g.bv1 = g.w2[0:1, CONTEXT_COLS + 2 * DC * D:CONTEXT_COLS + 2 * DC * D + D]
            g.bk1 = l0.enter_context(nc.sbuf_tensor("bk1", [P, DC], F32))
            with ExitStack() as attn:
                g.qT_all = attn.enter_context(nc.sbuf_tensor("qT_all", [P, NT * D], F32))
                qkv_phase(nc, g)
                attention0_phase(nc, g)
            g.w13_low = l0.enter_context(nc.sbuf_tensor("w13_low", [P, E0 * DC * 2 * M0], F32R))
            route0_phase(nc, g)
            moe0_phase(nc, g)
        with ExitStack() as l1:
            def sb1(name, n):
                return l1.enter_context(nc.sbuf_tensor(name, [P, n], F32))

            g.xn4T, g.logits = sb1("xn4T", DC * NTOK), sb1("logits", NT * E1)
            g.sg_w, g.su_w, g.sd_w = sb1("sg_w", DC * MS), sb1("su_w", DC * MS), sb1("sd_w", MS // P * D)
            with ExitStack() as routed:
                g.gu = routed.enter_context(nc.sbuf_tensor("gu", [P, E1 * DC * 2 * M1], F32))
                attention1_phase(nc, g)
                route1_phase(nc, g)
                g.dn = routed.enter_context(nc.sbuf_tensor("dn", [P, E1 * D], F32))
                moe1_phase(nc, g)
            sum_phase(nc, g)


def kernel(**inputs):
    import concourse.bacc as bacc
    from concourse.bass_utils import run_bass_kernel_spmd

    a = {k: np.asarray(v) for k, v in inputs.items()}

    def cols(w):
        return w.T.reshape(-1, P, w.shape[0]).transpose(1, 0, 2).reshape(P, -1)

    def row(b, n=P):
        return np.broadcast_to(b, (n, b.shape[0]))

    f = np.float32
    eye = np.eye(P, dtype=f)
    arrays = {
        "x": a["x"].reshape(NTOK, D),
        "ctx": a["ctx_1024"].reshape(NB, LK, DC, P).transpose(3, 2, 0, 1).reshape(P, DC * NB * LK),
        "wq": cols(a["L0_xattn_Wq"]),
        "wk": cols(a["L0_xattn_Wk"]),
        "wv": cols(a["L0_xattn_Wv"]),
        "bv": row(np.tile(a["L0_xattn_bv"], 2)),
        "wp": cols(a["L0_xattn_Wp"]),
        "bp": row(a["L0_xattn_bp"]),
        "gb": np.stack([np.tile(a["L0_xattn_" + n], HG) for n in ("q_gamma", "q_beta", "k_gamma", "k_beta")], 1),
        "bkq": np.concatenate([a["L0_xattn_bk"], a["L0_xattn_bq"]])[None, :],
        "wr0": cols(a["L0_ffn_moe_router"].T),
        "ident": eye,
        "tri": np.triu(np.ones((P, P), f), 1),
        "iota": np.broadcast_to(np.arange(NS1, dtype=f), (P, NS1)),
        "iota16": np.broadcast_to(np.arange(NS1, dtype=np.float16), (P, NS1)),
        "not_first": np.broadcast_to((np.arange(E1 * NT) % NT > 0).astype(f), (P, E1 * NT)),
        "tokval": np.arange(NT, dtype=f)[None, :] * P + np.arange(P, dtype=f)[:, None] - MID,
        "w13": a["L0_ffn_moe_w13"].reshape(E0, DC, P, 2 * M0).transpose(2, 0, 1, 3).reshape(P, -1),
        "wq1": cols(a["L1_xattn_Wq"]),
        "wk1": cols(a["L1_xattn_Wk"]),
        "wv1": cols(a["L1_xattn_Wv"]),
        "wo1": cols(a["L1_xattn_Wo"]),
        "wr1": cols(a["L1_ffn_router_w"]),
        "bq1": a["L1_xattn_bq"].reshape(DC, P).T,
        "bk1": a["L1_xattn_bk"].reshape(DC, P).T,
        "bv1": row(a["L1_xattn_bv"], 1),
        "bo1": row(a["L1_xattn_bo"], 1),
        "rb1": row(a["L1_ffn_router_bias"]),
        "gu": np.stack([a["L1_ffn_gate_w"], a["L1_ffn_up_w"]]).reshape(2, E1, M1, DC, P)
        .transpose(4, 1, 3, 0, 2).reshape(P, -1),
        "dn": a["L1_ffn_down_w"].transpose(2, 0, 1).reshape(P, -1),
        "sg": cols(a["L1_ffn_sgate_w"]),
        "su": cols(a["L1_ffn_sup_w"]),
        "sd": cols(a["L1_ffn_sdown_w"]),
        "w2": a["L0_ffn_moe_w2"].reshape(E0, M0 // P, P, D).transpose(2, 0, 1, 3).reshape(P, -1),
        "hmask": np.repeat(np.eye(HG, dtype=f), DH, axis=0),
    }
    arrays = {k: np.ascontiguousarray(v) for k, v in arrays.items()}
    nc = bacc.Bacc("TRN2", target_bir_lowering=False, num_devices=1)
    dram_in = {n: nc.dram_tensor("in_" + n, v.shape, mybir.dt.from_np(v.dtype), kind="ExternalInput").ap()
               for n, v in arrays.items()}
    out = nc.dram_tensor("out", (NTOK, D), F32, kind="ExternalOutput").ap()
    scratch = {n: nc.dram_tensor("t_" + n, s, F32, kind="Internal").ap() for n, s in (
        ("x1", (NTOK, D)), ("xn", (NTOK, D)), ("y0", (NS0 * P, D)), ("y1", (NS1 * P, D)), ("x2", (NTOK, D)), ("x3", (NTOK, D)), ("xn4", (NTOK, D)), ("xs", (NTOK, D)))}
    program(nc, dram_in, out, scratch)
    res = run_bass_kernel_spmd(nc, [{"in_" + n: v for n, v in arrays.items()}], core_ids=[0])
    return res.results[0]["out"].reshape(NB, SQ, D)
```
